# Optimizing a Trainium2 kernel written in Bass

```python
import numpy as np
import jax
import jax.numpy as jnp

def _softmax(x, axis=-1):
    return jax.nn.softmax(x, axis=axis)

def _gelu(x):
    return jax.nn.gelu(x, approximate=True)

def _silu(x):
    return jax.nn.silu(x)

def _sigmoid(x):
    return jax.nn.sigmoid(x)

def _layernorm(x, axis=-1, eps=1e-05):
    m = jnp.mean(x, axis=axis, keepdims=True)
    v = jnp.var(x, axis=axis, keepdims=True)
    return (x - m) / jnp.sqrt(v + eps)

def _scatter_add(tgt, idx, src, axis=0):
    return tgt.at[idx].add(src)

def _segment_sum(src, seg, n):
    return jax.ops.segment_sum(src, seg, n)
kernel_name = 'mk_xattn_seq_d4_seqx_r4_a1182f'

def setup_inputs(seed: int=0):
    np.random.seed(seed)
    _w = jnp.asarray

    def _rec_inputs():
        import jax
        import jax.numpy as jnp
        _rk = jax.random.key(seed)
        x = 7.22e-05 + 1 * jax.random.normal(jax.random.fold_in(_rk, 1), (16, 128, 512), jnp.float32)
        _lenS = 128 - jax.random.randint(jax.random.fold_in(_rk, 7), (16,), 0, max(1, 128 // 4) + 1, jnp.int32)
        _lenS2 = 128 - jax.random.randint(jax.random.fold_in(_rk, 8), (16,), 0, max(1, 128 // 4) + 1, jnp.int32)
        _ctx_2048P = jax.random.normal(jax.random.fold_in(_rk, 11), (16, 16, 512), jnp.float32)
        _ctx_2048c = jax.random.dirichlet(jax.random.fold_in(_rk, 511), 0.3 * jnp.ones((16,), jnp.float32), (16, 128))
        _ctx_2048t = jnp.einsum('bsk,bkd->bsd', _ctx_2048c, _ctx_2048P)
        _ctx_2048t = _ctx_2048t * jax.lax.rsqrt(jnp.mean(jnp.square(_ctx_2048t)) + 1e-12) * 0.953939
        ctx_2048 = 4.13588e-05 + 0.999923 * (_ctx_2048t + 0.3 * jax.random.normal(jax.random.fold_in(_rk, 611), (16, 128, 512), jnp.float32))
        _validS = jnp.arange(128)[None, :] < _lenS[:, None]
        _validS2 = jnp.arange(128)[None, :] < _lenS2[:, None]
        _causal = jnp.tril(jnp.ones((128, 128), dtype=bool))
        mask_BxS2_ik0 = jnp.where(jnp.broadcast_to(_validS2[:, :], (16, 128)), 0, 1).astype(jnp.int32)
        mask_Bx1xSxS2_ff0 = jnp.where(jnp.ones((16, 1, 128, 128), dtype=bool), 0.0, -1000000000.0).astype(jnp.float32)
        return (x, ctx_2048, mask_BxS2_ik0, mask_Bx1xSxS2_ff0)
    x, ctx_2048, mask_BxS2_ik0, mask_Bx1xSxS2_ff0 = _rec_inputs()

    def _L0_xattn_setup():
        import jax, jax.numpy as jnp
        import numpy as np
        B, C, CI, T = (8, 128, 64, 512)
        EPS = 1e-05
        key = jax.random.key(seed)
        ks = jax.random.split(key, 8)
        inv_c = 1.0 / np.sqrt(C)
        inv_ci = 1.0 / np.sqrt(CI)
        return {'x_this': jax.random.normal(ks[0], (B, C, T), jnp.float32), 'x_other': jax.random.normal(ks[1], (B, C, T), jnp.float32), 'Wg': jax.random.normal(ks[2], (CI, C), jnp.float32) * inv_c, 'bg': jnp.zeros((CI,), jnp.float32), 'Wtheta': jax.random.normal(ks[3], (CI, C), jnp.float32) * inv_c, 'btheta': jnp.zeros((CI,), jnp.float32), 'Wphi': jax.random.normal(ks[4], (CI, C), jnp.float32) * inv_c, 'bphi': jnp.zeros((CI,), jnp.float32), 'Wz': jax.random.normal(ks[5], (C, CI), jnp.float32) * inv_ci, 'bz': jnp.zeros((C,), jnp.float32), 'gamma': jax.random.normal(ks[6], (C,), jnp.float32), 'beta': jax.random.normal(ks[7], (C,), jnp.float32)}
    _L0_xattn_all = _L0_xattn_setup()
    _L0_xattn_in = {k: v for k, v in _L0_xattn_all.items() if k in ('Wg', 'bg', 'Wtheta', 'btheta', 'Wphi', 'bphi', 'Wz', 'bz', 'gamma', 'beta')}
    del _L0_xattn_all

    def _L1_xattn_setup():
        import jax, jax.numpy as jnp
        import numpy as np
        B, P, K, H, NH = (4, 512, 64, 512, 16)
        DH = H // NH
        EPS = 1e-06

        def rmsnorm(x, w):
            var = jnp.mean(jnp.square(x), axis=-1, keepdims=True)
            return x * jax.lax.rsqrt(var + EPS) * w
        key = jax.random.key(seed)
        ks = jax.random.split(key, 12)
        s = 0.02
        return {'x': jax.random.normal(ks[0], (B, P, H), jnp.float32), 'latents': jax.random.normal(ks[1], (B, K, H), jnp.float32), 'attention_mask': jax.random.randint(ks[2], (B, P), 0, 2, jnp.int32), 'q_w': s * jax.random.normal(ks[3], (H, H), jnp.float32), 'q_b': jnp.zeros((H,), jnp.float32), 'kv_w': s * jax.random.normal(ks[4], (H, 2 * H), jnp.float32), 'kv_b': jnp.zeros((2 * H,), jnp.float32), 'out_w': s * jax.random.normal(ks[5], (H, H), jnp.float32), 'out_b': jnp.zeros((H,), jnp.float32), 'postnorm_w': jnp.ones((H,), jnp.float32), 'mlp_w1': s * jax.random.normal(ks[6], (H, 4 * H), jnp.float32), 'mlp_b1': jnp.zeros((4 * H,), jnp.float32), 'mlp_w2': s * jax.random.normal(ks[7], (4 * H, H), jnp.float32), 'mlp_b2': jnp.zeros((H,), jnp.float32)}
    _L1_xattn_all = _L1_xattn_setup()
    _L1_xattn_in = {k: v for k, v in _L1_xattn_all.items() if k in ('q_w', 'q_b', 'kv_w', 'kv_b', 'out_w', 'out_b', 'postnorm_w', 'mlp_w1', 'mlp_b1', 'mlp_w2', 'mlp_b2')}
    del _L1_xattn_all

    def _L2_xattn_setup():
        import jax, jax.numpy as jnp
        import numpy as np
        E, H, L, B = (512, 32, 256, 4)
        S = E // H
        DM, DD = (32, 64)

        def _ln(x, w, b, eps=1e-05):
            m = x.mean(-1, keepdims=True)
            v = ((x - m) ** 2).mean(-1, keepdims=True)
            return (x - m) / jnp.sqrt(v + eps) * w + b

        def _block(x, state, ln1_w, ln1_b, ln2_w, ln2_b, maa_x, maa_w1, maa_w2, maa_stack, time_decay, td_w1, td_w2, u, Wr, Wk, Wv, Wg, Wo, gn_w, gn_b, ffn_maa_k, ffn_maa_r, Wfk, Wfr, Wfv):
            b, l, e = x.shape
            h = u.shape[0]
            s_ = e // h
            xa = _ln(x, ln1_w, ln1_b)
            sx = jnp.concatenate([state[:, 1:2] - xa[:, :1], xa[:, :-1] - xa[:, 1:]], axis=1)
            xxx = jnp.tanh((xa + sx * maa_x) @ maa_w1).reshape(b, l, 5, DM)
            xxx = jnp.einsum('blfd,fde->blfe', xxx, maa_w2)
            xm = xa[:, :, None] + sx[:, :, None] * (maa_stack + xxx)
            xk, xw, xv, xr, xg = (xm[:, :, j] for j in range(5))
            w = jnp.exp(-jnp.exp(time_decay + jnp.tanh(xw @ td_w1) @ td_w2)).reshape(b, l, h, s_)
            r = (xr @ Wr.T).reshape(b, l, h, s_)
            k = (xk @ Wk.T).reshape(b, l, h, s_)
            v = (xv @ Wv.T).reshape(b, l, h, s_)
            g = jax.nn.silu(xg @ Wg.T)
            s0 = state[:, 2:2 + s_].reshape(b, h, s_, s_)

            def step(s, rkvw):
                r_t, k_t, v_t, w_t = rkvw
                a = k_t[..., :, None] * v_t[..., None, :]
                out = jnp.einsum('bhi,bhij->bhj', r_t, u * a + s)
                s = a + w_t[..., :, None] * s
                return (s, out)
            rkvw = tuple((jnp.moveaxis(t, 1, 0) for t in (r, k, v, w)))
            _, out = jax.lax.scan(step, s0, rkvw)
            out = jnp.moveaxis(out, 0, 1).reshape(b, l, e)
            og = out.reshape(b, l, h, s_)
            m = og.mean(-1, keepdims=True)
            va = ((og - m) ** 2).mean(-1, keepdims=True)
            og = ((og - m) / jnp.sqrt(va + 1e-05)).reshape(b, l, e) * gn_w + gn_b
            x1 = x + og * g @ Wo.T
            xc = _ln(x1, ln2_w, ln2_b)
            sx2 = jnp.concatenate([state[:, 0:1] - xc[:, :1], xc[:, :-1] - xc[:, 1:]], axis=1)
            xk2 = xc + sx2 * ffn_maa_k
            xr2 = xc + sx2 * ffn_maa_r
            rr = jax.nn.sigmoid(xr2 @ Wfr.T)
            kk = jnp.square(jax.nn.relu(xk2 @ Wfk.T))
            return x1 + rr * (kk @ Wfv.T)
        key = jax.random.key(seed)
        ks = jax.random.split(key, 24)
        sc = 0.02
        d = {'x': jax.random.normal(ks[0], (B, L, E), jnp.float32), 'state': jax.random.normal(ks[1], (B, 2 + S, E), jnp.float32) * 0.1, 'ln1_w': jnp.ones((E,), jnp.float32), 'ln1_b': jnp.zeros((E,), jnp.float32), 'ln2_w': jnp.ones((E,), jnp.float32), 'ln2_b': jnp.zeros((E,), jnp.float32), 'maa_x': jax.random.normal(ks[2], (E,), jnp.float32) * 0.1, 'maa_w1': jax.random.normal(ks[3], (E, 5 * DM), jnp.float32) * sc, 'maa_w2': jax.random.normal(ks[4], (5, DM, E), jnp.float32) * sc, 'maa_stack': jax.random.normal(ks[5], (1, 5, E), jnp.float32) * 0.1, 'time_decay': jax.random.normal(ks[6], (E,), jnp.float32) * 0.5, 'td_w1': jax.random.normal(ks[7], (E, DD), jnp.float32) * sc, 'td_w2': jax.random.normal(ks[8], (DD, E), jnp.float32) * sc, 'u': jax.random.normal(ks[9], (H, S, 1), jnp.float32) * 0.1, 'Wr': jax.random.normal(ks[10], (E, E), jnp.float32) * sc, 'Wk': jax.random.normal(ks[11], (E, E), jnp.float32) * sc, 'Wv': jax.random.normal(ks[12], (E, E), jnp.float32) * sc, 'Wg': jax.random.normal(ks[13], (E, E), jnp.float32) * sc, 'Wo': jax.random.normal(ks[14], (E, E), jnp.float32) * sc, 'gn_w': jnp.ones((E,), jnp.float32), 'gn_b': jnp.zeros((E,), jnp.float32), 'ffn_maa_k': jax.random.normal(ks[15], (E,), jnp.float32) * 0.1, 'ffn_maa_r': jax.random.normal(ks[16], (E,), jnp.float32) * 0.1, 'Wfk': jax.random.normal(ks[17], (E, E), jnp.float32) * sc, 'Wfr': jax.random.normal(ks[18], (E, E), jnp.float32) * sc, 'Wfv': jax.random.normal(ks[19], (E, E), jnp.float32) * sc}
        return d
    _L2_xattn_all = _L2_xattn_setup()
    _L2_xattn_in = {k: v for k, v in _L2_xattn_all.items() if k in ('ln1_w', 'ln1_b', 'ln2_w', 'ln2_b', 'maa_x', 'maa_w1', 'maa_w2', 'maa_stack', 'time_decay', 'td_w1', 'td_w2', 'u', 'Wr', 'Wk', 'Wv', 'Wg', 'Wo', 'gn_w', 'gn_b', 'ffn_maa_k', 'ffn_maa_r', 'Wfk', 'Wfr', 'Wfv')}
    del _L2_xattn_all

    def _L3_xattn_setup():
        import jax, jax.numpy as jnp
        import numpy as np
        H = 512
        NH = 32
        KVH = 8
        HD = H // NH
        GROUPS = NH // KVH
        EPS = 1e-06
        B, L, S = (4, 256, 256)

        def _gqa_forward(hidden_state, encoder_hidden_state, encoder_attention_mask, Wq, bq, Wk, bk, Wv, bv, Wo, bo, gamma, beta):
            b, l, _ = hidden_state.shape
            s = encoder_hidden_state.shape[1]
            q = hidden_state @ Wq + bq
            k = encoder_hidden_state @ Wk + bk
            v = encoder_hidden_state @ Wv + bv
            q = q.reshape(b, l, KVH, GROUPS, HD).transpose(0, 2, 3, 1, 4)
            k = k.reshape(b, s, KVH, HD).transpose(0, 2, 1, 3)
            v = v.reshape(b, s, KVH, HD).transpose(0, 2, 1, 3)
            scale = 1.0 / jnp.sqrt(jnp.asarray(HD, q.dtype))
            scores = jnp.einsum('bkgld,bksd->bkgls', q, k) * scale
            scores = scores + encoder_attention_mask[:, :, None, :, :]
            attn = jax.nn.softmax(scores, axis=-1)
            out = jnp.einsum('bkgls,bksd->bkgld', attn, v)
            out = out.transpose(0, 3, 1, 2, 4).reshape(b, l, H)
            out = out @ Wo + bo
            x = out + hidden_state
            mu = jnp.mean(x, axis=-1, keepdims=True)
            var = jnp.var(x, axis=-1, keepdims=True)
            return (x - mu) * jax.lax.rsqrt(var + EPS) * gamma + beta
        key = jax.random.key(seed)
        ks = jax.random.split(key, 12)
        sd = 0.02
        return {'hidden_state': jax.random.normal(ks[0], (B, L, H), jnp.float32), 'encoder_hidden_state': jax.random.normal(ks[1], (B, S, H), jnp.float32), 'encoder_attention_mask': jnp.zeros((B, 1, L, S), jnp.float32), 'Wq': jax.random.normal(ks[2], (H, H), jnp.float32) * sd, 'bq': jnp.zeros((H,), jnp.float32), 'Wk': jax.random.normal(ks[3], (H, KVH * HD), jnp.float32) * sd, 'bk': jnp.zeros((KVH * HD,), jnp.float32), 'Wv': jax.random.normal(ks[4], (H, KVH * HD), jnp.float32) * sd, 'bv': jnp.zeros((KVH * HD,), jnp.float32), 'Wo': jax.random.normal(ks[5], (H, H), jnp.float32) * sd, 'bo': jnp.zeros((H,), jnp.float32), 'gamma': jnp.ones((H,), jnp.float32), 'beta': jnp.zeros((H,), jnp.float32)}
    _L3_xattn_all = _L3_xattn_setup()
    _L3_xattn_in = {k: v for k, v in _L3_xattn_all.items() if k in ('Wq', 'bq', 'Wk', 'bk', 'Wv', 'bv', 'Wo', 'bo', 'gamma', 'beta')}
    del _L3_xattn_all
    return {'x': x, 'ctx_2048': ctx_2048, 'mask_BxS2_ik0': mask_BxS2_ik0, 'mask_Bx1xSxS2_ff0': mask_Bx1xSxS2_ff0, 'L0_xattn_Wg': _L0_xattn_in['Wg'], 'L0_xattn_bg': _L0_xattn_in['bg'], 'L0_xattn_Wtheta': _L0_xattn_in['Wtheta'], 'L0_xattn_btheta': _L0_xattn_in['btheta'], 'L0_xattn_Wphi': _L0_xattn_in['Wphi'], 'L0_xattn_bphi': _L0_xattn_in['bphi'], 'L0_xattn_Wz': _L0_xattn_in['Wz'], 'L0_xattn_bz': _L0_xattn_in['bz'], 'L0_xattn_gamma': _L0_xattn_in['gamma'], 'L0_xattn_beta': _L0_xattn_in['beta'], 'L1_xattn_q_w': _L1_xattn_in['q_w'], 'L1_xattn_q_b': _L1_xattn_in['q_b'], 'L1_xattn_kv_w': _L1_xattn_in['kv_w'], 'L1_xattn_kv_b': _L1_xattn_in['kv_b'], 'L1_xattn_out_w': _L1_xattn_in['out_w'], 'L1_xattn_out_b': _L1_xattn_in['out_b'], 'L1_xattn_postnorm_w': _L1_xattn_in['postnorm_w'], 'L1_xattn_mlp_w1': _L1_xattn_in['mlp_w1'], 'L1_xattn_mlp_b1': _L1_xattn_in['mlp_b1'], 'L1_xattn_mlp_w2': _L1_xattn_in['mlp_w2'], 'L1_xattn_mlp_b2': _L1_xattn_in['mlp_b2'], 'L2_xattn_ln1_w': _L2_xattn_in['ln1_w'], 'L2_xattn_ln1_b': _L2_xattn_in['ln1_b'], 'L2_xattn_ln2_w': _L2_xattn_in['ln2_w'], 'L2_xattn_ln2_b': _L2_xattn_in['ln2_b'], 'L2_xattn_maa_x': _L2_xattn_in['maa_x'], 'L2_xattn_maa_w1': _L2_xattn_in['maa_w1'], 'L2_xattn_maa_w2': _L2_xattn_in['maa_w2'], 'L2_xattn_maa_stack': _L2_xattn_in['maa_stack'], 'L2_xattn_time_decay': _L2_xattn_in['time_decay'], 'L2_xattn_td_w1': _L2_xattn_in['td_w1'], 'L2_xattn_td_w2': _L2_xattn_in['td_w2'], 'L2_xattn_u': _L2_xattn_in['u'], 'L2_xattn_Wr': _L2_xattn_in['Wr'], 'L2_xattn_Wk': _L2_xattn_in['Wk'], 'L2_xattn_Wv': _L2_xattn_in['Wv'], 'L2_xattn_Wg': _L2_xattn_in['Wg'], 'L2_xattn_Wo': _L2_xattn_in['Wo'], 'L2_xattn_gn_w': _L2_xattn_in['gn_w'], 'L2_xattn_gn_b': _L2_xattn_in['gn_b'], 'L2_xattn_ffn_maa_k': _L2_xattn_in['ffn_maa_k'], 'L2_xattn_ffn_maa_r': _L2_xattn_in['ffn_maa_r'], 'L2_xattn_Wfk': _L2_xattn_in['Wfk'], 'L2_xattn_Wfr': _L2_xattn_in['Wfr'], 'L2_xattn_Wfv': _L2_xattn_in['Wfv'], 'L3_xattn_Wq': _L3_xattn_in['Wq'], 'L3_xattn_bq': _L3_xattn_in['bq'], 'L3_xattn_Wk': _L3_xattn_in['Wk'], 'L3_xattn_bk': _L3_xattn_in['bk'], 'L3_xattn_Wv': _L3_xattn_in['Wv'], 'L3_xattn_bv': _L3_xattn_in['bv'], 'L3_xattn_Wo': _L3_xattn_in['Wo'], 'L3_xattn_bo': _L3_xattn_in['bo'], 'L3_xattn_gamma': _L3_xattn_in['gamma'], 'L3_xattn_beta': _L3_xattn_in['beta']}

def reference(x, ctx_2048, mask_BxS2_ik0, mask_Bx1xSxS2_ff0, L0_xattn_Wg, L0_xattn_bg, L0_xattn_Wtheta, L0_xattn_btheta, L0_xattn_Wphi, L0_xattn_bphi, L0_xattn_Wz, L0_xattn_bz, L0_xattn_gamma, L0_xattn_beta, L1_xattn_q_w, L1_xattn_q_b, L1_xattn_kv_w, L1_xattn_kv_b, L1_xattn_out_w, L1_xattn_out_b, L1_xattn_postnorm_w, L1_xattn_mlp_w1, L1_xattn_mlp_b1, L1_xattn_mlp_w2, L1_xattn_mlp_b2, L2_xattn_ln1_w, L2_xattn_ln1_b, L2_xattn_ln2_w, L2_xattn_ln2_b, L2_xattn_maa_x, L2_xattn_maa_w1, L2_xattn_maa_w2, L2_xattn_maa_stack, L2_xattn_time_decay, L2_xattn_td_w1, L2_xattn_td_w2, L2_xattn_u, L2_xattn_Wr, L2_xattn_Wk, L2_xattn_Wv, L2_xattn_Wg, L2_xattn_Wo, L2_xattn_gn_w, L2_xattn_gn_b, L2_xattn_ffn_maa_k, L2_xattn_ffn_maa_r, L2_xattn_Wfk, L2_xattn_Wfr, L2_xattn_Wfv, L3_xattn_Wq, L3_xattn_bq, L3_xattn_Wk, L3_xattn_bk, L3_xattn_Wv, L3_xattn_bv, L3_xattn_Wo, L3_xattn_bo, L3_xattn_gamma, L3_xattn_beta):
    import jax
    import jax.numpy as jnp

    def _L0_xattn_ref(x_this, x_other, Wg, bg, Wtheta, btheta, Wphi, bphi, Wz, bz, gamma, beta):
        import jax, jax.numpy as jnp
        import numpy as np
        B, C, CI, T = (8, 128, 64, 512)
        EPS = 1e-05
        g_x = jnp.einsum('oc,bct->bto', Wg, x_this) + bg
        theta = jnp.einsum('oc,bct->bot', Wtheta, x_this) + btheta[None, :, None]
        phi = jnp.einsum('oc,bct->bot', Wphi, x_other) + bphi[None, :, None]
        f = jnp.einsum('bci,bcj->bij', phi, theta)
        f_div_C = jax.nn.softmax(f, axis=-1)
        y = jnp.einsum('bij,bjo->bio', f_div_C, g_x)
        w_y = jnp.einsum('oc,btc->bot', Wz, y) + bz[None, :, None]
        mean = jnp.mean(w_y, axis=(0, 2), keepdims=True)
        var = jnp.var(w_y, axis=(0, 2), keepdims=True)
        w_y = gamma[None, :, None] * (w_y - mean) * jax.lax.rsqrt(var + EPS) + beta[None, :, None]
        return w_y + x_this

    def _L1_xattn_ref(x, latents, attention_mask, q_w, q_b, kv_w, kv_b, out_w, out_b, postnorm_w, mlp_w1, mlp_b1, mlp_w2, mlp_b2):
        import jax, jax.numpy as jnp
        import numpy as np
        B, P, K, H, NH = (4, 512, 64, 512, 16)
        DH = H // NH
        EPS = 1e-06

        def rmsnorm(x, w):
            var = jnp.mean(jnp.square(x), axis=-1, keepdims=True)
            return x * jax.lax.rsqrt(var + EPS) * w
        b, p, _ = x.shape
        k_len = latents.shape[1]
        residual = latents
        h = jnp.concatenate([x, latents], axis=1)
        q = (latents @ q_w + q_b).reshape(b, k_len, NH, DH)
        kv = (h @ kv_w + kv_b).reshape(b, p + k_len, NH, DH, 2)
        kmat, v = (kv[..., 0], kv[..., 1])
        attn = jnp.einsum('bkhd,bnhd->bhkn', q, kmat) / DH
        full_mask = jnp.concatenate([attention_mask.astype(bool), jnp.ones((b, k_len), bool)], axis=-1)
        attn = jnp.where(full_mask[:, None, None, :], attn, -jnp.inf)
        attn = jax.nn.softmax(attn.astype(jnp.float32), axis=-1).astype(q.dtype)
        attn_out = jnp.einsum('bhkn,bnhd->bkhd', attn, v).reshape(b, k_len, H)
        attn_out = attn_out @ out_w + out_b + residual
        out = rmsnorm(attn_out, postnorm_w)
        out = jax.nn.gelu(out @ mlp_w1 + mlp_b1) @ mlp_w2 + mlp_b2
        return out + residual

    def _L2_xattn_ref(x, state, ln1_w, ln1_b, ln2_w, ln2_b, maa_x, maa_w1, maa_w2, maa_stack, time_decay, td_w1, td_w2, u, Wr, Wk, Wv, Wg, Wo, gn_w, gn_b, ffn_maa_k, ffn_maa_r, Wfk, Wfr, Wfv):
        import jax, jax.numpy as jnp
        import numpy as np
        E, H, L, B = (512, 32, 256, 4)
        S = E // H
        DM, DD = (32, 64)

        def _ln(x, w, b, eps=1e-05):
            m = x.mean(-1, keepdims=True)
            v = ((x - m) ** 2).mean(-1, keepdims=True)
            return (x - m) / jnp.sqrt(v + eps) * w + b

        def _block(x, state, ln1_w, ln1_b, ln2_w, ln2_b, maa_x, maa_w1, maa_w2, maa_stack, time_decay, td_w1, td_w2, u, Wr, Wk, Wv, Wg, Wo, gn_w, gn_b, ffn_maa_k, ffn_maa_r, Wfk, Wfr, Wfv):
            b, l, e = x.shape
            h = u.shape[0]
            s_ = e // h
            xa = _ln(x, ln1_w, ln1_b)
            sx = jnp.concatenate([state[:, 1:2] - xa[:, :1], xa[:, :-1] - xa[:, 1:]], axis=1)
            xxx = jnp.tanh((xa + sx * maa_x) @ maa_w1).reshape(b, l, 5, DM)
            xxx = jnp.einsum('blfd,fde->blfe', xxx, maa_w2)
            xm = xa[:, :, None] + sx[:, :, None] * (maa_stack + xxx)
            xk, xw, xv, xr, xg = (xm[:, :, j] for j in range(5))
            w = jnp.exp(-jnp.exp(time_decay + jnp.tanh(xw @ td_w1) @ td_w2)).reshape(b, l, h, s_)
            r = (xr @ Wr.T).reshape(b, l, h, s_)
            k = (xk @ Wk.T).reshape(b, l, h, s_)
            v = (xv @ Wv.T).reshape(b, l, h, s_)
            g = jax.nn.silu(xg @ Wg.T)
            s0 = state[:, 2:2 + s_].reshape(b, h, s_, s_)

            def step(s, rkvw):
                r_t, k_t, v_t, w_t = rkvw
                a = k_t[..., :, None] * v_t[..., None, :]
                out = jnp.einsum('bhi,bhij->bhj', r_t, u * a + s)
                s = a + w_t[..., :, None] * s
                return (s, out)
            rkvw = tuple((jnp.moveaxis(t, 1, 0) for t in (r, k, v, w)))
            _, out = jax.lax.scan(step, s0, rkvw)
            out = jnp.moveaxis(out, 0, 1).reshape(b, l, e)
            og = out.reshape(b, l, h, s_)
            m = og.mean(-1, keepdims=True)
            va = ((og - m) ** 2).mean(-1, keepdims=True)
            og = ((og - m) / jnp.sqrt(va + 1e-05)).reshape(b, l, e) * gn_w + gn_b
            x1 = x + og * g @ Wo.T
            xc = _ln(x1, ln2_w, ln2_b)
            sx2 = jnp.concatenate([state[:, 0:1] - xc[:, :1], xc[:, :-1] - xc[:, 1:]], axis=1)
            xk2 = xc + sx2 * ffn_maa_k
            xr2 = xc + sx2 * ffn_maa_r
            rr = jax.nn.sigmoid(xr2 @ Wfr.T)
            kk = jnp.square(jax.nn.relu(xk2 @ Wfk.T))
            return x1 + rr * (kk @ Wfv.T)
        return _block(x, state, ln1_w, ln1_b, ln2_w, ln2_b, maa_x, maa_w1, maa_w2, maa_stack, time_decay, td_w1, td_w2, u, Wr, Wk, Wv, Wg, Wo, gn_w, gn_b, ffn_maa_k, ffn_maa_r, Wfk, Wfr, Wfv)

    def _L3_xattn_ref(hidden_state, encoder_hidden_state, encoder_attention_mask, Wq, bq, Wk, bk, Wv, bv, Wo, bo, gamma, beta):
        import jax, jax.numpy as jnp
        import numpy as np
        H = 512
        NH = 32
        KVH = 8
        HD = H // NH
        GROUPS = NH // KVH
        EPS = 1e-06
        B, L, S = (4, 256, 256)

        def _gqa_forward(hidden_state, encoder_hidden_state, encoder_attention_mask, Wq, bq, Wk, bk, Wv, bv, Wo, bo, gamma, beta):
            b, l, _ = hidden_state.shape
            s = encoder_hidden_state.shape[1]
            q = hidden_state @ Wq + bq
            k = encoder_hidden_state @ Wk + bk
            v = encoder_hidden_state @ Wv + bv
            q = q.reshape(b, l, KVH, GROUPS, HD).transpose(0, 2, 3, 1, 4)
            k = k.reshape(b, s, KVH, HD).transpose(0, 2, 1, 3)
            v = v.reshape(b, s, KVH, HD).transpose(0, 2, 1, 3)
            scale = 1.0 / jnp.sqrt(jnp.asarray(HD, q.dtype))
            scores = jnp.einsum('bkgld,bksd->bkgls', q, k) * scale
            scores = scores + encoder_attention_mask[:, :, None, :, :]
            attn = jax.nn.softmax(scores, axis=-1)
            out = jnp.einsum('bkgls,bksd->bkgld', attn, v)
            out = out.transpose(0, 3, 1, 2, 4).reshape(b, l, H)
            out = out @ Wo + bo
            x = out + hidden_state
            mu = jnp.mean(x, axis=-1, keepdims=True)
            var = jnp.var(x, axis=-1, keepdims=True)
            return (x - mu) * jax.lax.rsqrt(var + EPS) * gamma + beta
        return _gqa_forward(hidden_state, encoder_hidden_state, encoder_attention_mask, Wq, bq, Wk, bk, Wv, bv, Wo, bo, gamma, beta)
    x = _L0_xattn_ref(x, ctx_2048, L0_xattn_Wg, L0_xattn_bg, L0_xattn_Wtheta, L0_xattn_btheta, L0_xattn_Wphi, L0_xattn_bphi, L0_xattn_Wz, L0_xattn_bz, L0_xattn_gamma, L0_xattn_beta)
    x = _L1_xattn_ref(ctx_2048, x, mask_BxS2_ik0, L1_xattn_q_w, L1_xattn_q_b, L1_xattn_kv_w, L1_xattn_kv_b, L1_xattn_out_w, L1_xattn_out_b, L1_xattn_postnorm_w, L1_xattn_mlp_w1, L1_xattn_mlp_b1, L1_xattn_mlp_w2, L1_xattn_mlp_b2)
    x = _L2_xattn_ref(x, ctx_2048, L2_xattn_ln1_w, L2_xattn_ln1_b, L2_xattn_ln2_w, L2_xattn_ln2_b, L2_xattn_maa_x, L2_xattn_maa_w1, L2_xattn_maa_w2, L2_xattn_maa_stack, L2_xattn_time_decay, L2_xattn_td_w1, L2_xattn_td_w2, L2_xattn_u, L2_xattn_Wr, L2_xattn_Wk, L2_xattn_Wv, L2_xattn_Wg, L2_xattn_Wo, L2_xattn_gn_w, L2_xattn_gn_b, L2_xattn_ffn_maa_k, L2_xattn_ffn_maa_r, L2_xattn_Wfk, L2_xattn_Wfr, L2_xattn_Wfv)
    x = _L3_xattn_ref(x, ctx_2048, mask_Bx1xSxS2_ff0, L3_xattn_Wq, L3_xattn_bq, L3_xattn_Wk, L3_xattn_bk, L3_xattn_Wv, L3_xattn_bv, L3_xattn_Wo, L3_xattn_bo, L3_xattn_gamma, L3_xattn_beta)
    return x

_drawn_inputs = setup_inputs


def setup_inputs(seed=0):
    import zlib

    import numpy as np

    out = dict(_drawn_inputs(seed))
    spreads = {'L0_xattn_bg': (0.0, 2.0),
     'L0_xattn_btheta': (0.0, 2.0),
     'L0_xattn_bphi': (0.0, 0.1),
     'L0_xattn_bz': (0.0, 2.0),
     'L1_xattn_q_b': (0.0, 0.8),
     'L1_xattn_kv_b': (0.0, 2.0),
     'L1_xattn_out_b': (0.0, 2.0),
     'L1_xattn_postnorm_w': (1.0, 0.2),
     'L1_xattn_mlp_b1': (0.0, 0.1),
     'L1_xattn_mlp_b2': (0.0, 0.1),
     'L2_xattn_ln1_w': (1.0, 0.2),
     'L2_xattn_ln1_b': (0.0, 0.358),
     'L2_xattn_ln2_w': (1.0, 0.6),
     'L2_xattn_ln2_b': (0.0, 0.8),
     'L2_xattn_gn_w': (1.0, 0.6),
     'L2_xattn_gn_b': (0.0, 0.8),
     'L3_xattn_bq': (0.0, 0.8),
     'L3_xattn_bk': (0.0, 2.0),
     'L3_xattn_bv': (0.0, 0.268),
     'L3_xattn_bo': (0.0, 0.1),
     'L3_xattn_gamma': (1.0, 0.2),
     'L3_xattn_beta': (0.0, 0.1)}
    factors = {'L1_xattn_q_w': 8.0,
     'L1_xattn_kv_w': 8.0,
     'L1_xattn_out_w': 6.48,
     'L2_xattn_maa_x': 8.0,
     'L2_xattn_maa_w1': 3.71,
     'L2_xattn_maa_w2': 3.724,
     'L2_xattn_td_w1': 8.0,
     'L2_xattn_td_w2': 8.0,
     'L2_xattn_u': 3.818,
     'L2_xattn_ffn_maa_k': 6.902,
     'L2_xattn_ffn_maa_r': 8.0,
     'L2_xattn_Wfr': 4.974,
     'L3_xattn_Wq': 5.772,
     'L3_xattn_Wk': 5.64}
    for name, (base, spread) in spreads.items():
        noise = np.random.default_rng([zlib.crc32(name.encode()), seed]).standard_normal(out[name].shape)
        drawn = base * np.exp(spread * noise) if base else spread * noise
        out[name] = jnp.asarray(drawn.astype(out[name].dtype))
    for name, factor in factors.items():
        out[name] = (out[name] * factor).astype(out[name].dtype)
    return out
```

```python
from contextlib import ExitStack

import concourse.bass as bass
from concourse import mybir

F32 = mybir.dt.float32
I32 = mybir.dt.int32
ALU = mybir.AluOpType
ACT = mybir.ActivationFunctionType
AX = mybir.AxisListType

B = 16
P = 128
D = 512
NC = D // P
CI = 64
H1, D1 = 16, 32
NF = 2048 // P
H2, D2 = 32, 16
NM, DM, DD = 5, 32, 64
H3, D3, KV3 = 32, 16, 8
G3 = H3 // KV3
HC = P // D3
NEG = 1.0e30

COLS = [("btheta", 1), ("bphi", 1), ("bg", 1), ("bz", 1), ("bn_gamma", 1), ("bn_beta", 1),
        ("q_b", NC), ("k_b", NC), ("v_b", NC), ("post_w", NC), ("b1", NF),
        ("ln1_w", NC), ("ln1_b", NC), ("ln2_w", NC), ("ln2_b", NC), ("maa_x", NC),
        ("maa_stack", NM * NC), ("decay", NC), ("u", NC), ("ffn_k", NC), ("ffn_r", NC),
        ("gn_w", NC), ("gn_b", NC), ("bq3", NC), ("bk3", 1), ("bv3", 1)]
ROWS = ["bo3", "gamma3", "beta3", "out_b", "b2"]
ROWS1 = 2
NCOLS = sum(n for _, n in COLS)


class Ring:

    def __init__(self, ready, free, banks, per_batch):
        self.ready, self.free, self.banks, self.per_batch = ready, free, banks, per_batch
        assert per_batch % len(banks) == 0
        self.n = 0
        self.base = 0

    def begin(self, i):
        self.base, self.n = i * self.per_batch, 0

    def read(self, i, k):
        return i * self.per_batch + k + len(self.banks)

    def written(self, i, k):
        return i * self.per_batch + k

    def next(self):
        self.bank = self.banks[self.n % len(self.banks)]
        self.n += 1
        self.count = self.base + self.n
        assert self.n <= self.per_batch
        return self.bank


class Steps:

    def __init__(self, per_batch):
        self.per_batch, self.n, self.base = per_batch, 0, 0

    def begin(self, i):
        self.base, self.n = i * self.per_batch, 0

    def tick(self):
        self.n += 1
        assert self.n <= self.per_batch, "more steps than per_batch"
        return 1

    @property
    def now(self):
        return self.base + self.n

    def end(self):
        assert self.n == self.per_batch, f"per_batch should be {self.n}"


def layer0(nc, a, PS, sem, C, cols, rows, rows1, ident, hsum, halfs, s_const, s_ident, bn_scale, bn_shift, l0_out,
           weights1, s_w1):
    with ExitStack() as ctx:
        def sb(name, shape, dt=F32):
            return ctx.enter_context(nc.sbuf_tensor(name, shape, dt))

        w0 = sb("w0", [P, 3, CI])
        wz = sb("wz", [CI, P])
        xin = sb("x_in", [P, D])
        cin = sb("ctx_in", [P, D])
        theta = sb("theta", [CI, D])
        phi = sb("phi", [CI, D])
        g = sb("g", [P, NC, CI])
        probs = sb("probs", [P, NC, D])
        probsT = sb("probsT", [P, NC, D])
        nmax = sb("nmax", [P, NC])
        rsum = sb("rsum", [P, NC])
        rinv = sb("rinv", [P, NC])
        y = sb("y", [CI, D])
        wy = sb("wy", [P, D])
        stats = sb("stats", [P, B, 6])
        mv = sb("mv", [P, 2])
        bnt = sb("bnt", [P, 2])

        s_w0 = sem("l0_weights_loaded")
        s_in = sem("l0_inputs_loaded")
        s_in_used = sem("l0_inputs_used")
        s_nmax = sem("l0_max_ready")
        s_rinv = sem("l0_rinv_ready")
        s_norm = sem("l0_probs_ready")
        s_stat = sem("l0_stats_done")
        s_store = sem("l0_wy_stored")
        s_bnv = sem("l0_bn_step")
        rings = dict(tp=([4, 5], 2), g=([6], 1), f=([0, 1], 4), t=([2, 3], 4), o=([7], 2))
        S = {k: (sem(f"l0_{k}_psum_ready"), sem(f"l0_{k}_psum_free")) for k in rings}

        def ring(k):
            return Ring(*S[k], *rings[k])

        with nc.Block() as block:
            @block.sync
            def _(sp):
                sp.dma_start(w0[:, :, :], a["w0"]).then_inc(s_w0, 16)
                sp.dma_start(wz[:, :], a["wz"]).then_inc(s_w0, 16)
                sp.dma_start(cols[:, :], a["cols"]).then_inc(s_const, 16)
                sp.dma_start(hsum[:, :], a["hsum"]).then_inc(s_const, 16)
                sp.dma_start(rows[:, :, :], a["rows"].unsqueeze(0).to_broadcast([P, len(ROWS) - ROWS1, D])).then_inc(s_const, 16)
                sp.dma_start(rows1[:, :, :], a["rows1"].unsqueeze(0).to_broadcast([P, ROWS1, D])).then_inc(s_const, 16)
                with sp.Fori(0, B) as i:
                    sp.wait_ge(s_in_used, i + 1)
                    sp.dma_start(xin[:, :], a["x"][i]).then_inc(s_in, 16)
                    sp.dma_start(cin[:, :], a["ctx"][i]).then_inc(s_in, 16)

            @block.gpsimd
            def _(pool):
                nc.gpsimd.memset(ident[:, :], 0.0).then_inc(s_ident, 1)
                nc.gpsimd.memset(halfs[:, :], -0.5).then_inc(s_ident, 1)
                pool.wait_ge(s_ident, 2)
                nc.gpsimd.affine_select(out=ident[:, :], in_=ident[:, :], compare_op=ALU.not_equal, fill=1.0,
                                        base=0, pattern=[[-1, P]], channel_multiplier=1).then_inc(s_ident, 1)
                for w, name in zip(weights1, ("q_w", "k_w", "v_w", "out_w", "mlp_w1", "mlp_w2")):
                    pool.dma_start(w[:, :, :], a[name]).then_inc(s_w1, 16)
                pool.wait_ge(s_bnv, 2)
                nc.gpsimd.tensor_tensor(bnt[:, 1:2], bnt[:, 0:1], halfs[:, 0:1], ALU.pow).then_inc(s_bnv, 1)
                pool.wait_ge(s_const, 64)
                pool.wait_ge(s_w1, 16 * 6)

            @block.tensor
            def _(pe):
                for k in rings:
                    pe.sem_inc(S[k][1], len(rings[k][0]))
                pe.sem_inc(s_in_used, 1)
                pe.sem_inc(s_store, 16)
                TP, G, F, T, O = (ring(k) for k in ("tp", "g", "f", "t", "o"))
                pe.wait_ge(s_w0, 32)
                pe.wait_ge(s_ident, 3)

                def theta_phi(i):
                    TP.begin(i)
                    pe.wait_ge(s_in, 32 * i + 32)
                    for n, x in ((0, xin), (1, cin)):
                        b = TP.next()
                        pe.wait_ge(TP.free, TP.count)
                        nc.tensor.matmul(PS[b][0:CI, :], w0[:, n, :], x[:, :], start=True, stop=True)\
                            .then_inc(TP.ready, 1)

                def g_proj(i):
                    G.begin(i)
                    b = G.next()
                    pe.wait_ge(G.free, G.count)
                    for j in range(NC):
                        mm = nc.tensor.matmul(PS[b][:, j * CI:(j + 1) * CI], xin[:, j * P:(j + 1) * P], w0[:, 2, :],
                                              start=True, stop=True)
                    mm.then_inc(G.ready, 1)
                    pe.wait_ge(G.ready, G.count)
                    pe.sem_inc(s_in_used, 1)

                def scores(i):
                    F.begin(i)
                    pe.wait_ge(TP.free, TP.read(i, 2))
                    for c in range(NC):
                        b = F.next()
                        pe.wait_ge(F.free, F.count)
                        nc.tensor.matmul(PS[b][:, :], phi[:, c * P:(c + 1) * P], theta[:, :], start=True, stop=True)\
                            .then_inc(F.ready, 1)

                def turn_probs(i):
                    T.begin(i)
                    for c in range(NC):
                        b = T.next()
                        pe.wait_ge(T.free, T.count)
                        pe.wait_ge(s_norm, NC * i + c + 1)
                        for j in range(NC):
                            mm = nc.tensor.transpose(PS[b][:, j * P:(j + 1) * P], probs[:, c, j * P:(j + 1) * P], ident[:, :])
                        mm.then_inc(T.ready, 1)

                def out_y(i):
                    O.begin(i)
                    b = O.next()
                    pe.wait_ge(O.free, O.count)
                    pe.wait_ge(G.free, G.read(i, 1))
                    pe.wait_ge(T.free, T.read(i, NC))
                    for j in range(NC):
                        mm = nc.tensor.matmul(PS[b][0:CI, :], g[:, j, :], probsT[:, j, :], start=(j == 0), stop=(j == NC - 1))
                    mm.then_inc(O.ready, 1)

                def out_z(i):
                    b = O.next()
                    pe.wait_ge(O.free, O.count)
                    pe.wait_ge(O.free, O.read(i, 1))
                    nc.tensor.matmul(PS[b][:, :], wz[:, :], y[:, :], start=True, stop=True).then_inc(O.ready, 1)

                theta_phi(0)
                g_proj(0)
                scores(0)
                with pe.Fori(1, B) as i:
                    theta_phi(i)
                    turn_probs(i - 1)
                    out_y(i - 1)
                    g_proj(i)
                    scores(i)
                    out_z(i - 1)
                turn_probs(B - 1)
                out_y(B - 1)
                out_z(B - 1)

            @block.scalar
            def _(act):
                TP, G, F, O = (ring(k) for k in ("tp", "g", "f", "o"))
                act.wait_ge(s_const, 64)

                def theta_phi(i):
                    TP.begin(i)
                    for dst, bias in ((theta, "btheta"), (phi, "bphi")):
                        b = TP.next()
                        act.wait_ge(TP.ready, TP.count)
                        nc.scalar.activation(dst[:, :], PS[b][0:CI, :], ACT.Identity, bias=C(bias, 0, CI))\
                            .then_inc(TP.free, 1)

                def copy_g(i):
                    G.begin(i)
                    b = G.next()
                    act.wait_ge(G.ready, G.count)
                    nc.scalar.activation(g[:, :, :], PS[b][:, 0:NC * CI].rearrange("p (j o) -> p j o", j=NC), ACT.Copy)\
                        .then_inc(G.free, 1)

                def exps(i):
                    F.begin(i)
                    for c in range(NC):
                        b = F.next()
                        act.wait_ge(s_nmax, NC * i + c + 1)
                        nc.scalar.activation(probs[:, c, :], PS[b][:, :], ACT.Exp, bias=nmax[:, c:c + 1],
                                             accum_out=rsum[:, c:c + 1]).then_inc(F.free, 1)

                def copy_y(i):
                    O.begin(i)
                    b = O.next()
                    act.wait_ge(O.ready, O.count)
                    nc.scalar.activation(y[:, :], PS[b][0:CI, :], ACT.Identity, bias=C("bg", 0, CI)).then_inc(O.free, 1)

                def copy_z(i):
                    b = O.next()
                    act.wait_ge(O.ready, O.count)
                    act.wait_ge(s_store, 16 * i + 16)
                    if not isinstance(i, int) or i > 0:
                        act.wait_ge(s_stat, i)
                    nc.scalar.activation(wy[:, :], PS[b][:, :], ACT.Identity, bias=C("bz")).then_inc(O.free, 1)
                    act.wait_ge(O.free, O.read(i, 2))
                    act.dma_start(l0_out[i], wy[:, :]).then_inc(s_store, 16)

                theta_phi(0)
                copy_g(0)
                exps(0)
                theta_phi(1)
                copy_y(0)
                copy_g(1)
                exps(1)
                copy_z(0)
                with act.Fori(2, B) as i:
                    theta_phi(i)
                    copy_y(i - 1)
                    copy_g(i)
                    exps(i)
                    copy_z(i - 1)
                copy_y(B - 1)
                copy_z(B - 1)
                act.wait_ge(s_store, 16 * (B + 1))

            @block.vector
            def _(dve):
                F, T, O = ring("f"), ring("t"), ring("o")

                def maxima(i):
                    F.begin(i)
                    for c in range(NC):
                        b = F.next()
                        dve.wait_ge(F.ready, F.count)
                        nc.vector.tensor_reduce(nmax[:, c:c + 1], PS[b][:, :], AX.X, ALU.max, negate=True)\
                            .then_inc(s_nmax, 1)

                def normalise(i):
                    for c in range(NC):
                        dve.wait_ge(F.free, F.read(i, c + 1))
                        nc.vector.reciprocal(rinv[:, c:c + 1], rsum[:, c:c + 1]).then_inc(s_rinv, 1)
                        dve.wait_ge(s_rinv, NC * i + c + 1)
                        nc.vector.tensor_scalar(probs[:, c, :], probs[:, c, :], rinv[:, c:c + 1], None, ALU.mult)\
                            .then_inc(s_norm, 1)

                def copy_probsT(i):
                    T.begin(i)
                    for c in range(NC):
                        b = T.next()
                        dve.wait_ge(T.ready, T.count)
                        nc.vector.tensor_copy(probsT[:, :, c * P:(c + 1) * P],
                                              PS[b][:, :].rearrange("p (j i) -> p j i", j=NC)).then_inc(T.free, 1)

                def statistics(i):
                    dve.wait_ge(O.free, O.read(i, 2))
                    nc.vector.bn_stats(stats[:, i, :], wy[:, :]).then_inc(s_stat, 1)

                maxima(0)
                normalise(0)
                with dve.Fori(1, B) as i:
                    copy_probsT(i - 1)
                    maxima(i)
                    normalise(i)
                    statistics(i - 1)
                copy_probsT(B - 1)
                statistics(B - 1)
                dve.wait_ge(s_stat, B)
                nc.vector.bn_aggr(mv[:, :], stats[:, :, :].rearrange("p b s -> p (b s)")).then_inc(s_bnv, 1)
                dve.wait_ge(s_bnv, 1)
                nc.vector.tensor_scalar(bnt[:, 0:1], mv[:, 1:2], 1e-5, None, ALU.add).then_inc(s_bnv, 1)
                dve.wait_ge(s_bnv, 3)
                nc.vector.tensor_scalar(bn_scale[:, :], bnt[:, 1:2], C("bn_gamma"), None, ALU.mult).then_inc(s_bnv, 1)
                dve.wait_ge(s_bnv, 4)
                nc.vector.tensor_scalar(bn_shift[:, :], mv[:, 0:1], bn_scale[:, :], -1.0, ALU.mult, ALU.mult)\
                    .then_inc(s_bnv, 1)
                dve.wait_ge(s_bnv, 5)
                nc.vector.tensor_scalar(bn_shift[:, :], bn_shift[:, :], C("bn_beta"), None, ALU.add).then_inc(s_bnv, 1)
                dve.wait_ge(s_bnv, 6)


def layer1(nc, a, PS, sem, C, R, cols_of, ident, halfs, bn_scale, bn_shift, l0_out, l1_out, weights):
    q_w, k_w, v_w, out_w, mlp_w1, mlp_w2 = weights
    NK = 2
    NG = H1 // 2
    DV = D1 + 1

    def pair(g):
        return [(2 * (g // 4) + e) * 4 + g % 4 for e in range(2)]

    def score_job(g):
        return g + 1 if g < 4 else 2 * (g - 4) + 6

    def turn_job(g):
        return 2 * g + 5 if g < 4 else g + 9

    with ExitStack() as ctx:
        def sb(name, shape, dt=F32):
            return ctx.enter_context(nc.sbuf_tensor(name, shape, dt))

        wyin = sb("wy_in", [P, D])
        xin = sb("x_in1", [P, D])
        maski = sb("mask_in", [P, P], I32)
        negm = sb("neg_mask", [P, NK * P])
        lat = sb("latents", [P, D])
        latb = sb("latents_out_b", [P, D])
        latb2 = sb("latents_b2", [P, D])
        hT = sb("hT", [P, NC, NK * P])
        qT = sb("qT", [P, NC, P])
        kT = sb("kT", [P, NC, NK * P])
        v = sb("v", [P, NK, H1, DV])
        probs = sb("probs1", [P, H1, NK * P])
        probsT = sb("probsT1", [P, NG, 2 * NK, P])
        nmax = sb("nmax1", [P, H1])
        rinv = sb("rinv1", [P, H1])
        attn = sb("attn", [P, D])
        attnT = sb("attnT", [P, NC, P])
        ao = sb("attn_out", [P, D])
        sq = sb("squares", [P, D])
        ss = sb("sumsq", [P, 1])
        ms = sb("mean_square", [P, 1])
        rstd = sb("rstd1", [P, 1])
        an = sb("normed", [P, D])
        nT = sb("normedT", [P, NC, P])
        gT = sb("geluT", [P, NF, P])
        xo = sb("l1_x", [P, D])

        s_in = sem("l1_inputs_loaded")
        s_ctx = sem("l1_context_loaded")
        s_mask = sem("l1_mask_loaded")
        s_bn = sem("l1_bn_applied")
        s_lat = sem("l1_latents_ready")
        s_latb = sem("l1_latents_out_b_ready")
        s_latb2 = sem("l1_latents_b2_ready")
        s_negm = sem("l1_neg_mask_ready")
        s_exp = sem("l1_exp_ready")
        s_rinv = sem("l1_rinv_ready")
        s_ss = sem("l1_sumsq_ready")
        s_ms = sem("l1_mean_square_ready")
        s_rstd = sem("l1_rstd_ready")
        s_an = sem("l1_normed_ready")
        s_ones = sem("l1_ones_made")
        s_store = sem("l1_x_stored")
        s_hold = sem("l1_wait_held")
        rings = dict(d=([0, 1], 2 * NG), a=([2, 3], 6), o=([4], 4), h=([5, 6], NF // 4), m=([7], 2))
        S = {k: (sem(f"l1_{k}_psum_ready"), sem(f"l1_{k}_psum_free")) for k in rings}

        def ring(k):
            return Ring(*S[k], *rings[k])

        with nc.Block() as block:
            @block.sync
            def _(sp):
                A, DR = ring("a"), ring("d")

                def load(i):
                    sp.dma_start(wyin[:, :], l0_out[i]).then_inc(s_in, 16)
                    sp.dma_start(xin[:, :], a["x"][i]).then_inc(s_in, 16)
                    sp.dma_start(maski[:, :], a["mask1"][i].unsqueeze(0).to_broadcast([P, P])).then_inc(s_mask, 16)
                    sp.dma_start(hT[:, :, 0:P], a["ctxT"][i]).then_inc(s_ctx, 16)

                load(0)
                with sp.Fori(1, B) as i:
                    sp.wait_ge(s_lat, i)
                    sp.wait_ge(s_negm, i)
                    sp.wait_ge(A.free, A.read(i - 1, 6))
                    load(i)

            @block.gpsimd
            def _(pool):
                M, O = ring("m"), ring("o")
                nc.gpsimd.memset(v[:, :, :, D1:DV], 1.0).then_inc(s_ones, 1)
                nc.gpsimd.memset(negm[:, P:NK * P], 0.0).then_inc(s_ones, 1)

                def batch(i, first=False):
                    pool.wait_ge(s_bn, i + 1)
                    nc.gpsimd.tensor_tensor(lat[:, :], lat[:, :], xin[:, :], ALU.add).then_inc(s_lat, 1)
                    pool.wait_ge(s_lat, i + 1)
                    if not first:
                        pool.wait_ge(O.free, O.read(i - 1, 4))
                    nc.gpsimd.tensor_tensor(latb[:, :], lat[:, :], R("out_b"), ALU.add).then_inc(s_latb, 1)
                    if not first:
                        pool.wait_ge(M.free, M.read(i - 1, 2))
                    nc.gpsimd.tensor_tensor(latb2[:, :], lat[:, :], R("b2"), ALU.add).then_inc(s_latb2, 1)
                    pool.wait_ge(s_ms, i + 1)
                    nc.gpsimd.tensor_tensor(rstd[:, :], ms[:, :], halfs[:, 0:1], ALU.pow).then_inc(s_rstd, 1)

                batch(0, True)
                with pool.Fori(1, B) as i:
                    batch(i)

            @block.tensor
            def _(pe):
                for k in rings:
                    pe.sem_inc(S[k][1], len(rings[k][0]))
                DR, A, O, H, M = (ring(k) for k in "daohm")

                def turn_latents(i):
                    A.begin(i)
                    b = A.next()
                    pe.wait_ge(A.free, A.count)
                    pe.wait_ge(s_lat, i + 1)
                    for c in range(NC):
                        mm = nc.tensor.transpose(PS[b][:, c * P:(c + 1) * P], lat[:, c * P:(c + 1) * P], ident[:, :])
                    mm.then_inc(A.ready, 1)

                def queries(i):
                    b = A.next()
                    pe.wait_ge(A.free, A.count)
                    pe.wait_ge(A.free, A.read(i, 1))
                    for m in range(NC):
                        for c in range(NC):
                            mm = nc.tensor.matmul(PS[b][:, m * P:(m + 1) * P], q_w[:, c, m * P:(m + 1) * P],
                                                  hT[:, c, P:2 * P], start=(c == 0), stop=(c == NC - 1))
                    mm.then_inc(A.ready, 1)

                def keys(i):
                    pe.wait_ge(s_ctx, 16 * i + 16)
                    for half in range(2):
                        b = A.next()
                        pe.wait_ge(A.free, A.count)
                        for e in range(2):
                            m = 2 * half + e
                            for c in range(NC):
                                mm = nc.tensor.matmul(PS[b][:, e * 256:(e + 1) * 256], k_w[:, c, m * P:(m + 1) * P],
                                                      hT[:, c, :], start=(c == 0), stop=(c == NC - 1))
                        mm.then_inc(A.ready, 1)

                def values(i):
                    for n in range(NK):
                        b = A.next()
                        pe.wait_ge(A.free, A.count)
                        for c in range(NC):
                            mm = nc.tensor.matmul(PS[b][:, :], hT[:, c, n * P:(n + 1) * P], v_w[:, c, :],
                                                  start=(c == 0), stop=(c == NC - 1))
                        mm.then_inc(A.ready, 1)

                def scores(i, g):
                    b = DR.next()
                    pe.wait_ge(DR.free, DR.count)
                    if g == 0:
                        pe.wait_ge(A.free, A.read(i, 4))
                    for e, h in enumerate(pair(g)):
                        c, r = h // 4, 32 * (h % 4)
                        mm = nc.tensor.matmul(PS[b][:, e * 256:(e + 1) * 256], qT[r:r + 32, c, :], kT[r:r + 32, c, :],
                                              start=True, stop=True)
                    mm.then_inc(DR.ready, 1)

                def turn_probs(i, g):
                    b = DR.next()
                    pe.wait_ge(DR.free, DR.count)
                    pe.wait_ge(s_exp, NG * i + g + 1)
                    for e, h in enumerate(pair(g)):
                        for n in range(NK):
                            o = (e * NK + n) * P
                            mm = nc.tensor.transpose(PS[b][:, o:o + P], probs[:, h, n * P:(n + 1) * P], ident[:, :])
                    mm.then_inc(DR.ready, 1)

                def attend(i, half):
                    b = O.next()
                    pe.wait_ge(O.free, O.count)
                    if half == 0:
                        pe.wait_ge(A.free, A.read(i, 6))
                    pe.wait_ge(DR.free, DR.read(i, turn_job(4 * half + 3)))
                    for g in range(4 * half, 4 * half + 4):
                        for e, h in enumerate(pair(g)):
                            o = (h - 8 * half) * DV
                            for n in range(NK):
                                mm = nc.tensor.matmul(PS[b][:, o:o + DV], probsT[:, g, e * NK + n, :], v[:, n, h, :],
                                                      start=(n == 0), stop=(n == NK - 1))
                    mm.then_inc(O.ready, 1)

                def turn_attn(i):
                    b = O.next()
                    pe.wait_ge(O.free, O.count)
                    pe.wait_ge(O.free, O.read(i, 2))
                    for c in range(NC):
                        mm = nc.tensor.transpose(PS[b][:, c * P:(c + 1) * P], attn[:, c * P:(c + 1) * P], ident[:, :])
                    mm.then_inc(O.ready, 1)

                def project(i):
                    b = O.next()
                    pe.wait_ge(O.free, O.count)
                    for c in range(NC):
                        mm = nc.tensor.matmul(PS[b][:, :], attnT[:, c, :], out_w[:, c, :], start=(c == 0), stop=(c == NC - 1))
                    mm.then_inc(O.ready, 1)

                def turn_normed(i):
                    M.begin(i)
                    b = M.next()
                    pe.wait_ge(M.free, M.count)
                    pe.wait_ge(s_an, i + 1)
                    for c in range(NC):
                        mm = nc.tensor.transpose(PS[b][:, c * P:(c + 1) * P], an[:, c * P:(c + 1) * P], ident[:, :])
                    mm.then_inc(M.ready, 1)

                def hidden(i, j):
                    if j == 0:
                        H.begin(i)
                        pe.wait_ge(M.free, M.read(i, 1))
                    b = H.next()
                    pe.wait_ge(H.free, H.count)
                    for f in range(4):
                        m = 4 * j + f
                        for c in range(NC):
                            mm = nc.tensor.matmul(PS[b][:, f * P:(f + 1) * P], mlp_w1[:, c, m * P:(m + 1) * P],
                                                  nT[:, c, :], start=(c == 0), stop=(c == NC - 1))
                    mm.then_inc(H.ready, 1)

                def mlp_out(i, j):
                    if j == 0:
                        b = M.next()
                        pe.wait_ge(M.free, M.count)
                    pe.wait_ge(H.free, H.read(i, j + 1))
                    for f in range(4 * j, 4 * j + 4):
                        mm = nc.tensor.matmul(PS[M.bank][:, :], gT[:, f, :], mlp_w2[:, f, :], start=(f == 0), stop=(f == NF - 1))
                    if j == 3:
                        mm.then_inc(M.ready, 1)

                def batch(i, mlp):
                    turn_latents(i)
                    if mlp:
                        turn_normed(i - 1)
                    queries(i)
                    keys(i)
                    if mlp:
                        hidden(i - 1, 0)
                        hidden(i - 1, 1)
                    values(i)
                    DR.begin(i)
                    O.begin(i)
                    scores(i, 0)
                    scores(i, 1)
                    if mlp:
                        hidden(i - 1, 2)
                        hidden(i - 1, 3)
                    scores(i, 2)
                    scores(i, 3)
                    if mlp:
                        mlp_out(i - 1, 0)
                    for g in range(4):
                        turn_probs(i, g)
                        scores(i, 4 + g)
                    if mlp:
                        mlp_out(i - 1, 1)
                    attend(i, 0)
                    for g in range(4, 8):
                        turn_probs(i, g)
                    if mlp:
                        mlp_out(i - 1, 2)
                    attend(i, 1)
                    if mlp:
                        mlp_out(i - 1, 3)
                    turn_attn(i)
                    pe.wait_ge(O.free, O.read(i, 3))
                    project(i)

                batch(0, False)
                with pe.Fori(1, B) as i:
                    batch(i, True)
                turn_normed(B - 1)
                for j in range(4):
                    hidden(B - 1, j)
                for j in range(4):
                    mlp_out(B - 1, j)

            @block.scalar
            def _(act):
                DR, A, O, H, M = (ring(k) for k in "daohm")
                act.wait_ge(s_ones, 2)

                def batch_norm(i, first=False):
                    act.wait_ge(s_in, 32 * i + 32)
                    if not first:
                        act.wait_ge(s_latb2, i)
                        act.wait_ge(A.free, A.read(i - 1, 1))
                    nc.scalar.activation(lat[:, :], wyin[:, :], ACT.Identity, bias=bn_shift[:, :], scale=bn_scale[:, :])\
                        .then_inc(s_bn, 1)

                def copy_latents(i):
                    A.begin(i)
                    b = A.next()
                    act.wait_ge(A.ready, A.count)
                    nc.scalar.activation(hT[:, :, P:2 * P], PS[b][:, :].rearrange("p (c t) -> p c t", c=NC), ACT.Copy)\
                        .then_inc(A.free, 1)

                def copy_q(i):
                    b = A.next()
                    act.wait_ge(A.ready, A.count)
                    for c in range(NC):
                        ac = nc.scalar.activation(qT[:, c, :], PS[b][:, c * P:(c + 1) * P], ACT.Identity, bias=C("q_b", c))
                    ac.then_inc(A.free, 1)

                def copy_k(i):
                    for half in range(2):
                        b = A.next()
                        act.wait_ge(A.ready, A.count)
                        for e in range(2):
                            c = 2 * half + e
                            ac = nc.scalar.activation(kT[:, c, :], PS[b][:, e * 256:(e + 1) * 256], ACT.Identity,
                                                      bias=C("k_b", c))
                        ac.then_inc(A.free, 1)

                def copy_v(i):
                    for n in range(NK):
                        b = A.next()
                        act.wait_ge(A.ready, A.count)
                        nc.scalar.activation(v[:, n, :, 0:D1], PS[b][:, :].rearrange("p (h d) -> p h d", h=H1), ACT.Copy)\
                            .then_inc(A.free, 1)

                def gelu(i, j):
                    if j == 0:
                        H.begin(i)
                    b = H.next()
                    act.wait_ge(H.ready, H.count)
                    for f in range(4):
                        ac = nc.scalar.activation(gT[:, 4 * j + f, :], PS[b][:, f * P:(f + 1) * P], ACT.Gelu_apprx_tanh,
                                                  bias=C("b1", 4 * j + f))
                    ac.then_inc(H.free, 1)

                def exps(i, g):
                    act.wait_ge(DR.free, DR.read(i, score_job(g)))
                    for h in pair(g):
                        ac = nc.scalar.activation(probs[:, h, :], probs[:, h, :], ACT.Exp, bias=nmax[:, h:h + 1],
                                                  scale=-1.0)
                    ac.then_inc(s_exp, 1)

                def squares(i):
                    act.wait_ge(O.free, O.read(i, 4))
                    nc.scalar.activation(sq[:, :], ao[:, :], ACT.Square, accum_out=ss[:, :]).then_inc(s_ss, 1)

                def store(i):
                    act.wait_ge(M.free, M.read(i, 2))
                    act.dma_start(l1_out[i], xo[:, :]).then_inc(s_store, 16)

                def batch(i, mlp):
                    copy_latents(i)
                    copy_q(i)
                    copy_k(i)
                    if mlp:
                        gelu(i - 1, 0)
                        gelu(i - 1, 1)
                    copy_v(i)
                    if mlp:
                        gelu(i - 1, 2)
                        gelu(i - 1, 3)
                    for g in range(NG):
                        exps(i, g)
                    squares(i)
                    if mlp:
                        store(i - 1)

                batch_norm(0, True)
                batch(0, False)
                with act.Fori(1, B) as i:
                    batch_norm(i)
                    batch(i, True)
                for j in range(4):
                    gelu(B - 1, j)
                store(B - 1)
                act.wait_ge(s_store, 16 * (B + 1))

            @block.vector
            def _(dve):
                DR, O, M = (ring(k) for k in "dom")
                dve.wait_ge(s_ones, 2)

                def mask(i):
                    dve.wait_ge(s_mask, 16 * i + 16)
                    nc.vector.tensor_scalar(negm[:, 0:P], maski[:, :], 0.0, -NEG, ALU.is_equal, ALU.mult)\
                        .then_inc(s_negm, 1)
                    dve.wait_ge(s_negm, i + 1)

                def maxima(i, g):
                    b = DR.next()
                    dve.wait_ge(DR.ready, DR.count)
                    dve.sem_inc(s_hold, 1)
                    for e, h in enumerate(pair(g)):
                        mx = nc.vector.tensor_tensor_reduce(probs[:, h, :], PS[b][:, e * 256:(e + 1) * 256], negm[:, :],
                                                            -1.0 / D1, 3.0e38, ALU.add, ALU.min, nmax[:, h:h + 1])
                    mx.then_inc(DR.free, 1)

                def copy_probsT(i, g):
                    b = DR.next()
                    dve.wait_ge(DR.ready, DR.count)
                    nc.vector.tensor_copy(probsT[:, g, :, :], PS[b][:, :].rearrange("p (n q) -> p n q", q=P))\
                        .then_inc(DR.free, 1)

                def normalise(i, half):
                    b = O.next()
                    dve.wait_ge(O.ready, O.count)
                    ps = PS[b][:, 0:8 * DV].rearrange("p (h d) -> p h d", d=DV)
                    r = rinv[:, 8 * half:8 * half + 8]
                    nc.vector.reciprocal(r, ps[:, :, D1]).then_inc(s_rinv, 1)
                    dve.wait_ge(s_rinv, 2 * i + half + 1)
                    nc.vector.tensor_tensor(attn[:, 256 * half:256 * half + 256].rearrange("p (h d) -> p h d", h=8),
                                            ps[:, :, 0:D1], r.unsqueeze(2).to_broadcast([P, 8, D1]), ALU.mult)\
                        .then_inc(O.free, 1)

                def copy_attnT(i):
                    b = O.next()
                    dve.wait_ge(O.ready, O.count)
                    nc.vector.tensor_tensor(attnT[:, :, :], PS[b][:, :].rearrange("p (c t) -> p c t", c=NC),
                                            cols_of("v_b").unsqueeze(2).to_broadcast([P, NC, P]), ALU.add)\
                        .then_inc(O.free, 1)

                def residual(i):
                    b = O.next()
                    dve.wait_ge(O.ready, O.count)
                    dve.wait_ge(s_latb, i + 1)
                    nc.vector.tensor_tensor(ao[:, :], PS[b][:, :], latb[:, :], ALU.add).then_inc(O.free, 1)

                def rms_norm(i):
                    dve.wait_ge(s_ss, i + 1)
                    nc.vector.tensor_scalar(ms[:, :], ss[:, :], 1.0 / D, 1e-6, ALU.mult, ALU.add).then_inc(s_ms, 1)
                    dve.wait_ge(s_rstd, i + 1)
                    nc.vector.tensor_scalar(an[:, :], ao[:, :], rstd[:, :], None, ALU.mult).then_inc(s_an, 1)

                def copy_normed(i):
                    M.begin(i)
                    b = M.next()
                    dve.wait_ge(M.ready, M.count)
                    nc.vector.tensor_tensor(nT[:, :, :], PS[b][:, :].rearrange("p (c t) -> p c t", c=NC),
                                            cols_of("post_w").unsqueeze(2).to_broadcast([P, NC, P]), ALU.mult)\
                        .then_inc(M.free, 1)

                def output(i):
                    b = M.next()
                    dve.wait_ge(M.ready, M.count)
                    dve.wait_ge(s_latb2, i + 1)
                    dve.wait_ge(s_store, 16 * i + 16)
                    nc.vector.tensor_tensor(xo[:, :], PS[b][:, :], latb2[:, :], ALU.add).then_inc(M.free, 1)

                def batch(i, mlp):
                    mask(i)
                    if mlp:
                        copy_normed(i - 1)
                    DR.begin(i)
                    O.begin(i)
                    for g in range(4):
                        maxima(i, g)
                    for g in range(4):
                        copy_probsT(i, g)
                        maxima(i, 4 + g)
                    normalise(i, 0)
                    for g in range(4, 8):
                        copy_probsT(i, g)
                    normalise(i, 1)
                    if mlp:
                        output(i - 1)
                    copy_attnT(i)
                    residual(i)
                    rms_norm(i)

                dve.sem_inc(s_store, 16)
                batch(0, False)
                with dve.Fori(1, B) as i:
                    batch(i, True)
                copy_normed(B - 1)
                output(B - 1)


def layers23(nc, a, PS, sem, C, R, CS, ident, hsum, halfs, l1_out):
    JS = D2
    LAG = 3
    V2 = 2 * D3

    with ExitStack() as ctx:
        def sb(name, shape, dt=F32):
            return ctx.enter_context(nc.sbuf_tensor(name, shape, dt))

        def flat(t):
            return t[:, :, :].rearrange("p c t -> p (c t)")

        maa_w1 = sb("maa_w1", [P, NC, NM * DM])
        maa_w2 = sb("maa_w2", [P, D])
        maa_w2b = sb("maa_w2b", [P, D])
        td_w1 = sb("td_w1", [P, NC, DD])
        td_w2 = sb("td_w2", [P, D])
        W = {n: sb(n, [P, NC, D]) for n in ("Wk", "Wv", "Wr", "Wg", "Wo", "Wfk", "Wfr", "Wfv", "Wq3", "Wo3")}
        Wk3 = sb("Wk3", [P, NC, KV3 * D3])
        Wv3 = sb("Wv3", [P, NC, KV3 * D3])
        spread = sb("spread", [P, JS, P])
        gather = sb("gather", [P, JS, P])
        blocks = sb("head_blocks", [P, 2, P])
        x = sb("x_in2", [P, D])
        row1 = sb("state_row1", [P, NC])
        st6 = sb("ln1_stats", [P, 6])
        mv = sb("ln1_mean_var", [P, 2])
        ve = sb("ln1_var_eps", [P, 1])
        rstd = sb("ln1_rstd", [P, 1])
        nx = sb("ln1_x", [P, D])
        xaT = sb("xaT", [P, NC, P + 1])
        sx = sb("shifted", [P, NC, P])
        z = sb("z", [P, NC, P])
        t5 = sb("t5", [P, NM - 1, P])
        t5b = sb("t5b", [P, P])
        xm = [sb(f"xm{f}", [P, NC, P]) for f in range(NM)]
        u1 = sb("u1", [P, P])
        kT = sb("kT2", [P, NC, P])
        rT = sb("rT2", [P, NC, P])
        vT = sb("vT2", [P, NC, P])
        wS = sb("w_shifted", [P, NC, P])
        ruk = sb("ruk", [P, NC, P])
        g = sb("g2", [P, NC, P])
        eps5 = sb("eps5", [P, 1])
        xres = sb("x_res2", [P, D])
        s0 = sb("state0", [P, NC, D2])
        row0 = sb("state_row0", [P, NC])
        bonus = sb("bonus", [P, NC, P])
        kv = [sb(f"kv{q}", [P, NC, P]) for q in range(3)]
        state = [sb(f"states{q}", [P, NC, P]) for q in range(2)]
        rs = [sb(f"r_states{q}", [P, NC, P]) for q in range(2)]
        xcT = sb("xcT", [P, NC, P + 1])
        x1 = sb("x1", [P, D])
        st6b = sb("ln2_stats", [P, 6])
        mvb = sb("ln2_mean_var", [P, 2])
        veb = sb("ln2_var_eps", [P, 1])
        rstdb = sb("ln2_rstd", [P, 1])
        x3 = sb("x3", [P, D])
        og, dev, sq, gstd, grstd = state[0], state[1], kv[0], kv[1], kv[2]
        gated = rs[0]
        nx2 = flat(rs[1])
        sx2, xk2, xr2, kk, sig = kv[0], kv[1], state[0], state[1], flat(bonus)
        ctxT = sb("ctxT3", [P, NC, P])
        mask = sb("mask3", [P, P])
        x3T = sb("x3T", [P, NC, P])
        x3b = sb("x3_bo", [P, D])
        qT = sb("qT3", [P, G3, P])
        kS = sb("kT3", [P, P])
        kbd = sb("k_blocks", [P, KV3, P])
        v3 = sb("v3", [P, KV3 // 2, 2, V2])
        sc = [sb(f"scores{q}", [P, G3, P]) for q in range(3)]
        scT = [sb(f"probsT3_{q}", [P, G3, P]) for q in range(2)]
        nmax = sb("nmax3", [P, KV3, G3])
        rsum = sb("rsum3", [P, KV3, G3])
        rinv = sb("rinv3", [P, KV3, G3])
        rrep = sb("rinv3_repeated", [P, G3, KV3, D3])
        attn = sb("attn3", [P, G3, P])
        attnT = x3T
        y = rrep[:, :, :, :].rearrange("p a b d -> p (a b d)")
        lst6 = sb("ln3_stats", [P, 6])
        lmv = sb("ln3_mean_var", [P, 2])
        lve = sb("ln3_var_eps", [P, 1])
        lrstd = sb("ln3_rstd", [P, 1])
        out = sb("out3", [P, D])

        s_w2 = sem("l2_weights_loaded")
        s_w3 = sem("l3_weights_loaded")
        s_zero = sem("l23_zeros_made")
        s_inP = sem("p_inputs_loaded")
        s_inW = sem("w_inputs_loaded")
        s_inA = sem("a_inputs_loaded")
        s_hold = sem("l23_wait_held")
        s_dveP, s_dveW, s_dveA = sem("p_dve_step"), sem("w_dve_step"), sem("a_dve_step")
        s_var1 = sem("p_ln1_var_ready")
        s_rstd1 = sem("p_ln1_rstd_ready")
        s_nx1 = sem("p_ln1_ready")
        s_first1 = sem("p_first_row1_ready")
        s_z = sem("p_z_ready")
        s_xm = sem("p_mix_ready")
        s_wS = sem("p_decay_ready")
        s_ruk = sem("p_ruk_ready")
        s_scan = sem("w_states_ready")
        s_prod = sem("w_r_states_ready")
        s_sum = sem("w_sums_done")
        s_og = sem("w_outputs_read")
        s_sq = sem("w_gn_squares_ready")
        s_grstd = sem("w_gn_rstd_ready")
        s_scaled = sem("w_gn_scaled")
        s_gnorm = sem("w_gn_normed")
        s_gated = sem("w_gated_ready")
        s_var2 = sem("w_ln2_var_ready")
        s_rstd2 = sem("w_ln2_rstd_ready")
        s_nx2 = sem("w_ln2_ready")
        s_first2 = sem("w_first_row0_ready")
        s_xk2 = sem("w_ffn_k_ready")
        s_xr2 = sem("w_ffn_r_ready")
        s_kk = sem("w_ffn_kk_ready")
        s_x3 = sem("w_x_ready")
        s_x3b = sem("a_x_bo_ready")
        s_kbd = sem("a_k_blocks_ready")
        s_max = sem("a_max_ready")
        s_exp = sem("a_exp_ready")
        s_av = sem("a_values_weighted")
        s_rinv = sem("a_rinv_ready")
        s_rrep = sem("a_rinv_repeated")
        s_attn = sem("a_attention_ready")
        s_attnT = sem("a_attention_bias_added")
        s_var3 = sem("a_ln_var_ready")
        s_rstd3 = sem("a_ln_rstd_ready")
        s_out = sem("a_out_ready")
        s_store = sem("out_stored")
        OSUM, OAV = 2, 7
        rings = dict(pd=([3], NM), pa=([4], 8), w=([0, 1], JS + 8), ad=([5], KV3 + 1), aa=([6], 4 + KV3))
        S = {k: (sem(f"{k}_psum_ready"), sem(f"{k}_psum_free")) for k in rings}
        J_XA, J_T5, J_U1, J_K, J_Z, J_R, J_V, J_G = range(1, 9)
        J_BONUS, J_MEAN = 1, JS + 2
        J_GVAR, J_WO, J_XC, J_FK, J_FR, J_FV = (J_MEAN + k for k in range(1, 7))
        J3_X, J3_Q, J3_KV, J3_RINV = 1, 2, 3, 4 + KV3
        J3_WO = KV3 + 1

        def ring(k):
            return Ring(*S[k], *rings[k])

        beside = {0: [("a_q",)], 1: [("p_xa",)], 2: [("a_kv",)], 3: [("p_shift",)], 4: [("p_t5",)],
                  5: [("a_score", 0)], 6: [("p_mix", 0), ("a_exp", 0)], 7: [("a_score", 1)],
                  8: [("p_mix", 1), ("a_turn", 0), ("a_exp", 1)], 9: [("a_score", 2)],
                  10: [("p_mix", 2), ("a_value", 0), ("a_turn", 1), ("a_exp", 2)], 11: [("a_score", 3)],
                  12: [("p_mix", 3), ("a_value", 1), ("a_turn", 2), ("a_exp", 3)], 13: [("a_score", 4)],
                  14: [("p_mix", 4), ("a_value", 2), ("a_turn", 3), ("a_exp", 4)]}
        ORDER = [("a_x",), ("p_ln1",), ("w_bonus",)]
        for j in range(JS + LAG):
            ORDER += [("w_step", j)] + beside.get(j, [])
        ORDER += [("p_u1",), ("a_score", 5), ("w_og",), ("a_exp", 5), ("p_k",), ("w_mean",), ("p_w",), ("a_value", 3),
                  ("a_turn", 4), ("w_var",), ("a_score", 6), ("p_r",), ("p_ruk",), ("w_scale",), ("w_gnorm",), ("a_exp", 6),
                  ("w_gate",), ("w_out",), ("a_value", 4), ("a_turn", 5), ("a_score", 7), ("p_v",), ("w_ln2",),
                  ("a_exp", 7), ("w_xc",), ("a_value", 5), ("a_turn", 6), ("p_g",), ("a_rinv",), ("w_fk",),
                  ("a_value", 6), ("a_turn", 7), ("w_fr",), ("p_gate",), ("a_value", 7), ("a_norm",), ("w_fv",),
                  ("a_out",), ("a_ln",), ("a_store",)]

        def steps(eng, segments, begin):
            def step(p, w, av):
                index = dict(p=p, w=w, a=av)
                for stage in "pwa":
                    if index[stage] is not None:
                        begin(stage, index[stage])
                for name, *k in ORDER:
                    if index[name[0]] is not None and name in segments:
                        segments[name](index[name[0]], *k)

            step(0, None, None)
            step(1, 0, None)
            with eng.Fori(2, B) as i:
                step(i, i - 1, i - 2)
            step(None, B - 1, B - 2)
            step(None, None, B - 1)

        with nc.Block() as block:
            @block.sync
            def _(sp):
                def load_p(i):
                    sp.dma_start(x[:, :], l1_out[i]).then_inc(s_inP, 16)
                    sp.dma_start(row1[:, :], a["row1"][i]).then_inc(s_inP, 16)

                def load_w(i):
                    sp.dma_start(s0[:, :, :], a["state"][i]).then_inc(s_inW, 16)
                    sp.dma_start(xres[:, :], l1_out[i]).then_inc(s_inW, 16)
                    sp.dma_start(row0[:, :], a["row0"][i]).then_inc(s_inW, 16)

                def load_a(i):
                    sp.dma_start(ctxT[:, :, :], a["ctxT"][i]).then_inc(s_inA, 16)
                    sp.dma_start(mask[:, :], a["mask3"][i]).then_inc(s_inA, 16)

                def reload_p(i):
                    sp.wait_ge(s_nx1, i)
                    sp.wait_ge(s_first1, i)
                    load_p(i)

                def reload_w(i):
                    sp.wait_ge(s_scan, JS * i)
                    sp.wait_ge(s_var2, i)
                    sp.wait_ge(s_first2, i)
                    load_w(i)

                def reload_a(i):
                    sp.wait_ge(s_max, KV3 * i)
                    load_a(i)

                load_p(0)
                sp.dma_start(maa_w1[:, :, :], a["maa_w1"]).then_inc(s_w2, 16)
                sp.dma_start(maa_w2[:, :], a["maa_w2"][0:P]).then_inc(s_w2, 16)
                sp.dma_start(maa_w2b[:, :], a["maa_w2"][P:2 * P]).then_inc(s_w2, 16)
                sp.dma_start(td_w1[:, :, :], a["td_w1"]).then_inc(s_w2, 16)
                sp.dma_start(td_w2[:, :], a["td_w2"]).then_inc(s_w2, 16)
                for n in ("Wk", "Wr", "Wv", "Wg"):
                    sp.dma_start(W[n][:, :, :], a[n]).then_inc(s_w2, 16)
                load_w(0)
                reload_p(1)
                for t, n in ((spread, "spread"), (gather, "gather"), (blocks, "blocks"), (W["Wo"], "Wo"),
                             (W["Wfk"], "Wfk"), (W["Wfr"], "Wfr"), (W["Wfv"], "Wfv"), (W["Wq3"], "Wq3"),
                             (Wk3, "Wk3"), (Wv3, "Wv3"), (W["Wo3"], "Wo3")):
                    sp.dma_start(t[:, :, :], a[n]).then_inc(s_w3, 16)
                load_a(0)
                reload_w(1)
                with sp.Fori(2, B) as i:
                    reload_p(i)
                    reload_a(i - 1)
                    reload_w(i)
                reload_a(B - 1)

            @block.gpsimd
            def _(pool):
                PD, PA, WR, AA = ring("pd"), ring("pa"), ring("w"), ring("aa")
                for t in (t5[:, :, :], t5b[:, :], u1[:, :], wS[:, :, 0:1], v3[:, :, :, :]):
                    nc.gpsimd.memset(t, 0.0).then_inc(s_zero, 1)
                nc.gpsimd.memset(eps5[:, :], 1e-5).then_inc(s_zero, 1)

                def power(dst, src):
                    return nc.gpsimd.tensor_tensor(dst, src, halfs[:, 0:1], ALU.pow)

                def p_ln1(i):
                    pool.wait_ge(s_inP, 32 * i + 32)
                    if not isinstance(i, int) or i > 0:
                        pool.wait_ge(s_z, i)
                    pool.sem_inc(s_hold, 1)
                    nc.gpsimd.tensor_copy(xaT[:, :, 0], row1[:, :]).then_inc(s_first1, 1)
                    pool.wait_ge(s_var1, i + 1)
                    power(rstd[:, :], ve[:, :]).then_inc(s_rstd1, 1)

                def p_mix(i, f):
                    pool.wait_ge(PD.free, PD.read(i, f + 1))
                    nc.gpsimd.tensor_tensor(xm[f][:, :, :], xm[f][:, :, :], xaT[:, :, 1:P + 1], ALU.add)\
                        .then_inc(s_xm, 1)

                def w_step(i, j):
                    if not 1 <= j <= JS:
                        return
                    j -= 1
                    pool.wait_ge(s_scan, JS * i + j + 1)
                    if j >= 2:
                        pool.wait_ge(s_sum, JS * i + j - 1)
                    nc.gpsimd.tensor_tensor(rs[j % 2][:, :, :], state[j % 2][:, :, :], rT[:, :, :], ALU.mult)\
                        .then_inc(s_prod, 1)

                def w_out(i):
                    pool.wait_ge(s_inW, 48 * i + 48)
                    pool.sem_inc(s_hold, 1)
                    nc.gpsimd.tensor_copy(xcT[:, :, 0], row0[:, :]).then_inc(s_first2, 1)
                    pool.wait_ge(s_var2, i + 1)
                    power(rstdb[:, :], veb[:, :]).then_inc(s_rstd2, 1)

                def a_x(i):
                    pool.wait_ge(s_x3, i + 1)
                    nc.gpsimd.tensor_tensor(x3b[:, :], x3[:, :], R("bo3"), ALU.add).then_inc(s_x3b, 1)

                def a_kv(i):
                    pool.wait_ge(AA.free, AA.read(i, J3_KV))
                    nc.gpsimd.tensor_tensor(kbd[:, :, :], kS[:, :].unsqueeze(1).to_broadcast([P, KV3, P]),
                                            hsum[:, :].unsqueeze(2).to_broadcast([P, KV3, P]), ALU.mult)\
                        .then_inc(s_kbd, 1)

                def a_norm(i):
                    pool.wait_ge(s_rinv, i + 1)
                    pool.sem_inc(s_hold, 1)
                    nc.gpsimd.tensor_copy(rrep[:, :, :, :], rinv[:, :, :].rearrange("p g c -> p c g").unsqueeze(3)
                                          .to_broadcast([P, G3, KV3, D3])).then_inc(s_rrep, 1)

                def a_out(i):
                    pool.wait_ge(s_var3, i + 1)
                    power(lrstd[:, :], lve[:, :]).then_inc(s_rstd3, 1)

                steps(pool, dict(p_ln1=p_ln1, p_mix=p_mix, w_step=w_step, w_out=w_out, a_x=a_x,
                                 a_kv=a_kv, a_norm=a_norm, a_out=a_out), lambda stage, i: None)

            @block.tensor
            def _(pe):
                for k in rings:
                    pe.sem_inc(S[k][1], len(rings[k][0]))
                pe.sem_inc(s_og, 1)
                pe.sem_inc(s_attn, 1)
                PD, PA, WR, AD, AA = (ring(k) for k in ("pd", "pa", "w", "ad", "aa"))

                def begin(stage, i):
                    for r in dict(p=(PD, PA), w=(WR,), a=(AD, AA))[stage]:
                        r.begin(i)
                    if stage == "w" and isinstance(i, int) and i == 0:
                        pe.wait_ge(s_w3, 16 * 11)

                def turn4(r, src):
                    b = r.next()
                    pe.wait_ge(r.free, r.count)
                    for c in range(NC):
                        mm = nc.tensor.transpose(PS[b][:, c * P:(c + 1) * P], src[:, c * P:(c + 1) * P], ident[:, :])
                    mm.then_inc(r.ready, 1)

                def channel_major(r, w, xT):
                    b = r.next()
                    pe.wait_ge(r.free, r.count)
                    for m in range(NC):
                        for c in range(NC):
                            mm = nc.tensor.matmul(PS[b][:, m * P:(m + 1) * P], w[:, c, m * P:(m + 1) * P], xT[:, c, :],
                                                  start=(c == 0), stop=(c == NC - 1))
                    mm.then_inc(r.ready, 1)

                def token_major(r, w, xT):
                    b = r.next()
                    pe.wait_ge(r.free, r.count)
                    for c in range(NC):
                        mm = nc.tensor.matmul(PS[b][:, :], xT[:, c, :], w[:, c, :], start=(c == 0), stop=(c == NC - 1))
                    mm.then_inc(r.ready, 1)

                def over_head(r, k, src):
                    b = r.next()
                    pe.wait_ge(r.free, r.count)
                    nc.tensor.matmul(PS[b][:, :], blocks[:, k, :], flat(src), start=True, stop=True).then_inc(r.ready, 1)

                def p_xa(i):
                    pe.wait_ge(s_nx1, i + 1)
                    turn4(PA, nx)

                def p_t5(i):
                    b = PA.next()
                    pe.wait_ge(PA.free, PA.count)
                    pe.wait_ge(s_z, i + 1)
                    for c in range(NC):
                        nc.tensor.matmul(PS[b][:, 0:P], maa_w1[:, c, 0:P], z[:, c, :], start=(c == 0), stop=(c == NC - 1))
                    for c in range(NC):
                        mm = nc.tensor.matmul(PS[b][0:DM, P:2 * P], maa_w1[:, c, P:P + DM], z[:, c, :],
                                              start=(c == 0), stop=(c == NC - 1))
                    mm.then_inc(PA.ready, 1)

                def p_mix(i, f):
                    b = PD.next()
                    pe.wait_ge(PD.free, PD.count)
                    if f == 0:
                        pe.wait_ge(PA.free, PA.read(i, J_T5))
                    w, t = (maa_w2, t5[:, f, :]) if f < NM - 1 else (maa_w2b, t5b[:, :])
                    for m in range(NC):
                        mm = nc.tensor.matmul(PS[b][:, m * P:(m + 1) * P], w[:, m * P:(m + 1) * P], t, start=True, stop=True)
                    mm.then_inc(PD.ready, 1)

                def p_u1(i):
                    b = PA.next()
                    pe.wait_ge(PA.free, PA.count)
                    pe.wait_ge(s_xm, NM * i + 2)
                    for c in range(NC):
                        mm = nc.tensor.matmul(PS[b][0:DD, 0:P], td_w1[:, c, :], xm[1][:, c, :], start=(c == 0), stop=(c == NC - 1))
                    mm.then_inc(PA.ready, 1)

                def p_w(i):
                    b = PA.next()
                    pe.wait_ge(PA.free, PA.count)
                    pe.wait_ge(PA.free, PA.read(i, J_U1))
                    for m in range(NC):
                        mm = nc.tensor.matmul(PS[b][:, m * P:(m + 1) * P], td_w2[:, m * P:(m + 1) * P], u1[:, :], start=True, stop=True)
                    mm.then_inc(PA.ready, 1)

                def projected(f, w):
                    def seg(i):
                        pe.wait_ge(s_xm, NM * i + f + 1)
                        channel_major(PA, W[w], xm[f])
                    return seg

                def w_bonus(i):
                    pe.wait_ge(s_ruk, i + 1)
                    over_head(WR, 0, ruk)

                def w_step(i, j):
                    if j < JS:
                        b = WR.next()
                        pe.wait_ge(WR.free, WR.count)
                        nc.tensor.matmul(PS[b][:, :], spread[:, j, :], flat(vT), start=True, stop=True).then_inc(WR.ready, 1)
                    if j >= LAG:
                        j -= LAG
                        if j == 0:
                            pe.wait_ge(s_og, i + 1)
                        pe.wait_ge(s_prod, JS * i + j + 1)
                        nc.tensor.matmul(PS[OSUM][:, :], gather[:, j, :], flat(rs[j % 2]), start=(j == 0), stop=(j == JS - 1))\
                            .then_inc(s_sum, 1)

                def w_mean(i):
                    pe.wait_ge(s_og, i + 2)
                    over_head(WR, 1, og)

                def w_var(i):
                    pe.wait_ge(s_sq, i + 1)
                    over_head(WR, 1, sq)

                def w_out(i):
                    pe.wait_ge(s_gated, i + 1)
                    token_major(WR, W["Wo"], gated)

                def w_xc(i):
                    pe.wait_ge(s_nx2, i + 1)
                    turn4(WR, nx2)

                def w_fk(i):
                    pe.wait_ge(s_xk2, i + 1)
                    channel_major(WR, W["Wfk"], xk2)

                def w_fr(i):
                    pe.wait_ge(s_xr2, i + 1)
                    token_major(WR, W["Wfr"], xr2)

                def w_fv(i):
                    pe.wait_ge(s_kk, i + 1)
                    token_major(WR, W["Wfv"], kk)

                def a_x(i):
                    pe.wait_ge(s_x3, i + 1)
                    turn4(AA, x3)

                def a_q(i):
                    pe.wait_ge(AA.free, AA.read(i, J3_X))
                    channel_major(AA, W["Wq3"], x3T)

                def a_kv(i):
                    b = AA.next()
                    pe.wait_ge(AA.free, AA.count)
                    pe.wait_ge(s_inA, 32 * i + 32)
                    for c in range(NC):
                        nc.tensor.matmul(PS[b][:, 0:P], Wk3[:, c, :], ctxT[:, c, :], start=(c == 0), stop=(c == NC - 1))
                    for c in range(NC):
                        mm = nc.tensor.matmul(PS[b][:, P:2 * P], ctxT[:, c, :], Wv3[:, c, :], start=(c == 0), stop=(c == NC - 1))
                    mm.then_inc(AA.ready, 1)

                def a_score(i, u):
                    b = AD.next()
                    pe.wait_ge(AD.free, AD.count)
                    if u == 0:
                        pe.wait_ge(s_kbd, i + 1)
                    for c in range(G3):
                        mm = nc.tensor.matmul(PS[b][:, c * P:(c + 1) * P], qT[:, c, :], kbd[:, u, :], start=True, stop=True)
                    mm.then_inc(AD.ready, 1)

                def a_turn(i, u):
                    pe.wait_ge(s_exp, KV3 * i + u + 1)
                    turn4(AA, flat(sc[u % 3]))

                def a_value(i, u):
                    if u == 0:
                        pe.wait_ge(s_attn, i + 1)
                    pe.wait_ge(AA.free, AA.read(i, J3_KV + 1 + u))
                    nc.tensor.matmul(PS[OAV][V2 * (u // 2):V2 * (u // 2 + 1), :], v3[:, u // 2, u % 2, :], flat(scT[u % 2]),
                                     start=(u % 2 == 0), stop=(u % 2 == 1)).then_inc(s_av, 1)

                def a_norm(i):
                    pe.wait_ge(s_rrep, i + 1)
                    turn4(AA, y)

                def a_out(i):
                    pe.wait_ge(s_attnT, i + 1)
                    token_major(AD, W["Wo3"], attnT)

                pe.wait_ge(s_w2, 16 * 9)
                steps(pe, dict(p_xa=p_xa, p_t5=p_t5, p_mix=p_mix, p_u1=p_u1, p_w=p_w, p_k=projected(0, "Wk"),
                               p_r=projected(3, "Wr"), p_v=projected(2, "Wv"), p_g=projected(4, "Wg"),
                               w_bonus=w_bonus, w_step=w_step, w_mean=w_mean, w_var=w_var, w_out=w_out, w_xc=w_xc,
                               w_fk=w_fk, w_fr=w_fr, w_fv=w_fv, a_x=a_x, a_q=a_q, a_kv=a_kv, a_score=a_score,
                               a_turn=a_turn, a_value=a_value, a_norm=a_norm, a_out=a_out), begin)

            @block.scalar
            def _(act):
                PD, PA, WR, AA = ring("pd"), ring("pa"), ring("w"), ring("aa")
                act.wait_ge(s_zero, 6)

                def begin(stage, i):
                    dict(p=PA, w=WR, a=AA)[stage].begin(i)

                def c4(ps):
                    return ps[:, :].rearrange("p (c t) -> p c t", c=NC)

                def next_bank(r):
                    b = r.next()
                    act.wait_ge(r.ready, r.count)
                    return PS[b]

                def later(i):
                    return not isinstance(i, int) or i > 0

                def scaled(dst, ps, w, b, free):
                    for c in range(NC):
                        ac = nc.scalar.activation(dst[:, c, 1:P + 1], ps[:, c * P:(c + 1) * P], ACT.Identity,
                                                  bias=C(b, c), scale=C(w, c))
                    ac.then_inc(free, 1)

                def p_xa(i):
                    ps = next_bank(PA)
                    if later(i):
                        act.wait_ge(s_xm, NM * i)
                    scaled(xaT, ps, "ln1_w", "ln1_b", PA.free)

                def p_t5(i):
                    ps = next_bank(PA)
                    if later(i):
                        act.wait_ge(PD.ready, PD.written(i - 1, NM))
                    for f in range(NM - 1):
                        rows = slice(DM * f, DM * f + DM)
                        nc.scalar.activation(t5[rows, f, :], ps[rows, 0:P], ACT.Tanh)
                    nc.scalar.activation(t5b[0:DM, :], ps[0:DM, P:2 * P], ACT.Tanh).then_inc(PA.free, 1)

                def p_u1(i):
                    ps = next_bank(PA)
                    nc.scalar.activation(u1[0:DD, :], ps[0:DD, 0:P], ACT.Tanh).then_inc(PA.free, 1)

                def p_w(i):
                    ps = next_bank(PA)
                    for c in range(NC):
                        ac = nc.scalar.activation(z[:, c, :], ps[:, c * P:(c + 1) * P], ACT.Exp, bias=C("decay", c))
                    ac.then_inc(PA.free, 1)
                    act.wait_ge(PA.free, PA.read(i, J_Z))
                    if later(i):
                        act.wait_ge(s_scan, JS * i)
                    nc.scalar.activation(wS[:, :, 1:P], z[:, :, 0:P - 1], ACT.Exp, scale=-1.0).then_inc(s_wS, 1)

                def p_k(i):
                    ps = next_bank(PA)
                    if later(i):
                        act.wait_ge(s_scan, JS * i)
                    nc.scalar.activation(kT[:, :, :], c4(ps), ACT.Copy).then_inc(PA.free, 1)

                def p_r(i):
                    ps = next_bank(PA)
                    if later(i):
                        act.wait_ge(s_prod, JS * i)
                    nc.scalar.activation(rT[:, :, :], c4(ps), ACT.Copy).then_inc(PA.free, 1)

                def p_v(i):
                    ps = next_bank(PA)
                    nc.scalar.activation(vT[:, :, :], c4(ps), ACT.Copy).then_inc(PA.free, 1)

                def p_g(i):
                    ps = next_bank(PA)
                    nc.scalar.activation(z[:, :, :], c4(ps), ACT.Tanh, scale=0.5)
                    if later(i):
                        act.wait_ge(s_gated, i)
                    nc.scalar.activation(g[:, :, :], c4(ps), ACT.Copy).then_inc(PA.free, 1)

                def w_mean(i):
                    WR.n += 1 + JS + 1
                    act.wait_ge(WR.free, WR.read(i, J_MEAN))
                    nc.scalar.activation(sq[:, :, :], dev[:, :, :], ACT.Square).then_inc(s_sq, 1)

                def w_var(i):
                    nc.scalar.activation(gstd[:, :, :], c4(next_bank(WR)), ACT.Sqrt, bias=eps5[:, :]).then_inc(WR.free, 1)

                def w_gnorm(i):
                    WR.n += 1
                    act.wait_ge(s_scaled, i + 1)
                    for c in range(NC):
                        ac = nc.scalar.activation(dev[:, c, :], dev[:, c, :], ACT.Identity, bias=C("gn_b", c), scale=C("gn_w", c))
                    ac.then_inc(s_gnorm, 1)

                def w_xc(i):
                    scaled(xcT, next_bank(WR), "ln2_w", "ln2_b", WR.free)

                def w_fk(i):
                    nc.scalar.activation(kk[:, :, :], c4(next_bank(WR)), ACT.Relu).then_inc(WR.free, 1)
                    act.wait_ge(WR.free, WR.read(i, J_FK))
                    nc.scalar.activation(kk[:, :, :], kk[:, :, :], ACT.Square).then_inc(s_kk, 1)

                def w_fr(i):
                    nc.scalar.activation(sig, next_bank(WR)[:, :], ACT.Tanh, scale=0.5).then_inc(WR.free, 1)

                def a_x(i):
                    nc.scalar.activation(x3T[:, :, :], c4(next_bank(AA)), ACT.Copy).then_inc(AA.free, 1)

                def a_q(i):
                    ps = next_bank(AA)
                    for c in range(G3):
                        ac = nc.scalar.activation(qT[:, c, :], ps[:, c * P:(c + 1) * P], ACT.Identity, bias=C("bq3", c))
                    ac.then_inc(AA.free, 1)

                def a_kv(i):
                    ps = next_bank(AA)
                    nc.scalar.activation(kS[:, :], ps[:, 0:P], ACT.Identity, bias=C("bk3"))
                    vals = ps[:, P:2 * P].rearrange("p (g two d) -> p g two d", two=2, d=D3)
                    nc.scalar.activation(v3[:, :, 0, 0:D3], vals[:, :, 0, :], ACT.Copy)
                    nc.scalar.activation(v3[:, :, 1, D3:V2], vals[:, :, 1, :], ACT.Copy).then_inc(AA.free, 1)

                def a_exp(i, u):
                    act.wait_ge(s_max, KV3 * i + u + 1)
                    for c in range(G3):
                        s = sc[u % 3][:, c, :]
                        ac = nc.scalar.activation(s, s, ACT.Exp, bias=nmax[:, u, c:c + 1], accum_out=rsum[:, u, c:c + 1])
                    ac.then_inc(s_exp, 1)

                def a_turn(i, u):
                    ps = next_bank(AA)
                    if u >= 2:
                        act.wait_ge(s_av, KV3 * i + u - 1)
                    nc.scalar.activation(scT[u % 2][:, :, :], c4(ps), ACT.Copy).then_inc(AA.free, 1)

                def a_norm(i):
                    nc.scalar.activation(attn[:, :, :], c4(next_bank(AA)), ACT.Copy).then_inc(AA.free, 1)
                    act.wait_ge(s_attn, i + 2)
                    nc.scalar.activation(attnT[:, :, :], attn[:, :, :], ACT.Identity, bias=C("bv3")).then_inc(s_attnT, 1)

                def a_out(i):
                    act.wait_ge(s_out, i + 1)
                    act.dma_start(a["out"][i], out[:, :]).then_inc(s_store, 16)

                steps(act, dict(p_xa=p_xa, p_t5=p_t5, p_u1=p_u1, p_w=p_w, p_k=p_k, p_r=p_r, p_v=p_v, p_g=p_g,
                                w_mean=w_mean, w_var=w_var, w_gnorm=w_gnorm, w_xc=w_xc, w_fk=w_fk, w_fr=w_fr, a_x=a_x, a_q=a_q,
                                a_kv=a_kv, a_exp=a_exp, a_turn=a_turn, a_norm=a_norm, a_store=a_out), begin)
                act.wait_ge(s_store, 16 * (B + 1))

            @block.vector
            def _(dve):
                PD, PA, WR, AD, AA = (ring(k) for k in ("pd", "pa", "w", "ad", "aa"))
                E = dict(p=Steps(4), w=Steps(3), a=Steps(4))
                dve.sem_inc(s_store, 16)

                def begin(stage, i):
                    for r in dict(p=(PD,), w=(WR,), a=(AD,))[stage]:
                        r.begin(i)
                    E[stage].begin(i)

                def next_bank(r):
                    b = r.next()
                    dve.wait_ge(r.ready, r.count)
                    return PS[b]

                def c4(ps):
                    return ps[:, :].rearrange("p (c t) -> p c t", c=NC)

                def layer_norm_stats(src, t6, tmv, tve, eps, steps, s_step, s_var):
                    nc.vector.bn_stats(t6[:, :], src).then_inc(s_step, steps.tick())
                    dve.wait_ge(s_step, steps.now)
                    dve.sem_inc(s_hold, 1)
                    nc.vector.bn_aggr(tmv[:, :], t6[:, :]).then_inc(s_step, steps.tick())
                    dve.wait_ge(s_step, steps.now)
                    nc.vector.tensor_scalar(tve[:, :], tmv[:, 1:2], eps, None, ALU.add).then_inc(s_var, 1)

                def p_ln1(i):
                    dve.wait_ge(s_inP, 32 * i + 32)
                    layer_norm_stats(x[:, :], st6, mv, ve, 1e-5, E["p"], s_dveP, s_var1)

                def p_xa(i):
                    dve.wait_ge(s_rstd1, i + 1)
                    nc.vector.tensor_scalar(nx[:, :], x[:, :], mv[:, 0:1], rstd[:, :], ALU.subtract, ALU.mult)\
                        .then_inc(s_nx1, 1)

                def p_shift(i):
                    dve.wait_ge(PA.free, PA.read(i, J_XA))
                    dve.wait_ge(s_first1, i + 1)
                    nc.vector.tensor_tensor(sx[:, :, :], xaT[:, :, 0:P], xaT[:, :, 1:P + 1], ALU.subtract)\
                        .then_inc(s_dveP, E["p"].tick())
                    dve.wait_ge(s_dveP, E["p"].now)
                    for c in range(NC):
                        v_ = nc.vector.scalar_tensor_tensor(out=z[:, c, :], in0=sx[:, c, :], scalar=C("maa_x", c),
                                                            in1=xaT[:, c, 1:P + 1], op0=ALU.mult, op1=ALU.add)
                    v_.then_inc(s_z, 1)

                def p_mix(i, f):
                    ps = next_bank(PD)
                    for c in range(NC):
                        v_ = nc.vector.scalar_tensor_tensor(out=xm[f][:, c, :], in0=ps[:, c * P:(c + 1) * P],
                                                            scalar=C("maa_stack", f * NC + c), in1=sx[:, c, :],
                                                            op0=ALU.add, op1=ALU.mult)
                    v_.then_inc(PD.free, 1)

                def p_ruk(i):
                    dve.wait_ge(PA.free, PA.read(i, J_R))
                    for c in range(NC):
                        v_ = nc.vector.scalar_tensor_tensor(out=ruk[:, c, :], in0=kT[:, c, :], scalar=C("u", c),
                                                            in1=rT[:, c, :], op0=ALU.mult, op1=ALU.mult)
                    v_.then_inc(s_ruk, 1)

                def p_gate(i):
                    dve.wait_ge(PA.free, PA.read(i, J_G))
                    nc.vector.scalar_tensor_tensor(out=g[:, :, :], in0=z[:, :, :], scalar=1.0, in1=g[:, :, :],
                                                   op0=ALU.add, op1=ALU.mult).then_inc(s_dveP, E["p"].tick())
                    E["p"].end()

                def w_bonus(i):
                    ps = next_bank(WR)
                    dve.wait_ge(PA.free, PA.read(i, J_V))
                    nc.vector.tensor_tensor(bonus[:, :, :], c4(ps), vT[:, :, :], ALU.mult).then_inc(WR.free, 1)
                    dve.wait_ge(s_wS, i + 1)
                    dve.wait_ge(s_inW, 48 * i + 48)

                def w_step(i, j):
                    if j < JS:
                        if j >= 3:
                            dve.wait_ge(s_scan, JS * i + j - 2)
                        nc.vector.tensor_copy(kv[j % 3][:, :, 0], s0[:, :, j])
                        ps = next_bank(WR)
                        nc.vector.tensor_tensor(kv[j % 3][:, :, 1:P], c4(ps)[:, :, 0:P - 1], kT[:, :, 0:P - 1], ALU.mult)\
                            .then_inc(WR.free, 1)
                    if 1 <= j <= JS:
                        j -= 1
                        if j >= 2:
                            dve.wait_ge(s_prod, JS * i + j - 1)
                        dve.wait_ge(WR.free, WR.read(i, J_BONUS + 1 + j))
                        nc.vector.tensor_tensor_scan(flat(state[j % 2]), flat(wS), flat(kv[j % 3]), 0.0,
                                                     ALU.mult, ALU.add).then_inc(s_scan, 1)

                def w_og(i):
                    dve.wait_ge(s_sum, JS * i + JS)
                    nc.vector.tensor_tensor(og[:, :, :], c4(PS[OSUM]), bonus[:, :, :], ALU.add).then_inc(s_og, 1)

                def w_mean(i):
                    ps = next_bank(WR)
                    dve.wait_ge(s_og, i + 2)
                    nc.vector.tensor_tensor(dev[:, :, :], og[:, :, :], c4(ps), ALU.subtract).then_inc(WR.free, 1)

                def w_scale(i):
                    WR.n += 1
                    dve.wait_ge(WR.free, WR.read(i, J_GVAR))
                    nc.vector.reciprocal(grstd[:, :, :], gstd[:, :, :]).then_inc(s_grstd, 1)
                    dve.wait_ge(s_grstd, i + 1)
                    nc.vector.tensor_tensor(dev[:, :, :], dev[:, :, :], grstd[:, :, :], ALU.mult).then_inc(s_scaled, 1)

                def w_gate(i):
                    dve.wait_ge(s_gnorm, i + 1)
                    nc.vector.scalar_tensor_tensor(out=gated[:, :, :], in0=dev[:, :, :], scalar=0.5, in1=g[:, :, :],
                                                   op0=ALU.mult, op1=ALU.mult).then_inc(s_gated, 1)

                def w_out(i):
                    nc.vector.tensor_tensor(x1[:, :], next_bank(WR)[:, :], xres[:, :], ALU.add).then_inc(WR.free, 1)
                    dve.wait_ge(WR.free, WR.read(i, J_WO))
                    layer_norm_stats(x1[:, :], st6b, mvb, veb, 1e-5, E["w"], s_dveW, s_var2)

                def w_ln2(i):
                    dve.wait_ge(s_rstd2, i + 1)
                    nc.vector.tensor_scalar(nx2, x1[:, :], mvb[:, 0:1], rstdb[:, :], ALU.subtract, ALU.mult)\
                        .then_inc(s_nx2, 1)

                def w_xc(i):
                    dve.wait_ge(WR.free, WR.read(i, J_XC))
                    dve.wait_ge(s_first2, i + 1)
                    nc.vector.tensor_tensor(sx2[:, :, :], xcT[:, :, 0:P], xcT[:, :, 1:P + 1], ALU.subtract)\
                        .then_inc(s_dveW, E["w"].tick())
                    dve.wait_ge(s_dveW, E["w"].now)
                    for dst, name, done in ((xk2, "ffn_k", s_xk2), (xr2, "ffn_r", s_xr2)):
                        for c in range(NC):
                            v_ = nc.vector.scalar_tensor_tensor(out=dst[:, c, :], in0=sx2[:, c, :], scalar=C(name, c),
                                                                in1=xcT[:, c, 1:P + 1], op0=ALU.mult, op1=ALU.add)
                        v_.then_inc(done, 1)
                    E["w"].end()

                def w_fv(i):
                    WR.n += 3
                    ps = next_bank(WR)
                    dve.wait_ge(WR.free, WR.read(i, J_FR))
                    nc.vector.scalar_tensor_tensor(out=sig, in0=sig, scalar=1.0, in1=ps[:, :],
                                                   op0=ALU.add, op1=ALU.mult).then_inc(WR.free, 1)
                    dve.wait_ge(WR.free, WR.read(i, J_FV))
                    if later(i):
                        dve.wait_ge(s_x3b, i)
                        dve.wait_ge(AA.ready, AA.written(i - 1, J3_X))
                    nc.vector.scalar_tensor_tensor(out=x3[:, :], in0=sig, scalar=0.5, in1=x1[:, :],
                                                   op0=ALU.mult, op1=ALU.add).then_inc(s_x3, 1)

                def later(i):
                    return not isinstance(i, int) or i > 0

                def a_score(i, u):
                    ps = next_bank(AD)
                    if u >= 3:
                        dve.wait_ge(AA.ready, AA.written(i, J3_KV + 1 + u - 3))
                    s = sc[u % 3]
                    nc.vector.scalar_tensor_tensor(out=s[:, :, :], in0=c4(ps), scalar=0.25,
                                                   in1=mask[:, :].unsqueeze(1).to_broadcast([P, G3, P]),
                                                   op0=ALU.mult, op1=ALU.add).then_inc(AD.free, 1)
                    dve.wait_ge(AD.free, AD.read(i, u + 1))
                    nc.vector.tensor_reduce(nmax[:, u, :], s[:, :, :], AX.X, ALU.max, negate=True).then_inc(s_max, 1)

                def a_rinv(i):
                    dve.wait_ge(s_exp, KV3 * i + KV3)
                    nc.vector.reciprocal(rinv[:, :, :], rsum[:, :, :]).then_inc(s_rinv, 1)

                def a_norm(i):
                    dve.wait_ge(s_av, KV3 * i + KV3)
                    dve.wait_ge(AA.free, AA.read(i, J3_RINV))
                    nc.vector.tensor_tensor(attn[:, :, :], c4(PS[OAV]), attn[:, :, :], ALU.mult).then_inc(s_attn, 1)

                def a_out(i):
                    ps = next_bank(AD)
                    dve.wait_ge(s_x3b, i + 1)
                    nc.vector.tensor_tensor(y, ps[:, :], x3b[:, :], ALU.add).then_inc(AD.free, 1)
                    dve.wait_ge(AD.free, AD.read(i, J3_WO))
                    layer_norm_stats(y, lst6, lmv, lve, 1e-6, E["a"], s_dveA, s_var3)

                def a_ln(i):
                    dve.wait_ge(s_rstd3, i + 1)
                    nc.vector.tensor_scalar(y, y, lmv[:, 0:1], lrstd[:, :], ALU.subtract, ALU.mult)\
                        .then_inc(s_dveA, E["a"].tick())
                    dve.wait_ge(s_dveA, E["a"].now)
                    dve.wait_ge(s_store, 16 * i + 16)
                    nc.vector.tensor_tensor(out[:, :], y, R("gamma3"), ALU.mult).then_inc(s_dveA, E["a"].tick())
                    dve.wait_ge(s_dveA, E["a"].now)
                    nc.vector.tensor_tensor(out[:, :], out[:, :], R("beta3"), ALU.add).then_inc(s_out, 1)
                    E["a"].end()

                steps(dve, dict(p_ln1=p_ln1, p_xa=p_xa, p_shift=p_shift, p_mix=p_mix, p_ruk=p_ruk, p_gate=p_gate,
                                w_bonus=w_bonus, w_step=w_step, w_og=w_og, w_mean=w_mean,
                                w_scale=w_scale, w_gate=w_gate, w_out=w_out, w_ln2=w_ln2, w_xc=w_xc, w_fv=w_fv,
                                a_score=a_score, a_rinv=a_rinv, a_norm=a_norm, a_out=a_out, a_ln=a_ln), begin)


def program(nc, a):
    ctx = ExitStack()
    with ctx:
        def sb(name, shape, dt=F32):
            return ctx.enter_context(nc.sbuf_tensor(name, shape, dt))

        def sem(name):
            return ctx.enter_context(nc.semaphore(name))

        PS = [ctx.enter_context(nc.psum_tensor(f"bank{k}", [P, 512], F32)) for k in range(8)]

        cols = sb("cols", [P, NCOLS])
        rows = sb("rows", [P, len(ROWS) - ROWS1, D])
        ident = sb("ident", [P, P])
        hsum = sb("hsum", [P, HC])
        halfs = sb("halfs", [P, H2])
        at, col = 0, {}
        for name, n in COLS:
            col[name] = (at, n)
            at += n

        def C(name, k=0, parts=P):
            return cols[0:parts, col[name][0] + k:col[name][0] + k + 1]

        def CS(name):
            return cols[:, col[name][0]:col[name][0] + col[name][1]]

        def R(name):
            k = ROWS.index(name)
            return rows[:, k, :] if k < len(ROWS) - ROWS1 else rows1[:, k - len(ROWS) + ROWS1, :]


        s_const = sem("const_loaded")
        s_ident = sem("ident_made")
        s_bn = sem("bn_scale_ready")
        l0_out = nc.dram_tensor("l0_out", (B, P, D), F32, kind="Internal").ap()
        l1_out = nc.dram_tensor("l1_out", (B, P, D), F32, kind="Internal").ap()
        bn_scale = sb("bn_scale", [P, 1])
        bn_shift = sb("bn_shift", [P, 1])

        w1_scope = ctx.enter_context(ExitStack())

        def sb1(name, shape, dt=F32):
            return w1_scope.enter_context(nc.sbuf_tensor(name, shape, dt))

        rows1 = sb1("rows1", [P, ROWS1, D])
        q_w = sb1("q_w", [P, NC, D])
        k_w = sb1("k_w", [P, NC, D])
        v_w = sb1("v_w", [P, NC, D])
        out_w = sb1("out_w", [P, NC, D])
        mlp_w1 = sb1("mlp_w1", [P, NC, NF * P])
        mlp_w2 = sb1("mlp_w2", [P, NF, D])
        s_w1 = sem("layer1_weights_loaded")

        layer0(nc, a, PS, sem, C, cols, rows, rows1, ident, hsum, halfs, s_const, s_ident, bn_scale, bn_shift,
               l0_out, (q_w, k_w, v_w, out_w, mlp_w1, mlp_w2), s_w1)
        layer1(nc, a, PS, sem, C, R, CS, ident, halfs, bn_scale, bn_shift, l0_out, l1_out,
               (q_w, k_w, v_w, out_w, mlp_w1, mlp_w2))
        w1_scope.close()
        layers23(nc, a, PS, sem, C, R, CS, ident, hsum, halfs, l1_out)


def _layout(v):
    import numpy as np

    f = {k: np.asarray(x) for k, x in v.items()}

    def chunks(w):
        w = np.asarray(w)
        return np.ascontiguousarray(w.reshape(w.shape[0] // P, P, w.shape[1]).transpose(1, 0, 2))

    def col(x):
        x = np.asarray(x).reshape(-1)
        if x.size < P:
            x = np.pad(x, (0, P - x.size))
        return x.reshape(-1, P).T

    l0, l1, l2, l3 = (lambda n: f["L0_xattn_" + n]), (lambda n: f["L1_xattn_" + n]), \
        (lambda n: f["L2_xattn_" + n]), (lambda n: f["L3_xattn_" + n])
    byq = np.arange(H3 * D3).reshape(KV3, G3, D3).transpose(1, 0, 2).reshape(-1)

    def padded(w, rows):
        return np.pad(w, ((0, rows - w.shape[0]), (0, 0)))

    o = {}
    o["x"] = f["x"]
    o["ctx"] = f["ctx_2048"]
    o["ctxT"] = np.ascontiguousarray(f["ctx_2048"].reshape(B, P, NC, P).transpose(0, 3, 2, 1))
    state = f["ctx_2048"]
    o["state"] = state[:, 2:2 + D2].reshape(B, NC, P, D2).transpose(0, 2, 1, 3)
    o["row0"] = state[:, 0].reshape(B, NC, P).transpose(0, 2, 1)
    o["row1"] = state[:, 1].reshape(B, NC, P).transpose(0, 2, 1)
    o["mask1"] = f["mask_BxS2_ik0"]
    o["mask3"] = f["mask_Bx1xSxS2_ff0"].reshape(B, P, P)
    o["w0"] = np.stack([l0("Wtheta").T, l0("Wphi").T, l0("Wg").T], axis=1)
    o["wz"] = l0("Wz").T
    o["q_w"] = chunks(l1("q_w"))
    o["k_w"] = chunks(l1("kv_w")[:, 0::2])
    o["v_w"] = chunks(l1("kv_w")[:, 1::2])
    o["out_w"] = chunks(l1("out_w"))
    o["mlp_w1"] = chunks(l1("mlp_w1"))
    o["mlp_w2"] = chunks(l1("mlp_w2"))
    o["maa_w1"] = chunks(l2("maa_w1"))
    o["maa_w2"] = padded(l2("maa_w2").reshape(NM * DM, D), 2 * P)
    o["td_w1"] = chunks(l2("td_w1"))
    o["td_w2"] = padded(l2("td_w2"), P)
    for n in ("Wr", "Wk", "Wv", "Wg", "Wo", "Wfk", "Wfr", "Wfv"):
        o[n] = chunks(l2(n).T)
    o["Wq3"] = chunks(l3("Wq")[:, byq])
    o["Wk3"] = chunks(l3("Wk"))
    o["Wv3"] = chunks(l3("Wv"))
    o["Wo3"] = chunks(l3("Wo")[byq])
    vec = dict(btheta=l0("btheta"), bphi=l0("bphi"), bg=l0("bg"), bz=l0("bz"), bn_gamma=l0("gamma"),
               bn_beta=l0("beta"), q_b=l1("q_b"), k_b=l1("kv_b")[0::2], v_b=l1("kv_b")[1::2],
               post_w=l1("postnorm_w"), b1=l1("mlp_b1"), ln1_w=l2("ln1_w"), ln1_b=l2("ln1_b"),
               ln2_w=l2("ln2_w"), ln2_b=l2("ln2_b"), maa_x=l2("maa_x"), maa_stack=l2("maa_stack"),
               decay=l2("time_decay"), u=l2("u"), ffn_k=l2("ffn_maa_k"), ffn_r=l2("ffn_maa_r"),
               gn_w=l2("gn_w"), gn_b=l2("gn_b"),
               bq3=l3("bq")[byq], bk3=l3("bk"), bv3=l3("bv"))
    o["cols"] = np.concatenate([col(vec[n]) for n, _ in COLS], axis=1)
    row = dict(out_b=l1("out_b"), b2=l1("mlp_b2"), bo3=l3("bo"),
               gamma3=l3("gamma"), beta3=l3("beta"))
    o["rows"] = np.stack([row[n] for n in ROWS[:-ROWS1]])
    o["rows1"] = np.stack([row[n] for n in ROWS[-ROWS1:]])
    o["hsum"] = (np.arange(P)[:, None] // D2 == np.arange(HC)[None, :]).astype(np.float32)
    head, place = np.arange(P) // D2, np.arange(P) % D2
    same = head[:, None] == head[None, :]
    o["spread"] = (same[:, None, :] & (place[:, None, None] == np.arange(D2)[None, :, None])).astype(np.float32)
    o["gather"] = (same[:, None, :] & (place[None, None, :] == np.arange(D2)[None, :, None])).astype(np.float32)
    o["blocks"] = np.stack([same, same / np.float32(D2)], axis=1).astype(np.float32)
    return {k: np.ascontiguousarray(x) for k, x in o.items()}


def kernel(**inputs):
    from concourse import bacc
    from concourse.bass_utils import run_bass_kernel_spmd

    nc = bacc.Bacc("TRN2", target_bir_lowering=False, num_devices=1)
    arrays, args = {}, {}
    for name, x in _layout(inputs).items():
        arrays[f"in_{name}"] = x
        args[name] = nc.dram_tensor(f"in_{name}", x.shape, mybir.dt.from_np(x.dtype), kind="ExternalInput").ap()
    args["out"] = nc.dram_tensor("out", (B, P, D), F32, kind="ExternalOutput").ap()
    program(nc, args)
    r = run_bass_kernel_spmd(nc, [arrays], core_ids=[0])
    return r.results[0]["out"]
```

```python
from contextlib import ExitStack

import concourse.bass as bass
from concourse import mybir

F32 = mybir.dt.float32
I32 = mybir.dt.int32
ALU = mybir.AluOpType
ACT = mybir.ActivationFunctionType
AX = mybir.AxisListType

B = 16
P = 128
D = 512
NC = D // P
CI = 64
H1, D1 = 16, 32
NF = 2048 // P
H2, D2 = 32, 16
NM, DM, DD = 5, 32, 64
H3, D3, KV3 = 32, 16, 8
G3 = H3 // KV3
HC = P // D3
NEG = 1.0e30

COLS = [("btheta", 1), ("bphi", 1), ("bg", 1), ("bz", 1), ("bn_gamma", 1), ("bn_beta", 1),
        ("q_b", NC), ("k_b", NC), ("v_b", NC), ("post_w", NC), ("b1", NF),
        ("ln1_w", NC), ("ln1_b", NC), ("ln2_w", NC), ("ln2_b", NC), ("maa_x", NC),
        ("maa_stack", NM * NC), ("decay", NC), ("u", NC), ("ffn_k", NC), ("ffn_r", NC),
        ("gn_w", NC), ("gn_b", NC), ("bq3", NC), ("bk3", 1), ("bv3", 1)]
ROWS = ["bo3", "gamma3", "beta3", "out_b", "b2"]
ROWS1 = 2
NCOLS = sum(n for _, n in COLS)


class Ring:

    def __init__(self, ready, free, banks, per_batch):
        self.ready, self.free, self.banks, self.per_batch = ready, free, banks, per_batch
        assert per_batch % len(banks) == 0
        self.n = 0
        self.base = 0

    def begin(self, i):
        self.base, self.n = i * self.per_batch, 0

    def read(self, i, k):
        return i * self.per_batch + k + len(self.banks)

    def written(self, i, k):
        return i * self.per_batch + k

    def next(self):
        self.bank = self.banks[self.n % len(self.banks)]
        self.n += 1
        self.count = self.base + self.n
        assert self.n <= self.per_batch
        return self.bank


class Steps:

    def __init__(self, per_batch):
        self.per_batch, self.n, self.base = per_batch, 0, 0

    def begin(self, i):
        self.base, self.n = i * self.per_batch, 0

    def tick(self):
        self.n += 1
        assert self.n <= self.per_batch, "more steps than per_batch"
        return 1

    @property
    def now(self):
        return self.base + self.n

    def end(self):
        assert self.n == self.per_batch, f"per_batch should be {self.n}"


def layer0(nc, a, PS, sem, C, cols, rows, rows1, ident, hsum, hsum4, halfs, s_const, s_ident, bn_scale, bn_shift, l0_out,
           weights1, s_w1):
    with ExitStack() as ctx:
        def sb(name, shape, dt=F32):
            return ctx.enter_context(nc.sbuf_tensor(name, shape, dt))

        w0 = sb("w0", [P, 3, CI])
        wz = sb("wz", [CI, P])
        xin = sb("x_in", [P, D])
        cin = sb("ctx_in", [P, D])
        theta = sb("theta", [CI, D])
        phi = sb("phi", [CI, D])
        g = sb("g", [P, NC, CI])
        probs = sb("probs", [P, NC, D])
        probsT = sb("probsT", [P, NC, D])
        nmax = sb("nmax", [P, NC])
        rsum = sb("rsum", [P, NC])
        rinv = sb("rinv", [P, NC])
        y = sb("y", [CI, D])
        wy = sb("wy", [P, D])
        stats = sb("stats", [P, B, 6])
        mv = sb("mv", [P, 2])
        bnt = sb("bnt", [P, 2])

        s_w0 = sem("l0_weights_loaded")
        s_in = sem("l0_inputs_loaded")
        s_in_used = sem("l0_inputs_used")
        s_nmax = sem("l0_max_ready")
        s_rinv = sem("l0_rinv_ready")
        s_norm = sem("l0_probs_ready")
        s_stat = sem("l0_stats_done")
        s_store = sem("l0_wy_stored")
        s_bnv = sem("l0_bn_step")
        rings = dict(tp=([4, 5], 2), g=([6], 1), f=([0, 1], 4), t=([2, 3], 4), o=([7], 2))
        S = {k: (sem(f"l0_{k}_psum_ready"), sem(f"l0_{k}_psum_free")) for k in rings}

        def ring(k):
            return Ring(*S[k], *rings[k])

        with nc.Block() as block:
            @block.sync
            def _(sp):
                sp.dma_start(w0[:, :, :], a["w0"]).then_inc(s_w0, 16)
                sp.dma_start(wz[:, :], a["wz"]).then_inc(s_w0, 16)
                sp.dma_start(cols[:, :], a["cols"]).then_inc(s_const, 16)
                sp.dma_start(hsum[:, :], a["hsum"]).then_inc(s_const, 16)
                sp.dma_start(hsum4[:, :], a["hsum4"]).then_inc(s_const, 16)
                sp.dma_start(rows[:, :, :], a["rows"].unsqueeze(0).to_broadcast([P, len(ROWS) - ROWS1, D])).then_inc(s_const, 16)
                sp.dma_start(rows1[:, :, :], a["rows1"].unsqueeze(0).to_broadcast([P, ROWS1, D])).then_inc(s_const, 16)
                with sp.Fori(0, B) as i:
                    sp.wait_ge(s_in_used, i + 1)
                    sp.dma_start(xin[:, :], a["x"][i]).then_inc(s_in, 16)
                    sp.dma_start(cin[:, :], a["ctx"][i]).then_inc(s_in, 16)

            @block.gpsimd
            def _(pool):
                nc.gpsimd.memset(ident[:, :], 0.0).then_inc(s_ident, 1)
                nc.gpsimd.memset(halfs[:, :], -0.5).then_inc(s_ident, 1)
                pool.wait_ge(s_ident, 2)
                nc.gpsimd.affine_select(out=ident[:, :], in_=ident[:, :], compare_op=ALU.not_equal, fill=1.0,
                                        base=0, pattern=[[-1, P]], channel_multiplier=1).then_inc(s_ident, 1)
                for w, name in zip(weights1, ("q_w", "k_w", "v_w", "out_w", "mlp_w1", "mlp_w2")):
                    pool.dma_start(w[:, :, :], a[name]).then_inc(s_w1, 16)
                pool.wait_ge(s_bnv, 2)
                nc.gpsimd.tensor_tensor(bnt[:, 1:2], bnt[:, 0:1], halfs[:, 0:1], ALU.pow).then_inc(s_bnv, 1)
                pool.wait_ge(s_const, 80)
                pool.wait_ge(s_w1, 16 * 6)

            @block.tensor
            def _(pe):
                for k in rings:
                    pe.sem_inc(S[k][1], len(rings[k][0]))
                pe.sem_inc(s_in_used, 1)
                pe.sem_inc(s_store, 16)
                TP, G, F, T, O = (ring(k) for k in ("tp", "g", "f", "t", "o"))
                pe.wait_ge(s_w0, 32)
                pe.wait_ge(s_ident, 3)

                def theta_phi(i):
                    TP.begin(i)
                    pe.wait_ge(s_in, 32 * i + 32)
                    for n, x in ((0, xin), (1, cin)):
                        b = TP.next()
                        pe.wait_ge(TP.free, TP.count)
                        nc.tensor.matmul(PS[b][0:CI, :], w0[:, n, :], x[:, :], start=True, stop=True)\
                            .then_inc(TP.ready, 1)

                def g_proj(i):
                    G.begin(i)
                    b = G.next()
                    pe.wait_ge(G.free, G.count)
                    for j in range(NC):
                        mm = nc.tensor.matmul(PS[b][:, j * CI:(j + 1) * CI], xin[:, j * P:(j + 1) * P], w0[:, 2, :],
                                              start=True, stop=True)
                    mm.then_inc(G.ready, 1)
                    pe.wait_ge(G.ready, G.count)
                    pe.sem_inc(s_in_used, 1)

                def scores(i):
                    F.begin(i)
                    pe.wait_ge(TP.free, TP.read(i, 2))
                    for c in range(NC):
                        b = F.next()
                        pe.wait_ge(F.free, F.count)
                        nc.tensor.matmul(PS[b][:, :], phi[:, c * P:(c + 1) * P], theta[:, :], start=True, stop=True)\
                            .then_inc(F.ready, 1)

                def turn_probs(i):
                    T.begin(i)
                    for c in range(NC):
                        b = T.next()
                        pe.wait_ge(T.free, T.count)
                        pe.wait_ge(s_norm, NC * i + c + 1)
                        for j in range(NC):
                            mm = nc.tensor.transpose(PS[b][:, j * P:(j + 1) * P], probs[:, c, j * P:(j + 1) * P], ident[:, :])
                        mm.then_inc(T.ready, 1)

                def out_y(i):
                    O.begin(i)
                    b = O.next()
                    pe.wait_ge(O.free, O.count)
                    pe.wait_ge(G.free, G.read(i, 1))
                    pe.wait_ge(T.free, T.read(i, NC))
                    for j in range(NC):
                        mm = nc.tensor.matmul(PS[b][0:CI, :], g[:, j, :], probsT[:, j, :], start=(j == 0), stop=(j == NC - 1))
                    mm.then_inc(O.ready, 1)

                def out_z(i):
                    b = O.next()
                    pe.wait_ge(O.free, O.count)
                    pe.wait_ge(O.free, O.read(i, 1))
                    nc.tensor.matmul(PS[b][:, :], wz[:, :], y[:, :], start=True, stop=True).then_inc(O.ready, 1)

                theta_phi(0)
                g_proj(0)
                scores(0)
                with pe.Fori(1, B) as i:
                    theta_phi(i)
                    turn_probs(i - 1)
                    out_y(i - 1)
                    g_proj(i)
                    scores(i)
                    out_z(i - 1)
                turn_probs(B - 1)
                out_y(B - 1)
                out_z(B - 1)

            @block.scalar
            def _(act):
                TP, G, F, O = (ring(k) for k in ("tp", "g", "f", "o"))
                act.wait_ge(s_const, 80)

                def theta_phi(i):
                    TP.begin(i)
                    for dst, bias in ((theta, "btheta"), (phi, "bphi")):
                        b = TP.next()
                        act.wait_ge(TP.ready, TP.count)
                        nc.scalar.activation(dst[:, :], PS[b][0:CI, :], ACT.Identity, bias=C(bias, 0, CI))\
                            .then_inc(TP.free, 1)

                def copy_g(i):
                    G.begin(i)
                    b = G.next()
                    act.wait_ge(G.ready, G.count)
                    nc.scalar.activation(g[:, :, :], PS[b][:, 0:NC * CI].rearrange("p (j o) -> p j o", j=NC), ACT.Copy)\
                        .then_inc(G.free, 1)

                def exps(i):
                    F.begin(i)
                    for c in range(NC):
                        b = F.next()
                        act.wait_ge(s_nmax, NC * i + c + 1)
                        nc.scalar.activation(probs[:, c, :], PS[b][:, :], ACT.Exp, bias=nmax[:, c:c + 1],
                                             accum_out=rsum[:, c:c + 1]).then_inc(F.free, 1)

                def copy_y(i):
                    O.begin(i)
                    b = O.next()
                    act.wait_ge(O.ready, O.count)
                    nc.scalar.activation(y[:, :], PS[b][0:CI, :], ACT.Identity, bias=C("bg", 0, CI)).then_inc(O.free, 1)

                def copy_z(i):
                    b = O.next()
                    act.wait_ge(O.ready, O.count)
                    act.wait_ge(s_store, 16 * i + 16)
                    if not isinstance(i, int) or i > 0:
                        act.wait_ge(s_stat, i)
                    nc.scalar.activation(wy[:, :], PS[b][:, :], ACT.Identity, bias=C("bz")).then_inc(O.free, 1)
                    act.wait_ge(O.free, O.read(i, 2))
                    act.dma_start(l0_out[i], wy[:, :]).then_inc(s_store, 16)

                theta_phi(0)
                copy_g(0)
                exps(0)
                theta_phi(1)
                copy_y(0)
                copy_g(1)
                exps(1)
                copy_z(0)
                with act.Fori(2, B) as i:
                    theta_phi(i)
                    copy_y(i - 1)
                    copy_g(i)
                    exps(i)
                    copy_z(i - 1)
                copy_y(B - 1)
                copy_z(B - 1)
                act.wait_ge(s_store, 16 * (B + 1))

            @block.vector
            def _(dve):
                F, T, O = ring("f"), ring("t"), ring("o")

                def maxima(i):
                    F.begin(i)
                    for c in range(NC):
                        b = F.next()
                        dve.wait_ge(F.ready, F.count)
                        nc.vector.tensor_reduce(nmax[:, c:c + 1], PS[b][:, :], AX.X, ALU.max, negate=True)\
                            .then_inc(s_nmax, 1)

                def normalise(i):
                    for c in range(NC):
                        dve.wait_ge(F.free, F.read(i, c + 1))
                        nc.vector.reciprocal(rinv[:, c:c + 1], rsum[:, c:c + 1]).then_inc(s_rinv, 1)
                        dve.wait_ge(s_rinv, NC * i + c + 1)
                        nc.vector.tensor_scalar(probs[:, c, :], probs[:, c, :], rinv[:, c:c + 1], None, ALU.mult)\
                            .then_inc(s_norm, 1)

                def copy_probsT(i):
                    T.begin(i)
                    for c in range(NC):
                        b = T.next()
                        dve.wait_ge(T.ready, T.count)
                        nc.vector.tensor_copy(probsT[:, :, c * P:(c + 1) * P],
                                              PS[b][:, :].rearrange("p (j i) -> p j i", j=NC)).then_inc(T.free, 1)

                def statistics(i):
                    dve.wait_ge(O.free, O.read(i, 2))
                    nc.vector.bn_stats(stats[:, i, :], wy[:, :]).then_inc(s_stat, 1)

                maxima(0)
                normalise(0)
                with dve.Fori(1, B) as i:
                    copy_probsT(i - 1)
                    maxima(i)
                    normalise(i)
                    statistics(i - 1)
                copy_probsT(B - 1)
                statistics(B - 1)
                dve.wait_ge(s_stat, B)
                nc.vector.bn_aggr(mv[:, :], stats[:, :, :].rearrange("p b s -> p (b s)")).then_inc(s_bnv, 1)
                dve.wait_ge(s_bnv, 1)
                nc.vector.tensor_scalar(bnt[:, 0:1], mv[:, 1:2], 1e-5, None, ALU.add).then_inc(s_bnv, 1)
                dve.wait_ge(s_bnv, 3)
                nc.vector.tensor_scalar(bn_scale[:, :], bnt[:, 1:2], C("bn_gamma"), None, ALU.mult).then_inc(s_bnv, 1)
                dve.wait_ge(s_bnv, 4)
                nc.vector.tensor_scalar(bn_shift[:, :], mv[:, 0:1], bn_scale[:, :], -1.0, ALU.mult, ALU.mult)\
                    .then_inc(s_bnv, 1)
                dve.wait_ge(s_bnv, 5)
                nc.vector.tensor_scalar(bn_shift[:, :], bn_shift[:, :], C("bn_beta"), None, ALU.add).then_inc(s_bnv, 1)
                dve.wait_ge(s_bnv, 6)


def layer1(nc, a, PS, sem, C, R, cols_of, ident, hsum4, halfs, bn_scale, bn_shift, l0_out, l1_out, weights):
    q_w, k_w, v_w, out_w, mlp_w1, mlp_w2 = weights
    NK = 2
    NG = H1 // 2
    HQ = P // D1
    J_SCORE, J_TURN, J_RINV = list(range(1, 9)), [9, 10, 11, 12, 13, 15, 16, 17], [14, 18]

    def pair(g):
        return [2 * g, 2 * g + 1]

    with ExitStack() as ctx:
        def sb(name, shape, dt=F32):
            return ctx.enter_context(nc.sbuf_tensor(name, shape, dt))

        wyin = sb("wy_in", [P, D])
        xin = sb("x_in1", [P, D])
        maski = sb("mask_in", [P, P], I32)
        negm = sb("neg_mask", [P, NK * P])
        lat = sb("latents", [P, D])
        latb = sb("latents_out_b", [P, D])
        latb2n = sb("latents_b2_next", [P, D])
        latb2 = sb("latents_b2", [P, D])
        hT = sb("hT", [P, NC, NK * P])
        qT = sb("qT", [P, NC, P])
        kT = sb("kT", [P, NC, NK * P])
        kbd = [sb(f"k_blocks1_{q}", [P, HQ, NK * P]) for q in range(2)]
        v = sb("v", [P, NK, H1, D1])
        probs = sb("probs1", [P, H1, NK * P])
        probsT = sb("probsT1", [P, NG, 2 * NK, P])
        nmax = sb("nmax1", [P, H1])
        rinv = sb("rinv1", [P, H1])
        rsum = sb("rsum1", [P, H1])
        rrep = sb("rinv1_repeated", [P, H1, D1])
        rT = sb("rinv1_T", [P, NC, P])
        attn = sb("attn", [P, NC, P])
        attnT = sb("attnT", [P, NC, P])
        ao = sb("attn_out", [P, D])
        sq = sb("squares", [P, D])
        ss = sb("sumsq", [P, 1])
        ms = sb("mean_square", [P, 1])
        rstd = sb("rstd1", [P, 1])
        an = sb("normed", [P, D])
        nT = sb("normedT", [P, NC, P])
        gT = sb("geluT", [P, NF, P])
        xo = sb("l1_x", [P, D])

        s_in = sem("l1_inputs_loaded")
        s_ctx = sem("l1_context_loaded")
        s_mask = sem("l1_mask_loaded")
        s_bn = sem("l1_bn_applied")
        s_lat = sem("l1_latents_ready")
        s_latb = sem("l1_latents_out_b_ready")
        s_latb2n = sem("l1_latents_b2_made")
        s_latb2 = sem("l1_latents_b2_ready")
        s_negm = sem("l1_neg_mask_ready")
        s_exp = sem("l1_exp_ready")
        s_kbd = sem("l1_k_blocks_ready")
        s_rinv = sem("l1_rinv_ready")
        s_rrep = sem("l1_rinv_repeated")
        s_attnT = sem("l1_attention_ready")
        s_ss = sem("l1_sumsq_ready")
        s_ms = sem("l1_mean_square_ready")
        s_rstd = sem("l1_rstd_ready")
        s_an = sem("l1_normed_ready")
        s_ones = sem("l1_ones_made")
        s_store = sem("l1_x_stored")
        s_hold = sem("l1_wait_held")
        rings = dict(d=([0, 1], 2 * NG + 2), a=([2, 3], 6), o=([4], 2), h=([5, 6], NF // 4), m=([7], 2))
        S = {k: (sem(f"l1_{k}_psum_ready"), sem(f"l1_{k}_psum_free")) for k in rings}

        def ring(k):
            return Ring(*S[k], *rings[k])

        with nc.Block() as block:
            @block.sync
            def _(sp):
                A, DR = ring("a"), ring("d")

                def load_x(i):
                    sp.dma_start(wyin[:, :], l0_out[i]).then_inc(s_in, 16)
                    sp.dma_start(xin[:, :], a["x"][i]).then_inc(s_in, 16)

                def load_ctx(i):
                    sp.dma_start(maski[:, :], a["mask1"][i].unsqueeze(0).to_broadcast([P, P])).then_inc(s_mask, 16)
                    sp.dma_start(hT[:, :, 0:P], a["ctxT"][i]).then_inc(s_ctx, 16)

                load_x(0)
                load_ctx(0)
                with sp.Fori(1, B) as i:
                    sp.wait_ge(s_lat, i)
                    load_x(i)
                    sp.wait_ge(s_negm, i)
                    sp.wait_ge(A.free, A.read(i - 1, 6))
                    load_ctx(i)

            @block.gpsimd
            def _(pool):
                M, O, A, DR = (ring(k) for k in "moad")
                nc.gpsimd.memset(negm[:, P:NK * P], 0.0).then_inc(s_ones, 1)

                def latents(i):
                    pool.wait_ge(s_bn, i + 1)
                    nc.gpsimd.tensor_tensor(lat[:, :], lat[:, :], xin[:, :], ALU.add).then_inc(s_lat, 1)

                def latents_b2(i):
                    pool.wait_ge(s_lat, i + 1)
                    if not isinstance(i, int) or i > 0:
                        pool.wait_ge(s_latb2, i)
                    nc.gpsimd.tensor_tensor(latb2n[:, :], lat[:, :], R("b2"), ALU.add).then_inc(s_latb2n, 1)

                def latents_out_b(i):
                    if not isinstance(i, int) or i > 0:
                        pool.wait_ge(O.free, O.read(i - 1, 2))
                    nc.gpsimd.tensor_tensor(latb[:, :], lat[:, :], R("out_b"), ALU.add).then_inc(s_latb, 1)

                def blocks(i, c):
                    if c == 0:
                        pool.wait_ge(A.free, A.read(i, 4))
                    if c >= 2:
                        pool.wait_ge(DR.ready, DR.written(i, J_SCORE[2 * (c - 2) + 1]))
                    nc.gpsimd.tensor_tensor(kbd[c % 2][:, :, :], kT[:, c, :].unsqueeze(1).to_broadcast([P, HQ, NK * P]),
                                            hsum4[:, :].unsqueeze(2).to_broadcast([P, HQ, NK * P]), ALU.mult)\
                        .then_inc(s_kbd, 1)

                def repeat_rinv(i, half):
                    pool.wait_ge(s_rinv, 2 * i + half + 1)
                    pool.sem_inc(s_hold, 1)
                    nc.gpsimd.tensor_copy(rrep[:, 8 * half:8 * half + 8, :],
                                          rinv[:, 8 * half:8 * half + 8].unsqueeze(2).to_broadcast([P, 8, D1]))\
                        .then_inc(s_rrep, 1)

                def batch(i, first=False, last=False):
                    for c in range(NC):
                        blocks(i, c)
                    if not last:
                        latents(i + 1)
                    repeat_rinv(i, 0)
                    repeat_rinv(i, 1)
                    if not first:
                        pool.wait_ge(M.free, M.read(i - 1, 2))
                    pool.wait_ge(s_latb2n, i + 1)
                    pool.sem_inc(s_hold, 1)
                    nc.gpsimd.tensor_copy(latb2[:, :], latb2n[:, :]).then_inc(s_latb2, 1)
                    if not last:
                        latents_b2(i + 1)
                    pool.wait_ge(s_ms, i + 1)
                    nc.gpsimd.tensor_tensor(rstd[:, :], ms[:, :], halfs[:, 0:1], ALU.pow).then_inc(s_rstd, 1)
                    if not last:
                        latents_out_b(i + 1)

                latents(0)
                latents_b2(0)
                latents_out_b(0)
                batch(0, first=True)
                with pool.Fori(1, B - 1) as i:
                    batch(i)
                batch(B - 1, last=True)

            @block.tensor
            def _(pe):
                for k in rings:
                    pe.sem_inc(S[k][1], len(rings[k][0]))
                DR, A, O, H, M = (ring(k) for k in "daohm")
                AL = ring("a")

                def turn_latents(i):
                    AL.begin(i)
                    b = AL.next()
                    pe.wait_ge(AL.free, AL.count)
                    pe.wait_ge(s_lat, i + 1)
                    for c in range(NC):
                        mm = nc.tensor.transpose(PS[b][:, c * P:(c + 1) * P], lat[:, c * P:(c + 1) * P], ident[:, :])
                    mm.then_inc(AL.ready, 1)

                def queries(i):
                    A.begin(i)
                    A.next()
                    b = A.next()
                    pe.wait_ge(A.free, A.count)
                    pe.wait_ge(A.free, A.read(i, 1))
                    for m in range(NC):
                        for c in range(NC):
                            mm = nc.tensor.matmul(PS[b][:, m * P:(m + 1) * P], q_w[:, c, m * P:(m + 1) * P],
                                                  hT[:, c, P:2 * P], start=(c == 0), stop=(c == NC - 1))
                    mm.then_inc(A.ready, 1)

                def keys(i):
                    pe.wait_ge(s_ctx, 16 * i + 16)
                    for half in range(2):
                        b = A.next()
                        pe.wait_ge(A.free, A.count)
                        for e in range(2):
                            m = 2 * half + e
                            for c in range(NC):
                                mm = nc.tensor.matmul(PS[b][:, e * 256:(e + 1) * 256], k_w[:, c, m * P:(m + 1) * P],
                                                      hT[:, c, :], start=(c == 0), stop=(c == NC - 1))
                        mm.then_inc(A.ready, 1)

                def values(i):
                    for n in range(NK):
                        b = A.next()
                        pe.wait_ge(A.free, A.count)
                        for c in range(NC):
                            mm = nc.tensor.matmul(PS[b][:, :], hT[:, c, n * P:(n + 1) * P], v_w[:, c, :],
                                                  start=(c == 0), stop=(c == NC - 1))
                        mm.then_inc(A.ready, 1)

                def scores(i, g):
                    b = DR.next()
                    pe.wait_ge(DR.free, DR.count)
                    c = g // 2
                    pe.wait_ge(s_kbd, NC * i + c + 1)
                    nc.tensor.matmul(PS[b][:, :], qT[:, c, :], kbd[c % 2][:, 2 * (g % 2):2 * (g % 2) + 2, :]
                                     .rearrange("p h k -> p (h k)"), start=True, stop=True).then_inc(DR.ready, 1)

                def turn_probs(i, g):
                    b = DR.next()
                    pe.wait_ge(DR.free, DR.count)
                    pe.wait_ge(s_exp, NG * i + g + 1)
                    for e, h in enumerate(pair(g)):
                        for n in range(NK):
                            o = (e * NK + n) * P
                            mm = nc.tensor.transpose(PS[b][:, o:o + P], probs[:, h, n * P:(n + 1) * P], ident[:, :])
                    mm.then_inc(DR.ready, 1)

                def turn_rinv(i, half):
                    b = DR.next()
                    pe.wait_ge(DR.free, DR.count)
                    pe.wait_ge(s_rrep, 2 * i + half + 1)
                    for c in range(2):
                        mm = nc.tensor.transpose(PS[b][:, c * P:(c + 1) * P],
                                                 rrep[:, 8 * half + 4 * c:8 * half + 4 * c + 4, :].rearrange("p h d -> p (h d)"),
                                                 ident[:, :])
                    mm.then_inc(DR.ready, 1)

                def attend(i, half):
                    if half == 0:
                        O.next()
                        pe.wait_ge(O.free, O.count)
                        pe.wait_ge(A.free, A.read(i, 6))
                    pe.wait_ge(DR.free, DR.read(i, J_TURN[4 * half + 3]))
                    for c in (2 * half, 2 * half + 1):
                        for n in range(NK):
                            for q in range(HQ):
                                h = HQ * c + q
                                mm = nc.tensor.matmul(PS[O.bank][D1 * q:D1 * (q + 1), c * P:(c + 1) * P], v[:, n, h, :],
                                                      probsT[:, h // 2, (h % 2) * NK + n, :],
                                                      start=(n == 0), stop=(n == NK - 1))
                    if half == 1:
                        mm.then_inc(O.ready, 1)

                def project(i):
                    b = O.next()
                    pe.wait_ge(O.free, O.count)
                    pe.wait_ge(s_attnT, i + 1)
                    for c in range(NC):
                        mm = nc.tensor.matmul(PS[b][:, :], attnT[:, c, :], out_w[:, c, :], start=(c == 0), stop=(c == NC - 1))
                    mm.then_inc(O.ready, 1)

                def turn_normed(i):
                    M.begin(i)
                    b = M.next()
                    pe.wait_ge(M.free, M.count)
                    pe.wait_ge(s_an, i + 1)
                    for c in range(NC):
                        mm = nc.tensor.transpose(PS[b][:, c * P:(c + 1) * P], an[:, c * P:(c + 1) * P], ident[:, :])
                    mm.then_inc(M.ready, 1)

                def hidden(i, j):
                    if j == 0:
                        H.begin(i)
                        pe.wait_ge(M.free, M.read(i, 1))
                    b = H.next()
                    pe.wait_ge(H.free, H.count)
                    for f in range(4):
                        m = 4 * j + f
                        for c in range(NC):
                            mm = nc.tensor.matmul(PS[b][:, f * P:(f + 1) * P], mlp_w1[:, c, m * P:(m + 1) * P],
                                                  nT[:, c, :], start=(c == 0), stop=(c == NC - 1))
                    mm.then_inc(H.ready, 1)

                def mlp_out(i, j):
                    if j == 0:
                        b = M.next()
                        pe.wait_ge(M.free, M.count)
                    pe.wait_ge(H.free, H.read(i, j + 1))
                    for f in range(4 * j, 4 * j + 4):
                        mm = nc.tensor.matmul(PS[M.bank][:, :], gT[:, f, :], mlp_w2[:, f, :], start=(f == 0), stop=(f == NF - 1))
                    if j == 3:
                        mm.then_inc(M.ready, 1)

                def batch(i, mlp, last=False):
                    queries(i)
                    keys(i)
                    if mlp:
                        turn_normed(i - 1)
                    values(i)
                    DR.begin(i)
                    O.begin(i)
                    scores(i, 0)
                    scores(i, 1)
                    for j in range(4):
                        if mlp:
                            hidden(i - 1, j)
                        scores(i, 2 + j)
                    if mlp:
                        mlp_out(i - 1, 0)
                    scores(i, 6)
                    scores(i, 7)
                    turn_probs(i, 0)
                    turn_probs(i, 1)
                    if mlp:
                        mlp_out(i - 1, 1)
                    for g in range(2, 6):
                        turn_probs(i, g)
                        if g == 4:
                            turn_rinv(i, 0)
                            attend(i, 0)
                    if mlp:
                        mlp_out(i - 1, 2)
                    turn_probs(i, 6)
                    turn_probs(i, 7)
                    turn_rinv(i, 1)
                    if not last:
                        turn_latents(i + 1)
                    attend(i, 1)
                    if mlp:
                        mlp_out(i - 1, 3)
                    project(i)

                turn_latents(0)
                batch(0, False)
                with pe.Fori(1, B - 1) as i:
                    batch(i, True)
                batch(B - 1, True, last=True)
                turn_normed(B - 1)
                for j in range(4):
                    hidden(B - 1, j)
                for j in range(4):
                    mlp_out(B - 1, j)

            @block.scalar
            def _(act):
                DR, A, O, H, M = (ring(k) for k in "daohm")
                AL = ring("a")
                act.wait_ge(s_ones, 1)

                def batch_norm(i, first=False):
                    act.wait_ge(s_in, 32 * i + 32)
                    if not first:
                        act.wait_ge(s_latb2n, i)
                        act.wait_ge(s_latb, i)
                        act.wait_ge(A.free, A.read(i - 1, 1))
                    nc.scalar.activation(lat[:, :], wyin[:, :], ACT.Identity, bias=bn_shift[:, :], scale=bn_scale[:, :])\
                        .then_inc(s_bn, 1)

                def copy_latents(i):
                    AL.begin(i)
                    b = AL.next()
                    act.wait_ge(AL.ready, AL.count)
                    nc.scalar.activation(hT[:, :, P:2 * P], PS[b][:, :].rearrange("p (c t) -> p c t", c=NC), ACT.Copy)\
                        .then_inc(AL.free, 1)

                def copy_q(i):
                    A.begin(i)
                    A.next()
                    b = A.next()
                    act.wait_ge(A.ready, A.count)
                    for c in range(NC):
                        ac = nc.scalar.activation(qT[:, c, :], PS[b][:, c * P:(c + 1) * P], ACT.Identity, bias=C("q_b", c))
                    ac.then_inc(A.free, 1)

                def copy_k(i):
                    for half in range(2):
                        b = A.next()
                        act.wait_ge(A.ready, A.count)
                        for e in range(2):
                            c = 2 * half + e
                            ac = nc.scalar.activation(kT[:, c, :], PS[b][:, e * 256:(e + 1) * 256], ACT.Identity,
                                                      bias=C("k_b", c))
                        ac.then_inc(A.free, 1)

                def copy_v(i):
                    for n in range(NK):
                        b = A.next()
                        act.wait_ge(A.ready, A.count)
                        nc.scalar.activation(v[:, n, :, :], PS[b][:, :].rearrange("p (h d) -> p h d", h=H1), ACT.Copy)\
                            .then_inc(A.free, 1)

                def gelu(i, j):
                    if j == 0:
                        H.begin(i)
                    b = H.next()
                    act.wait_ge(H.ready, H.count)
                    for f in range(4):
                        ac = nc.scalar.activation(gT[:, 4 * j + f, :], PS[b][:, f * P:(f + 1) * P], ACT.Gelu_apprx_tanh,
                                                  bias=C("b1", 4 * j + f))
                    ac.then_inc(H.free, 1)

                def exps(i, g):
                    act.wait_ge(DR.free, DR.read(i, J_SCORE[g]))
                    for h in pair(g):
                        ac = nc.scalar.activation(probs[:, h, :], probs[:, h, :], ACT.Exp, bias=nmax[:, h:h + 1],
                                                  scale=-1.0, accum_out=rsum[:, h:h + 1])
                    ac.then_inc(s_exp, 1)

                def squares(i):
                    act.wait_ge(O.free, O.read(i, 2))
                    nc.scalar.activation(sq[:, :], ao[:, :], ACT.Square, accum_out=ss[:, :]).then_inc(s_ss, 1)

                def store(i):
                    act.wait_ge(M.free, M.read(i, 2))
                    act.dma_start(l1_out[i], xo[:, :]).then_inc(s_store, 16)

                def batch(i, mlp, last=False):
                    copy_q(i)
                    copy_k(i)
                    copy_v(i)
                    if not last:
                        batch_norm(i + 1)
                    if mlp:
                        for j in range(4):
                            gelu(i - 1, j)
                    for g in range(NG):
                        exps(i, g)
                    if not last:
                        copy_latents(i + 1)
                    squares(i)
                    if mlp:
                        store(i - 1)

                batch_norm(0, True)
                copy_latents(0)
                batch(0, False)
                with act.Fori(1, B - 1) as i:
                    batch(i, True)
                batch(B - 1, True, last=True)
                for j in range(4):
                    gelu(B - 1, j)
                store(B - 1)
                act.wait_ge(s_store, 16 * (B + 1))

            @block.vector
            def _(dve):
                DR, O, M = (ring(k) for k in "dom")
                dve.wait_ge(s_ones, 1)

                def mask(i):
                    dve.wait_ge(s_mask, 16 * i + 16)
                    nc.vector.tensor_scalar(negm[:, 0:P], maski[:, :], 0.0, -NEG, ALU.is_equal, ALU.mult)\
                        .then_inc(s_negm, 1)
                    dve.wait_ge(s_negm, i + 1)

                def maxima(i, g):
                    b = DR.next()
                    dve.wait_ge(DR.ready, DR.count)
                    dve.sem_inc(s_hold, 1)
                    for e, h in enumerate(pair(g)):
                        mx = nc.vector.tensor_tensor_reduce(probs[:, h, :], PS[b][:, e * 256:(e + 1) * 256], negm[:, :],
                                                            -1.0 / D1, 3.0e38, ALU.add, ALU.min, nmax[:, h:h + 1])
                    mx.then_inc(DR.free, 1)

                def copy_probsT(i, g):
                    b = DR.next()
                    dve.wait_ge(DR.ready, DR.count)
                    nc.vector.tensor_copy(probsT[:, g, :, :], PS[b][:, :].rearrange("p (n q) -> p n q", q=P))\
                        .then_inc(DR.free, 1)

                def reciprocals(i, half):
                    dve.wait_ge(s_exp, NG * i + 4 * half + 4)
                    r = slice(8 * half, 8 * half + 8)
                    nc.vector.reciprocal(rinv[:, r], rsum[:, r]).then_inc(s_rinv, 1)

                def copy_rinvT(i, half):
                    b = DR.next()
                    dve.wait_ge(DR.ready, DR.count)
                    nc.vector.tensor_copy(rT[:, 2 * half:2 * half + 2, :],
                                          PS[b][:, 0:2 * P].rearrange("p (c t) -> p c t", c=2)).then_inc(DR.free, 1)

                def normalise(i):
                    b = O.next()
                    dve.wait_ge(O.ready, O.count)
                    dve.wait_ge(DR.free, DR.read(i, J_RINV[1]))
                    nc.vector.tensor_tensor(attn[:, :, :], PS[b][:, :].rearrange("p (c t) -> p c t", c=NC), rT[:, :, :],
                                            ALU.mult).then_inc(O.free, 1)
                    dve.wait_ge(O.free, O.read(i, 1))
                    nc.vector.tensor_tensor(attnT[:, :, :], attn[:, :, :],
                                            cols_of("v_b").unsqueeze(2).to_broadcast([P, NC, P]), ALU.add)\
                        .then_inc(s_attnT, 1)

                def residual(i):
                    b = O.next()
                    dve.wait_ge(O.ready, O.count)
                    dve.wait_ge(s_latb, i + 1)
                    nc.vector.tensor_tensor(ao[:, :], PS[b][:, :], latb[:, :], ALU.add).then_inc(O.free, 1)

                def rms_norm(i):
                    dve.wait_ge(s_ss, i + 1)
                    nc.vector.tensor_scalar(ms[:, :], ss[:, :], 1.0 / D, 1e-6, ALU.mult, ALU.add).then_inc(s_ms, 1)
                    dve.wait_ge(s_rstd, i + 1)
                    nc.vector.tensor_scalar(an[:, :], ao[:, :], rstd[:, :], None, ALU.mult).then_inc(s_an, 1)

                def copy_normed(i):
                    M.begin(i)
                    b = M.next()
                    dve.wait_ge(M.ready, M.count)
                    nc.vector.tensor_tensor(nT[:, :, :], PS[b][:, :].rearrange("p (c t) -> p c t", c=NC),
                                            cols_of("post_w").unsqueeze(2).to_broadcast([P, NC, P]), ALU.mult)\
                        .then_inc(M.free, 1)

                def output(i):
                    b = M.next()
                    dve.wait_ge(M.ready, M.count)
                    dve.wait_ge(s_latb2, i + 1)
                    dve.wait_ge(s_store, 16 * i + 16)
                    nc.vector.tensor_tensor(xo[:, :], PS[b][:, :], latb2[:, :], ALU.add).then_inc(M.free, 1)

                def batch(i, mlp):
                    mask(i)
                    if mlp:
                        copy_normed(i - 1)
                    DR.begin(i)
                    O.begin(i)
                    for g in range(NG):
                        maxima(i, g)
                    for g in range(NG):
                        if g in (3, 6):
                            reciprocals(i, g // 6)
                        copy_probsT(i, g)
                        if g in (4, 7):
                            copy_rinvT(i, g // 7)
                    normalise(i)
                    if mlp:
                        output(i - 1)
                    residual(i)
                    rms_norm(i)

                dve.sem_inc(s_store, 16)
                batch(0, False)
                with dve.Fori(1, B) as i:
                    batch(i, True)
                copy_normed(B - 1)
                output(B - 1)


def layers23(nc, a, PS, sem, C, R, CS, ident, hsum, halfs, l1_out):
    JS = D2
    LAG = 3
    V2 = 2 * D3

    with ExitStack() as ctx:
        def sb(name, shape, dt=F32):
            return ctx.enter_context(nc.sbuf_tensor(name, shape, dt))

        def flat(t):
            return t[:, :, :].rearrange("p c t -> p (c t)")

        maa_w1 = sb("maa_w1", [P, NC, NM * DM])
        maa_w2 = sb("maa_w2", [P, D])
        maa_w2b = sb("maa_w2b", [P, D])
        td_w1 = sb("td_w1", [P, NC, DD])
        td_w2 = sb("td_w2", [P, D])
        W = {n: sb(n, [P, NC, D]) for n in ("Wk", "Wv", "Wr", "Wg", "Wo", "Wfk", "Wfr", "Wfv", "Wq3", "Wo3")}
        Wk3 = sb("Wk3", [P, NC, KV3 * D3])
        Wv3 = sb("Wv3", [P, NC, KV3 * D3])
        spread = sb("spread", [P, JS, P])
        gather = sb("gather", [P, JS, P])
        blocks = sb("head_blocks", [P, 2, P])
        x = sb("x_in2", [P, D])
        row1 = sb("state_row1", [P, NC])
        st6 = sb("ln1_stats", [P, 6])
        mv = sb("ln1_mean_var", [P, 2])
        ve = sb("ln1_var_eps", [P, 1])
        rstd = sb("ln1_rstd", [P, 1])
        nx = sb("ln1_x", [P, D])
        xaT = sb("xaT", [P, NC, P + 1])
        sx = sb("shifted", [P, NC, P])
        z = sb("z", [P, NC, P])
        t5 = sb("t5", [P, NM - 1, P])
        t5b = sb("t5b", [P, P])
        xm = [sb(f"xm{f}", [P, NC, P]) for f in range(NM)]
        u1 = sb("u1", [P, P])
        kT = sb("kT2", [P, NC, P])
        rT = sb("rT2", [P, NC, P])
        vT = sb("vT2", [P, NC, P])
        wS = sb("w_shifted", [P, NC, P])
        ruk = sb("ruk", [P, NC, P])
        g = sb("g2", [P, NC, P])
        eps5 = sb("eps5", [P, 1])
        xres = sb("x_res2", [P, D])
        s0 = sb("state0", [P, NC, D2])
        row0 = sb("state_row0", [P, NC])
        bonus = sb("bonus", [P, NC, P])
        kv = [sb(f"kv{q}", [P, NC, P]) for q in range(3)]
        state = [sb(f"states{q}", [P, NC, P]) for q in range(2)]
        rs = [sb(f"r_states{q}", [P, NC, P]) for q in range(2)]
        xcT = sb("xcT", [P, NC, P + 1])
        x1 = sb("x1", [P, D])
        st6b = sb("ln2_stats", [P, 6])
        mvb = sb("ln2_mean_var", [P, 2])
        veb = sb("ln2_var_eps", [P, 1])
        rstdb = sb("ln2_rstd", [P, 1])
        x3 = sb("x3", [P, D])
        og, dev, sq, gstd, grstd = state[0], state[1], kv[0], kv[1], kv[2]
        gated = rs[0]
        nx2 = flat(rs[1])
        sx2, xk2, xr2, kk, sig = kv[0], kv[1], state[0], state[1], flat(bonus)
        ctxT = sb("ctxT3", [P, NC, P])
        mask = sb("mask3", [P, P])
        x3T = sb("x3T", [P, NC, P])
        x3b = sb("x3_bo", [P, D])
        qT = sb("qT3", [P, G3, P])
        kS = sb("kT3", [P, P])
        kbd = sb("k_blocks", [P, KV3, P])
        v3 = sb("v3", [P, KV3 // 2, 2, V2])
        sc = [sb(f"scores{q}", [P, G3, P]) for q in range(3)]
        scT = [sb(f"probsT3_{q}", [P, G3, P]) for q in range(2)]
        nmax = sb("nmax3", [P, KV3, G3])
        rsum = sb("rsum3", [P, KV3, G3])
        rinv = sb("rinv3", [P, KV3, G3])
        rrep = sb("rinv3_repeated", [P, G3, KV3, D3])
        attn = sb("attn3", [P, G3, P])
        attnT = x3T
        y = rrep[:, :, :, :].rearrange("p a b d -> p (a b d)")
        lst6 = sb("ln3_stats", [P, 6])
        lmv = sb("ln3_mean_var", [P, 2])
        lve = sb("ln3_var_eps", [P, 1])
        lrstd = sb("ln3_rstd", [P, 1])
        out = sb("out3", [P, D])

        s_w2 = sem("l2_weights_loaded")
        s_w3 = sem("l3_weights_loaded")
        s_zero = sem("l23_zeros_made")
        s_inP = sem("p_inputs_loaded")
        s_inW = sem("w_inputs_loaded")
        s_inA = sem("a_inputs_loaded")
        s_hold = sem("l23_wait_held")
        s_dveP, s_dveW, s_dveA = sem("p_dve_step"), sem("w_dve_step"), sem("a_dve_step")
        s_var1 = sem("p_ln1_var_ready")
        s_rstd1 = sem("p_ln1_rstd_ready")
        s_nx1 = sem("p_ln1_ready")
        s_first1 = sem("p_first_row1_ready")
        s_z = sem("p_z_ready")
        s_xm = sem("p_mix_ready")
        s_wS = sem("p_decay_ready")
        s_ruk = sem("p_ruk_ready")
        s_scan = sem("w_states_ready")
        s_prod = sem("w_r_states_ready")
        s_sum = sem("w_sums_done")
        s_og = sem("w_outputs_read")
        s_sq = sem("w_gn_squares_ready")
        s_grstd = sem("w_gn_rstd_ready")
        s_scaled = sem("w_gn_scaled")
        s_gnorm = sem("w_gn_normed")
        s_gated = sem("w_gated_ready")
        s_var2 = sem("w_ln2_var_ready")
        s_rstd2 = sem("w_ln2_rstd_ready")
        s_nx2 = sem("w_ln2_ready")
        s_first2 = sem("w_first_row0_ready")
        s_xk2 = sem("w_ffn_k_ready")
        s_xr2 = sem("w_ffn_r_ready")
        s_kk = sem("w_ffn_kk_ready")
        s_x3 = sem("w_x_ready")
        s_x3b = sem("a_x_bo_ready")
        s_kbd = sem("a_k_blocks_ready")
        s_max = sem("a_max_ready")
        s_exp = sem("a_exp_ready")
        s_av = sem("a_values_weighted")
        s_rinv = sem("a_rinv_ready")
        s_rrep = sem("a_rinv_repeated")
        s_attn = sem("a_attention_ready")
        s_attnT = sem("a_attention_bias_added")
        s_var3 = sem("a_ln_var_ready")
        s_rstd3 = sem("a_ln_rstd_ready")
        s_out = sem("a_out_ready")
        s_store = sem("out_stored")
        OSUM, OAV = 2, 7
        rings = dict(pd=([3], NM), pa=([4], 8), w=([0, 1], JS + 8), ad=([5], KV3 + 1), aa=([6], 4 + KV3))
        S = {k: (sem(f"{k}_psum_ready"), sem(f"{k}_psum_free")) for k in rings}
        J_XA, J_T5, J_U1, J_Z, J_K, J_R, J_V, J_G = range(1, 9)
        J_BONUS, J_MEAN = 1, JS + 2
        J_GVAR, J_WO, J_XC, J_FK, J_FR, J_FV = (J_MEAN + k for k in range(1, 7))
        J3_X, J3_Q, J3_KV, J3_RINV = 1, 2, 3, 4 + KV3
        J3_WO = KV3 + 1

        def ring(k):
            return Ring(*S[k], *rings[k])

        beside = {0: [("b_out",)], 1: [("a_x",)], 2: [("p_xa",), ("b_ln",)], 3: [("a_q",)], 4: [("p_shift",)],
                  5: [("a_kv",), ("b_store",)], 7: [("p_t5",)], 8: [("a_score", 0)],
                  9: [("p_mix", 0), ("a_exp", 0)], 10: [("a_score", 1)],
                  11: [("p_mix", 1), ("a_turn", 0), ("a_exp", 1)], 12: [("a_score", 2)],
                  13: [("p_mix", 2), ("a_value", 0), ("a_turn", 1), ("a_exp", 2)], 14: [("a_score", 3)],
                  15: [("p_mix", 3), ("a_value", 1), ("a_turn", 2), ("a_exp", 3)], 16: [("a_score", 4)],
                  17: [("p_mix", 4), ("a_value", 2), ("a_turn", 3), ("a_exp", 4)]}
        ORDER = [("p_ln1",), ("w_bonus",)]
        for j in range(JS + LAG):
            ORDER += [("w_step", j)] + beside.get(j, [])
        ORDER += [("w_og",), ("p_u1",), ("a_score", 5), ("w_mean",), ("a_exp", 5), ("p_w",), ("a_value", 3), ("a_turn", 4),
                  ("w_var",), ("a_score", 6), ("p_k",), ("w_scale",), ("w_gnorm",), ("w_gate",), ("a_exp", 6),
                  ("a_value", 4), ("a_turn", 5), ("p_r",), ("a_score", 7), ("a_exp", 7), ("p_ruk",), ("w_out",),
                  ("a_value", 5), ("a_turn", 6), ("p_v",), ("w_ln2",), ("w_xc",), ("a_value", 6), ("a_turn", 7),
                  ("p_g",), ("w_fk",), ("a_rinv",), ("a_value", 7), ("a_norm",), ("w_fr",), ("w_fv",),
                  ("p_gate",)]

        def steps(eng, segments, begin):
            def step(*index):
                index = dict(zip("pwab", index))
                for stage in "pwab":
                    if index[stage] is not None:
                        begin(stage, index[stage])
                for name, *k in ORDER:
                    if index[name[0]] is not None and name in segments:
                        segments[name](index[name[0]], *k)

            for i in range(3):
                step(*(i - k if i >= k else None for k in range(4)))
            with eng.Fori(3, B) as i:
                step(i, i - 1, i - 2, i - 3)
            for i in range(B, B + 3):
                step(*(i - k if i - k < B else None for k in range(4)))

        with nc.Block() as block:
            @block.sync
            def _(sp):
                def load_p(i):
                    sp.dma_start(x[:, :], l1_out[i]).then_inc(s_inP, 16)
                    sp.dma_start(row1[:, :], a["row1"][i]).then_inc(s_inP, 16)

                def load_w(i):
                    sp.dma_start(s0[:, :, :], a["state"][i]).then_inc(s_inW, 16)
                    sp.dma_start(xres[:, :], l1_out[i]).then_inc(s_inW, 16)
                    sp.dma_start(row0[:, :], a["row0"][i]).then_inc(s_inW, 16)

                def load_a(i):
                    sp.dma_start(ctxT[:, :, :], a["ctxT"][i]).then_inc(s_inA, 16)
                    sp.dma_start(mask[:, :], a["mask3"][i]).then_inc(s_inA, 16)

                def reload_p(i):
                    sp.wait_ge(s_nx1, i)
                    sp.wait_ge(s_first1, i)
                    load_p(i)

                def reload_w(i):
                    sp.wait_ge(s_scan, JS * i)
                    sp.wait_ge(s_var2, i)
                    sp.wait_ge(s_first2, i)
                    load_w(i)

                def reload_a(i):
                    sp.wait_ge(s_max, KV3 * i)
                    load_a(i)

                load_p(0)
                sp.dma_start(maa_w1[:, :, :], a["maa_w1"]).then_inc(s_w2, 16)
                sp.dma_start(maa_w2[:, :], a["maa_w2"][0:P]).then_inc(s_w2, 16)
                sp.dma_start(maa_w2b[:, :], a["maa_w2"][P:2 * P]).then_inc(s_w2, 16)
                sp.dma_start(td_w1[:, :, :], a["td_w1"]).then_inc(s_w2, 16)
                sp.dma_start(td_w2[:, :], a["td_w2"]).then_inc(s_w2, 16)
                for n in ("Wk", "Wr", "Wv", "Wg"):
                    sp.dma_start(W[n][:, :, :], a[n]).then_inc(s_w2, 16)
                load_w(0)
                reload_p(1)
                for t, n in ((spread, "spread"), (gather, "gather"), (blocks, "blocks"), (W["Wo"], "Wo"),
                             (W["Wfk"], "Wfk"), (W["Wfr"], "Wfr"), (W["Wfv"], "Wfv"), (W["Wq3"], "Wq3"),
                             (Wk3, "Wk3"), (Wv3, "Wv3"), (W["Wo3"], "Wo3")):
                    sp.dma_start(t[:, :, :], a[n]).then_inc(s_w3, 16)
                load_a(0)
                reload_w(1)
                with sp.Fori(2, B) as i:
                    reload_p(i)
                    reload_a(i - 1)
                    reload_w(i)
                reload_a(B - 1)

            @block.gpsimd
            def _(pool):
                PD, AD, AA = ring("pd"), ring("ad"), ring("aa")
                for t in (t5[:, :, :], t5b[:, :], u1[:, :], wS[:, :, 0:1], v3[:, :, :, :]):
                    nc.gpsimd.memset(t, 0.0).then_inc(s_zero, 1)
                nc.gpsimd.memset(eps5[:, :], 1e-5).then_inc(s_zero, 1)

                def power(dst, src):
                    return nc.gpsimd.tensor_tensor(dst, src, halfs[:, 0:1], ALU.pow)

                def p_ln1(i):
                    pool.wait_ge(s_inP, 32 * i + 32)
                    if not isinstance(i, int) or i > 0:
                        pool.wait_ge(s_z, i)
                    pool.sem_inc(s_hold, 1)
                    nc.gpsimd.tensor_copy(xaT[:, :, 0], row1[:, :]).then_inc(s_first1, 1)
                    pool.wait_ge(s_var1, i + 1)
                    power(rstd[:, :], ve[:, :]).then_inc(s_rstd1, 1)

                def p_mix(i, f):
                    pool.wait_ge(PD.free, PD.read(i, f + 1))
                    nc.gpsimd.tensor_tensor(xm[f][:, :, :], xm[f][:, :, :], xaT[:, :, 1:P + 1], ALU.add)\
                        .then_inc(s_xm, 1)

                def w_step(i, j):
                    if not 1 <= j <= JS:
                        return
                    j -= 1
                    pool.wait_ge(s_scan, JS * i + j + 1)
                    if j >= 2:
                        pool.wait_ge(s_sum, JS * i + j - 1)
                    nc.gpsimd.tensor_tensor(rs[j % 2][:, :, :], state[j % 2][:, :, :], rT[:, :, :], ALU.mult)\
                        .then_inc(s_prod, 1)

                def w_out(i):
                    pool.wait_ge(s_inW, 48 * i + 48)
                    pool.sem_inc(s_hold, 1)
                    nc.gpsimd.tensor_copy(xcT[:, :, 0], row0[:, :]).then_inc(s_first2, 1)
                    pool.wait_ge(s_var2, i + 1)
                    power(rstdb[:, :], veb[:, :]).then_inc(s_rstd2, 1)

                def a_x(i):
                    pool.wait_ge(s_x3, i + 1)
                    if not isinstance(i, int) or i > 0:
                        pool.wait_ge(AD.free, AD.read(i - 1, J3_WO))
                    nc.gpsimd.tensor_tensor(x3b[:, :], x3[:, :], R("bo3"), ALU.add).then_inc(s_x3b, 1)

                def a_kv(i):
                    pool.wait_ge(AA.free, AA.read(i, J3_KV))
                    nc.gpsimd.tensor_tensor(kbd[:, :, :], kS[:, :].unsqueeze(1).to_broadcast([P, KV3, P]),
                                            hsum[:, :].unsqueeze(2).to_broadcast([P, KV3, P]), ALU.mult)\
                        .then_inc(s_kbd, 1)

                def a_norm(i):
                    pool.wait_ge(s_rinv, i + 1)
                    pool.sem_inc(s_hold, 1)
                    nc.gpsimd.tensor_copy(rrep[:, :, :, :], rinv[:, :, :].rearrange("p g c -> p c g").unsqueeze(3)
                                          .to_broadcast([P, G3, KV3, D3])).then_inc(s_rrep, 1)

                def b_out(i):
                    pool.wait_ge(s_var3, i + 1)
                    power(lrstd[:, :], lve[:, :]).then_inc(s_rstd3, 1)

                steps(pool, dict(p_ln1=p_ln1, p_mix=p_mix, w_step=w_step, w_out=w_out, a_x=a_x,
                                 a_kv=a_kv, a_norm=a_norm, b_out=b_out), lambda stage, i: None)

            @block.tensor
            def _(pe):
                for k in rings:
                    pe.sem_inc(S[k][1], len(rings[k][0]))
                pe.sem_inc(s_og, 1)
                pe.sem_inc(s_attn, 1)
                PD, PA, WR, AD, AA, BD = (ring(k) for k in ("pd", "pa", "w", "ad", "aa", "ad"))

                def begin(stage, i):
                    for r in dict(p=(PD, PA), w=(WR,), a=(AD, AA), b=(BD,))[stage]:
                        r.begin(i)
                    BD.n = KV3
                    if stage == "w" and isinstance(i, int) and i == 0:
                        pe.wait_ge(s_w3, 16 * 11)

                def turn4(r, src):
                    b = r.next()
                    pe.wait_ge(r.free, r.count)
                    for c in range(NC):
                        mm = nc.tensor.transpose(PS[b][:, c * P:(c + 1) * P], src[:, c * P:(c + 1) * P], ident[:, :])
                    mm.then_inc(r.ready, 1)

                def channel_major(r, w, xT):
                    b = r.next()
                    pe.wait_ge(r.free, r.count)
                    for m in range(NC):
                        for c in range(NC):
                            mm = nc.tensor.matmul(PS[b][:, m * P:(m + 1) * P], w[:, c, m * P:(m + 1) * P], xT[:, c, :],
                                                  start=(c == 0), stop=(c == NC - 1))
                    mm.then_inc(r.ready, 1)

                def token_major(r, w, xT):
                    b = r.next()
                    pe.wait_ge(r.free, r.count)
                    for c in range(NC):
                        mm = nc.tensor.matmul(PS[b][:, :], xT[:, c, :], w[:, c, :], start=(c == 0), stop=(c == NC - 1))
                    mm.then_inc(r.ready, 1)

                def over_head(r, k, src):
                    b = r.next()
                    pe.wait_ge(r.free, r.count)
                    nc.tensor.matmul(PS[b][:, :], blocks[:, k, :], flat(src), start=True, stop=True).then_inc(r.ready, 1)

                def p_xa(i):
                    pe.wait_ge(s_nx1, i + 1)
                    turn4(PA, nx)

                def p_t5(i):
                    b = PA.next()
                    pe.wait_ge(PA.free, PA.count)
                    pe.wait_ge(s_z, i + 1)
                    for c in range(NC):
                        nc.tensor.matmul(PS[b][:, 0:P], maa_w1[:, c, 0:P], z[:, c, :], start=(c == 0), stop=(c == NC - 1))
                    for c in range(NC):
                        mm = nc.tensor.matmul(PS[b][0:DM, P:2 * P], maa_w1[:, c, P:P + DM], z[:, c, :],
                                              start=(c == 0), stop=(c == NC - 1))
                    mm.then_inc(PA.ready, 1)

                def p_mix(i, f):
                    b = PD.next()
                    pe.wait_ge(PD.free, PD.count)
                    if f == 0:
                        pe.wait_ge(PA.free, PA.read(i, J_T5))
                    w, t = (maa_w2, t5[:, f, :]) if f < NM - 1 else (maa_w2b, t5b[:, :])
                    for m in range(NC):
                        mm = nc.tensor.matmul(PS[b][:, m * P:(m + 1) * P], w[:, m * P:(m + 1) * P], t, start=True, stop=True)
                    mm.then_inc(PD.ready, 1)

                def p_u1(i):
                    b = PA.next()
                    pe.wait_ge(PA.free, PA.count)
                    pe.wait_ge(s_xm, NM * i + 2)
                    for c in range(NC):
                        mm = nc.tensor.matmul(PS[b][0:DD, 0:P], td_w1[:, c, :], xm[1][:, c, :], start=(c == 0), stop=(c == NC - 1))
                    mm.then_inc(PA.ready, 1)

                def p_w(i):
                    b = PA.next()
                    pe.wait_ge(PA.free, PA.count)
                    pe.wait_ge(PA.free, PA.read(i, J_U1))
                    for m in range(NC):
                        mm = nc.tensor.matmul(PS[b][:, m * P:(m + 1) * P], td_w2[:, m * P:(m + 1) * P], u1[:, :], start=True, stop=True)
                    mm.then_inc(PA.ready, 1)

                def projected(f, w):
                    def seg(i):
                        pe.wait_ge(s_xm, NM * i + f + 1)
                        channel_major(PA, W[w], xm[f])
                    return seg

                def w_bonus(i):
                    pe.wait_ge(s_ruk, i + 1)
                    over_head(WR, 0, ruk)

                def w_step(i, j):
                    if j < JS:
                        b = WR.next()
                        pe.wait_ge(WR.free, WR.count)
                        nc.tensor.matmul(PS[b][:, :], spread[:, j, :], flat(vT), start=True, stop=True).then_inc(WR.ready, 1)
                    if j >= LAG:
                        j -= LAG
                        if j == 0:
                            pe.wait_ge(s_og, i + 1)
                        pe.wait_ge(s_prod, JS * i + j + 1)
                        nc.tensor.matmul(PS[OSUM][:, :], gather[:, j, :], flat(rs[j % 2]), start=(j == 0), stop=(j == JS - 1))\
                            .then_inc(s_sum, 1)

                def w_mean(i):
                    pe.wait_ge(s_og, i + 2)
                    over_head(WR, 1, og)

                def w_var(i):
                    pe.wait_ge(s_sq, i + 1)
                    over_head(WR, 1, sq)

                def w_out(i):
                    pe.wait_ge(s_gated, i + 1)
                    token_major(WR, W["Wo"], gated)

                def w_xc(i):
                    pe.wait_ge(s_nx2, i + 1)
                    turn4(WR, nx2)

                def w_fk(i):
                    pe.wait_ge(s_xk2, i + 1)
                    channel_major(WR, W["Wfk"], xk2)

                def w_fr(i):
                    pe.wait_ge(s_xr2, i + 1)
                    token_major(WR, W["Wfr"], xr2)

                def w_fv(i):
                    pe.wait_ge(s_kk, i + 1)
                    token_major(WR, W["Wfv"], kk)

                def a_x(i):
                    pe.wait_ge(s_x3, i + 1)
                    turn4(AA, x3)

                def a_q(i):
                    pe.wait_ge(AA.free, AA.read(i, J3_X))
                    channel_major(AA, W["Wq3"], x3T)

                def a_kv(i):
                    b = AA.next()
                    pe.wait_ge(AA.free, AA.count)
                    pe.wait_ge(s_inA, 32 * i + 32)
                    for c in range(NC):
                        nc.tensor.matmul(PS[b][:, 0:P], Wk3[:, c, :], ctxT[:, c, :], start=(c == 0), stop=(c == NC - 1))
                    for c in range(NC):
                        mm = nc.tensor.matmul(PS[b][:, P:2 * P], ctxT[:, c, :], Wv3[:, c, :], start=(c == 0), stop=(c == NC - 1))
                    mm.then_inc(AA.ready, 1)

                def a_score(i, u):
                    b = AD.next()
                    pe.wait_ge(AD.free, AD.count)
                    if u == 0:
                        pe.wait_ge(s_kbd, i + 1)
                    for c in range(G3):
                        mm = nc.tensor.matmul(PS[b][:, c * P:(c + 1) * P], qT[:, c, :], kbd[:, u, :], start=True, stop=True)
                    mm.then_inc(AD.ready, 1)

                def a_turn(i, u):
                    pe.wait_ge(s_exp, KV3 * i + u + 1)
                    turn4(AA, flat(sc[u % 3]))

                def a_value(i, u):
                    if u == 0:
                        pe.wait_ge(s_attn, i + 1)
                    pe.wait_ge(AA.free, AA.read(i, J3_KV + 1 + u))
                    nc.tensor.matmul(PS[OAV][V2 * (u // 2):V2 * (u // 2 + 1), :], v3[:, u // 2, u % 2, :], flat(scT[u % 2]),
                                     start=(u % 2 == 0), stop=(u % 2 == 1)).then_inc(s_av, 1)

                def a_norm(i):
                    pe.wait_ge(s_rrep, i + 1)
                    turn4(AA, y)

                def b_out(i):
                    pe.wait_ge(s_attnT, i + 1)
                    token_major(BD, W["Wo3"], attnT)

                pe.wait_ge(s_w2, 16 * 9)
                steps(pe, dict(p_xa=p_xa, p_t5=p_t5, p_mix=p_mix, p_u1=p_u1, p_w=p_w, p_k=projected(0, "Wk"),
                               p_r=projected(3, "Wr"), p_v=projected(2, "Wv"), p_g=projected(4, "Wg"),
                               w_bonus=w_bonus, w_step=w_step, w_mean=w_mean, w_var=w_var, w_out=w_out, w_xc=w_xc,
                               w_fk=w_fk, w_fr=w_fr, w_fv=w_fv, a_x=a_x, a_q=a_q, a_kv=a_kv, a_score=a_score,
                               a_turn=a_turn, a_value=a_value, a_norm=a_norm, b_out=b_out), begin)

            @block.scalar
            def _(act):
                PD, PA, WR, AA = ring("pd"), ring("pa"), ring("w"), ring("aa")
                act.wait_ge(s_zero, 6)

                def begin(stage, i):
                    if stage != "b":
                        dict(p=PA, w=WR, a=AA)[stage].begin(i)

                def c4(ps):
                    return ps[:, :].rearrange("p (c t) -> p c t", c=NC)

                def next_bank(r):
                    b = r.next()
                    act.wait_ge(r.ready, r.count)
                    return PS[b]

                def later(i):
                    return not isinstance(i, int) or i > 0

                def scaled(dst, ps, w, b, free):
                    for c in range(NC):
                        ac = nc.scalar.activation(dst[:, c, 1:P + 1], ps[:, c * P:(c + 1) * P], ACT.Identity,
                                                  bias=C(b, c), scale=C(w, c))
                    ac.then_inc(free, 1)

                def p_xa(i):
                    ps = next_bank(PA)
                    if later(i):
                        act.wait_ge(s_xm, NM * i)
                    scaled(xaT, ps, "ln1_w", "ln1_b", PA.free)

                def p_t5(i):
                    ps = next_bank(PA)
                    if later(i):
                        act.wait_ge(PD.ready, PD.written(i - 1, NM))
                    for f in range(NM - 1):
                        rows = slice(DM * f, DM * f + DM)
                        nc.scalar.activation(t5[rows, f, :], ps[rows, 0:P], ACT.Tanh)
                    nc.scalar.activation(t5b[0:DM, :], ps[0:DM, P:2 * P], ACT.Tanh).then_inc(PA.free, 1)

                def p_u1(i):
                    ps = next_bank(PA)
                    nc.scalar.activation(u1[0:DD, :], ps[0:DD, 0:P], ACT.Tanh).then_inc(PA.free, 1)

                def p_w(i):
                    ps = next_bank(PA)
                    for c in range(NC):
                        ac = nc.scalar.activation(z[:, c, :], ps[:, c * P:(c + 1) * P], ACT.Exp, bias=C("decay", c))
                    ac.then_inc(PA.free, 1)
                    act.wait_ge(PA.free, PA.read(i, J_Z))
                    if later(i):
                        act.wait_ge(s_scan, JS * i)
                    nc.scalar.activation(wS[:, :, 1:P], z[:, :, 0:P - 1], ACT.Exp, scale=-1.0).then_inc(s_wS, 1)

                def p_k(i):
                    ps = next_bank(PA)
                    if later(i):
                        act.wait_ge(s_scan, JS * i)
                    nc.scalar.activation(kT[:, :, :], c4(ps), ACT.Copy).then_inc(PA.free, 1)

                def p_r(i):
                    ps = next_bank(PA)
                    if later(i):
                        act.wait_ge(s_prod, JS * i)
                    nc.scalar.activation(rT[:, :, :], c4(ps), ACT.Copy).then_inc(PA.free, 1)

                def p_v(i):
                    ps = next_bank(PA)
                    nc.scalar.activation(vT[:, :, :], c4(ps), ACT.Copy).then_inc(PA.free, 1)

                def p_g(i):
                    ps = next_bank(PA)
                    nc.scalar.activation(z[:, :, :], c4(ps), ACT.Tanh, scale=0.5)
                    if later(i):
                        act.wait_ge(s_gated, i)
                    nc.scalar.activation(g[:, :, :], c4(ps), ACT.Copy).then_inc(PA.free, 1)

                def w_mean(i):
                    WR.n += 1 + JS + 1
                    act.wait_ge(WR.free, WR.read(i, J_MEAN))
                    nc.scalar.activation(sq[:, :, :], dev[:, :, :], ACT.Square).then_inc(s_sq, 1)

                def w_var(i):
                    nc.scalar.activation(gstd[:, :, :], c4(next_bank(WR)), ACT.Sqrt, bias=eps5[:, :]).then_inc(WR.free, 1)

                def w_gnorm(i):
                    WR.n += 1
                    act.wait_ge(s_scaled, i + 1)
                    for c in range(NC):
                        ac = nc.scalar.activation(dev[:, c, :], dev[:, c, :], ACT.Identity, bias=C("gn_b", c), scale=C("gn_w", c))
                    ac.then_inc(s_gnorm, 1)

                def w_xc(i):
                    scaled(xcT, next_bank(WR), "ln2_w", "ln2_b", WR.free)

                def w_fk(i):
                    nc.scalar.activation(kk[:, :, :], c4(next_bank(WR)), ACT.Relu).then_inc(WR.free, 1)
                    act.wait_ge(WR.free, WR.read(i, J_FK))
                    nc.scalar.activation(kk[:, :, :], kk[:, :, :], ACT.Square).then_inc(s_kk, 1)

                def w_fr(i):
                    nc.scalar.activation(sig, next_bank(WR)[:, :], ACT.Tanh, scale=0.5).then_inc(WR.free, 1)

                def a_x(i):
                    nc.scalar.activation(x3T[:, :, :], c4(next_bank(AA)), ACT.Copy).then_inc(AA.free, 1)

                def a_q(i):
                    ps = next_bank(AA)
                    for c in range(G3):
                        ac = nc.scalar.activation(qT[:, c, :], ps[:, c * P:(c + 1) * P], ACT.Identity, bias=C("bq3", c))
                    ac.then_inc(AA.free, 1)

                def a_kv(i):
                    ps = next_bank(AA)
                    nc.scalar.activation(kS[:, :], ps[:, 0:P], ACT.Identity, bias=C("bk3"))
                    vals = ps[:, P:2 * P].rearrange("p (g two d) -> p g two d", two=2, d=D3)
                    nc.scalar.activation(v3[:, :, 0, 0:D3], vals[:, :, 0, :], ACT.Copy)
                    nc.scalar.activation(v3[:, :, 1, D3:V2], vals[:, :, 1, :], ACT.Copy).then_inc(AA.free, 1)

                def a_exp(i, u):
                    act.wait_ge(s_max, KV3 * i + u + 1)
                    for c in range(G3):
                        s = sc[u % 3][:, c, :]
                        ac = nc.scalar.activation(s, s, ACT.Exp, bias=nmax[:, u, c:c + 1], accum_out=rsum[:, u, c:c + 1])
                    ac.then_inc(s_exp, 1)

                def a_turn(i, u):
                    ps = next_bank(AA)
                    if u >= 2:
                        act.wait_ge(s_av, KV3 * i + u - 1)
                    nc.scalar.activation(scT[u % 2][:, :, :], c4(ps), ACT.Copy).then_inc(AA.free, 1)

                def a_norm(i):
                    nc.scalar.activation(attn[:, :, :], c4(next_bank(AA)), ACT.Copy).then_inc(AA.free, 1)
                    act.wait_ge(s_attn, i + 2)
                    nc.scalar.activation(attnT[:, :, :], attn[:, :, :], ACT.Identity, bias=C("bv3")).then_inc(s_attnT, 1)

                def b_store(i):
                    act.wait_ge(s_out, i + 1)
                    act.dma_start(a["out"][i], out[:, :]).then_inc(s_store, 16)

                steps(act, dict(p_xa=p_xa, p_t5=p_t5, p_u1=p_u1, p_w=p_w, p_k=p_k, p_r=p_r, p_v=p_v, p_g=p_g,
                                w_mean=w_mean, w_var=w_var, w_gnorm=w_gnorm, w_xc=w_xc, w_fk=w_fk, w_fr=w_fr, a_x=a_x, a_q=a_q,
                                a_kv=a_kv, a_exp=a_exp, a_turn=a_turn, a_norm=a_norm, b_store=b_store), begin)
                act.wait_ge(s_store, 16 * (B + 1))

            @block.vector
            def _(dve):
                PD, PA, WR, AD, AA, BD = (ring(k) for k in ("pd", "pa", "w", "ad", "aa", "ad"))
                E = dict(p=Steps(4), w=Steps(3), b=Steps(4))
                dve.sem_inc(s_store, 16)

                def begin(stage, i):
                    for r in dict(p=(PD, E["p"]), w=(WR, E["w"]), a=(AD,), b=(BD, E["b"]))[stage]:
                        r.begin(i)
                    BD.n = KV3

                def next_bank(r):
                    b = r.next()
                    dve.wait_ge(r.ready, r.count)
                    return PS[b]

                def c4(ps):
                    return ps[:, :].rearrange("p (c t) -> p c t", c=NC)

                def layer_norm_stats(src, t6, tmv, tve, eps, steps, s_step, s_var):
                    nc.vector.bn_stats(t6[:, :], src).then_inc(s_step, steps.tick())
                    dve.wait_ge(s_step, steps.now)
                    dve.sem_inc(s_hold, 1)
                    nc.vector.bn_aggr(tmv[:, :], t6[:, :]).then_inc(s_step, steps.tick())
                    dve.wait_ge(s_step, steps.now)
                    nc.vector.tensor_scalar(tve[:, :], tmv[:, 1:2], eps, None, ALU.add).then_inc(s_var, 1)

                def p_ln1(i):
                    dve.wait_ge(s_inP, 32 * i + 32)
                    layer_norm_stats(x[:, :], st6, mv, ve, 1e-5, E["p"], s_dveP, s_var1)

                def p_xa(i):
                    dve.wait_ge(s_rstd1, i + 1)
                    nc.vector.tensor_scalar(nx[:, :], x[:, :], mv[:, 0:1], rstd[:, :], ALU.subtract, ALU.mult)\
                        .then_inc(s_nx1, 1)

                def p_shift(i):
                    dve.wait_ge(PA.free, PA.read(i, J_XA))
                    dve.wait_ge(s_first1, i + 1)
                    nc.vector.tensor_tensor(sx[:, :, :], xaT[:, :, 0:P], xaT[:, :, 1:P + 1], ALU.subtract)\
                        .then_inc(s_dveP, E["p"].tick())
                    dve.wait_ge(s_dveP, E["p"].now)
                    for c in range(NC):
                        v_ = nc.vector.scalar_tensor_tensor(out=z[:, c, :], in0=sx[:, c, :], scalar=C("maa_x", c),
                                                            in1=xaT[:, c, 1:P + 1], op0=ALU.mult, op1=ALU.add)
                    v_.then_inc(s_z, 1)

                def p_mix(i, f):
                    ps = next_bank(PD)
                    for c in range(NC):
                        v_ = nc.vector.scalar_tensor_tensor(out=xm[f][:, c, :], in0=ps[:, c * P:(c + 1) * P],
                                                            scalar=C("maa_stack", f * NC + c), in1=sx[:, c, :],
                                                            op0=ALU.add, op1=ALU.mult)
                    v_.then_inc(PD.free, 1)

                def p_ruk(i):
                    dve.wait_ge(PA.free, PA.read(i, J_R))
                    for c in range(NC):
                        v_ = nc.vector.scalar_tensor_tensor(out=ruk[:, c, :], in0=kT[:, c, :], scalar=C("u", c),
                                                            in1=rT[:, c, :], op0=ALU.mult, op1=ALU.mult)
                    v_.then_inc(s_ruk, 1)

                def p_gate(i):
                    dve.wait_ge(PA.free, PA.read(i, J_G))
                    nc.vector.scalar_tensor_tensor(out=g[:, :, :], in0=z[:, :, :], scalar=1.0, in1=g[:, :, :],
                                                   op0=ALU.add, op1=ALU.mult).then_inc(s_dveP, E["p"].tick())
                    E["p"].end()

                def w_bonus(i):
                    ps = next_bank(WR)
                    dve.wait_ge(PA.free, PA.read(i, J_V))
                    if later(i):
                        dve.wait_ge(s_x3, i)
                    nc.vector.tensor_tensor(bonus[:, :, :], c4(ps), vT[:, :, :], ALU.mult).then_inc(WR.free, 1)
                    dve.wait_ge(s_wS, i + 1)
                    dve.wait_ge(s_inW, 48 * i + 48)

                def w_step(i, j):
                    if j < JS:
                        if j >= 3:
                            dve.wait_ge(s_scan, JS * i + j - 2)
                        nc.vector.tensor_copy(kv[j % 3][:, :, 0], s0[:, :, j])
                        ps = next_bank(WR)
                        nc.vector.tensor_tensor(kv[j % 3][:, :, 1:P], c4(ps)[:, :, 0:P - 1], kT[:, :, 0:P - 1], ALU.mult)\
                            .then_inc(WR.free, 1)
                    if 1 <= j <= JS:
                        j -= 1
                        if j >= 2:
                            dve.wait_ge(s_prod, JS * i + j - 1)
                        dve.wait_ge(WR.free, WR.read(i, J_BONUS + 1 + j))
                        nc.vector.tensor_tensor_scan(flat(state[j % 2]), flat(wS), flat(kv[j % 3]), 0.0,
                                                     ALU.mult, ALU.add).then_inc(s_scan, 1)

                def w_og(i):
                    dve.wait_ge(s_sum, JS * i + JS)
                    nc.vector.tensor_tensor(og[:, :, :], c4(PS[OSUM]), bonus[:, :, :], ALU.add).then_inc(s_og, 1)

                def w_mean(i):
                    ps = next_bank(WR)
                    dve.wait_ge(s_og, i + 2)
                    nc.vector.tensor_tensor(dev[:, :, :], og[:, :, :], c4(ps), ALU.subtract).then_inc(WR.free, 1)

                def w_scale(i):
                    WR.n += 1
                    dve.wait_ge(WR.free, WR.read(i, J_GVAR))
                    nc.vector.reciprocal(grstd[:, :, :], gstd[:, :, :]).then_inc(s_grstd, 1)
                    dve.wait_ge(s_grstd, i + 1)
                    nc.vector.tensor_tensor(dev[:, :, :], dev[:, :, :], grstd[:, :, :], ALU.mult).then_inc(s_scaled, 1)

                def w_gate(i):
                    dve.wait_ge(s_gnorm, i + 1)
                    nc.vector.scalar_tensor_tensor(out=gated[:, :, :], in0=dev[:, :, :], scalar=0.5, in1=g[:, :, :],
                                                   op0=ALU.mult, op1=ALU.mult).then_inc(s_gated, 1)

                def w_out(i):
                    nc.vector.tensor_tensor(x1[:, :], next_bank(WR)[:, :], xres[:, :], ALU.add).then_inc(WR.free, 1)
                    dve.wait_ge(WR.free, WR.read(i, J_WO))
                    layer_norm_stats(x1[:, :], st6b, mvb, veb, 1e-5, E["w"], s_dveW, s_var2)

                def w_ln2(i):
                    dve.wait_ge(s_rstd2, i + 1)
                    nc.vector.tensor_scalar(nx2, x1[:, :], mvb[:, 0:1], rstdb[:, :], ALU.subtract, ALU.mult)\
                        .then_inc(s_nx2, 1)

                def w_xc(i):
                    dve.wait_ge(WR.free, WR.read(i, J_XC))
                    dve.wait_ge(s_first2, i + 1)
                    nc.vector.tensor_tensor(sx2[:, :, :], xcT[:, :, 0:P], xcT[:, :, 1:P + 1], ALU.subtract)\
                        .then_inc(s_dveW, E["w"].tick())
                    dve.wait_ge(s_dveW, E["w"].now)
                    for dst, name, done in ((xk2, "ffn_k", s_xk2), (xr2, "ffn_r", s_xr2)):
                        for c in range(NC):
                            v_ = nc.vector.scalar_tensor_tensor(out=dst[:, c, :], in0=sx2[:, c, :], scalar=C(name, c),
                                                                in1=xcT[:, c, 1:P + 1], op0=ALU.mult, op1=ALU.add)
                        v_.then_inc(done, 1)
                    E["w"].end()

                def w_fv(i):
                    WR.n += 3
                    ps = next_bank(WR)
                    dve.wait_ge(WR.free, WR.read(i, J_FR))
                    nc.vector.scalar_tensor_tensor(out=sig, in0=sig, scalar=1.0, in1=ps[:, :],
                                                   op0=ALU.add, op1=ALU.mult).then_inc(WR.free, 1)
                    dve.wait_ge(WR.free, WR.read(i, J_FV))
                    if later(i):
                        dve.wait_ge(s_x3b, i)
                        dve.wait_ge(AA.ready, AA.written(i - 1, J3_X))
                    nc.vector.scalar_tensor_tensor(out=x3[:, :], in0=sig, scalar=0.5, in1=x1[:, :],
                                                   op0=ALU.mult, op1=ALU.add).then_inc(s_x3, 1)

                def later(i):
                    return not isinstance(i, int) or i > 0

                def a_score(i, u):
                    ps = next_bank(AD)
                    if u >= 3:
                        dve.wait_ge(AA.ready, AA.written(i, J3_KV + 1 + u - 3))
                    s = sc[u % 3]
                    nc.vector.scalar_tensor_tensor(out=s[:, :, :], in0=c4(ps), scalar=0.25,
                                                   in1=mask[:, :].unsqueeze(1).to_broadcast([P, G3, P]),
                                                   op0=ALU.mult, op1=ALU.add).then_inc(AD.free, 1)
                    dve.wait_ge(AD.free, AD.read(i, u + 1))
                    nc.vector.tensor_reduce(nmax[:, u, :], s[:, :, :], AX.X, ALU.max, negate=True).then_inc(s_max, 1)

                def a_rinv(i):
                    dve.wait_ge(s_exp, KV3 * i + KV3)
                    nc.vector.reciprocal(rinv[:, :, :], rsum[:, :, :]).then_inc(s_rinv, 1)

                def a_norm(i):
                    dve.wait_ge(s_av, KV3 * i + KV3)
                    dve.wait_ge(AA.free, AA.read(i, J3_RINV))
                    nc.vector.tensor_tensor(attn[:, :, :], c4(PS[OAV]), attn[:, :, :], ALU.mult).then_inc(s_attn, 1)

                def b_out(i):
                    ps = next_bank(BD)
                    dve.wait_ge(s_x3b, i + 1)
                    nc.vector.tensor_tensor(y, ps[:, :], x3b[:, :], ALU.add).then_inc(BD.free, 1)
                    dve.wait_ge(BD.free, BD.read(i, J3_WO))
                    layer_norm_stats(y, lst6, lmv, lve, 1e-6, E["b"], s_dveA, s_var3)

                def b_ln(i):
                    dve.wait_ge(s_rstd3, i + 1)
                    nc.vector.tensor_scalar(y, y, lmv[:, 0:1], lrstd[:, :], ALU.subtract, ALU.mult)\
                        .then_inc(s_dveA, E["b"].tick())
                    dve.wait_ge(s_dveA, E["b"].now)
                    dve.wait_ge(s_store, 16 * i + 16)
                    nc.vector.tensor_tensor(out[:, :], y, R("gamma3"), ALU.mult).then_inc(s_dveA, E["b"].tick())
                    dve.wait_ge(s_dveA, E["b"].now)
                    nc.vector.tensor_tensor(out[:, :], out[:, :], R("beta3"), ALU.add).then_inc(s_out, 1)
                    E["b"].end()

                steps(dve, dict(p_ln1=p_ln1, p_xa=p_xa, p_shift=p_shift, p_mix=p_mix, p_ruk=p_ruk, p_gate=p_gate,
                                w_bonus=w_bonus, w_step=w_step, w_og=w_og, w_mean=w_mean,
                                w_scale=w_scale, w_gate=w_gate, w_out=w_out, w_ln2=w_ln2, w_xc=w_xc, w_fv=w_fv,
                                a_score=a_score, a_rinv=a_rinv, a_norm=a_norm, b_out=b_out, b_ln=b_ln), begin)


def program(nc, a):
    ctx = ExitStack()
    with ctx:
        def sb(name, shape, dt=F32):
            return ctx.enter_context(nc.sbuf_tensor(name, shape, dt))

        def sem(name):
            return ctx.enter_context(nc.semaphore(name))

        PS = [ctx.enter_context(nc.psum_tensor(f"bank{k}", [P, 512], F32)) for k in range(8)]

        cols = sb("cols", [P, NCOLS])
        rows = sb("rows", [P, len(ROWS) - ROWS1, D])
        ident = sb("ident", [P, P])
        hsum = sb("hsum", [P, HC])
        hsum4 = sb("hsum4", [P, P // D1])
        halfs = sb("halfs", [P, H2])
        at, col = 0, {}
        for name, n in COLS:
            col[name] = (at, n)
            at += n

        def C(name, k=0, parts=P):
            return cols[0:parts, col[name][0] + k:col[name][0] + k + 1]

        def CS(name):
            return cols[:, col[name][0]:col[name][0] + col[name][1]]

        def R(name):
            k = ROWS.index(name)
            return rows[:, k, :] if k < len(ROWS) - ROWS1 else rows1[:, k - len(ROWS) + ROWS1, :]


        s_const = sem("const_loaded")
        s_ident = sem("ident_made")
        s_bn = sem("bn_scale_ready")
        l0_out = nc.dram_tensor("l0_out", (B, P, D), F32, kind="Internal").ap()
        l1_out = nc.dram_tensor("l1_out", (B, P, D), F32, kind="Internal").ap()
        bn_scale = sb("bn_scale", [P, 1])
        bn_shift = sb("bn_shift", [P, 1])

        w1_scope = ctx.enter_context(ExitStack())

        def sb1(name, shape, dt=F32):
            return w1_scope.enter_context(nc.sbuf_tensor(name, shape, dt))

        rows1 = sb1("rows1", [P, ROWS1, D])
        q_w = sb1("q_w", [P, NC, D])
        k_w = sb1("k_w", [P, NC, D])
        v_w = sb1("v_w", [P, NC, D])
        out_w = sb1("out_w", [P, NC, D])
        mlp_w1 = sb1("mlp_w1", [P, NC, NF * P])
        mlp_w2 = sb1("mlp_w2", [P, NF, D])
        s_w1 = sem("layer1_weights_loaded")

        layer0(nc, a, PS, sem, C, cols, rows, rows1, ident, hsum, hsum4, halfs, s_const, s_ident, bn_scale, bn_shift,
               l0_out, (q_w, k_w, v_w, out_w, mlp_w1, mlp_w2), s_w1)
        layer1(nc, a, PS, sem, C, R, CS, ident, hsum4, halfs, bn_scale, bn_shift, l0_out, l1_out,
               (q_w, k_w, v_w, out_w, mlp_w1, mlp_w2))
        w1_scope.close()
        layers23(nc, a, PS, sem, C, R, CS, ident, hsum, halfs, l1_out)


def _layout(v):
    import numpy as np

    f = {k: np.asarray(x) for k, x in v.items()}

    def chunks(w):
        w = np.asarray(w)
        return np.ascontiguousarray(w.reshape(w.shape[0] // P, P, w.shape[1]).transpose(1, 0, 2))

    def col(x):
        x = np.asarray(x).reshape(-1)
        if x.size < P:
            x = np.pad(x, (0, P - x.size))
        return x.reshape(-1, P).T

    l0, l1, l2, l3 = (lambda n: f["L0_xattn_" + n]), (lambda n: f["L1_xattn_" + n]), \
        (lambda n: f["L2_xattn_" + n]), (lambda n: f["L3_xattn_" + n])
    byq = np.arange(H3 * D3).reshape(KV3, G3, D3).transpose(1, 0, 2).reshape(-1)

    def padded(w, rows):
        return np.pad(w, ((0, rows - w.shape[0]), (0, 0)))

    o = {}
    o["x"] = f["x"]
    o["ctx"] = f["ctx_2048"]
    o["ctxT"] = np.ascontiguousarray(f["ctx_2048"].reshape(B, P, NC, P).transpose(0, 3, 2, 1))
    state = f["ctx_2048"]
    o["state"] = state[:, 2:2 + D2].reshape(B, NC, P, D2).transpose(0, 2, 1, 3)
    o["row0"] = state[:, 0].reshape(B, NC, P).transpose(0, 2, 1)
    o["row1"] = state[:, 1].reshape(B, NC, P).transpose(0, 2, 1)
    o["mask1"] = f["mask_BxS2_ik0"]
    o["mask3"] = f["mask_Bx1xSxS2_ff0"].reshape(B, P, P)
    o["w0"] = np.stack([l0("Wtheta").T, l0("Wphi").T, l0("Wg").T], axis=1)
    o["wz"] = l0("Wz").T
    o["q_w"] = chunks(l1("q_w"))
    o["k_w"] = chunks(l1("kv_w")[:, 0::2])
    o["v_w"] = chunks(l1("kv_w")[:, 1::2])
    o["out_w"] = chunks(l1("out_w"))
    o["mlp_w1"] = chunks(l1("mlp_w1"))
    o["mlp_w2"] = chunks(l1("mlp_w2"))
    o["maa_w1"] = chunks(l2("maa_w1"))
    o["maa_w2"] = padded(l2("maa_w2").reshape(NM * DM, D), 2 * P)
    o["td_w1"] = chunks(l2("td_w1"))
    o["td_w2"] = padded(l2("td_w2"), P)
    for n in ("Wr", "Wk", "Wv", "Wg", "Wo", "Wfk", "Wfr", "Wfv"):
        o[n] = chunks(l2(n).T)
    o["Wq3"] = chunks(l3("Wq")[:, byq])
    o["Wk3"] = chunks(l3("Wk"))
    o["Wv3"] = chunks(l3("Wv"))
    o["Wo3"] = chunks(l3("Wo")[byq])
    vec = dict(btheta=l0("btheta"), bphi=l0("bphi"), bg=l0("bg"), bz=l0("bz"), bn_gamma=l0("gamma"),
               bn_beta=l0("beta"), q_b=l1("q_b"), k_b=l1("kv_b")[0::2], v_b=l1("kv_b")[1::2],
               post_w=l1("postnorm_w"), b1=l1("mlp_b1"), ln1_w=l2("ln1_w"), ln1_b=l2("ln1_b"),
               ln2_w=l2("ln2_w"), ln2_b=l2("ln2_b"), maa_x=l2("maa_x"), maa_stack=l2("maa_stack"),
               decay=l2("time_decay"), u=l2("u"), ffn_k=l2("ffn_maa_k"), ffn_r=l2("ffn_maa_r"),
               gn_w=l2("gn_w"), gn_b=l2("gn_b"),
               bq3=l3("bq")[byq], bk3=l3("bk"), bv3=l3("bv"))
    o["cols"] = np.concatenate([col(vec[n]) for n, _ in COLS], axis=1)
    row = dict(out_b=l1("out_b"), b2=l1("mlp_b2"), bo3=l3("bo"),
               gamma3=l3("gamma"), beta3=l3("beta"))
    o["rows"] = np.stack([row[n] for n in ROWS[:-ROWS1]])
    o["rows1"] = np.stack([row[n] for n in ROWS[-ROWS1:]])
    o["hsum"] = (np.arange(P)[:, None] // D2 == np.arange(HC)[None, :]).astype(np.float32)
    o["hsum4"] = (np.arange(P)[:, None] // D1 == np.arange(P // D1)[None, :]).astype(np.float32)
    head, place = np.arange(P) // D2, np.arange(P) % D2
    same = head[:, None] == head[None, :]
    o["spread"] = (same[:, None, :] & (place[:, None, None] == np.arange(D2)[None, :, None])).astype(np.float32)
    o["gather"] = (same[:, None, :] & (place[None, None, :] == np.arange(D2)[None, :, None])).astype(np.float32)
    o["blocks"] = np.stack([same, same / np.float32(D2)], axis=1).astype(np.float32)
    return {k: np.ascontiguousarray(x) for k, x in o.items()}


def kernel(**inputs):
    from concourse import bacc
    from concourse.bass_utils import run_bass_kernel_spmd

    nc = bacc.Bacc("TRN2", target_bir_lowering=False, num_devices=1)
    arrays, args = {}, {}
    for name, x in _layout(inputs).items():
        arrays[f"in_{name}"] = x
        args[name] = nc.dram_tensor(f"in_{name}", x.shape, mybir.dt.from_np(x.dtype), kind="ExternalInput").ap()
    args["out"] = nc.dram_tensor("out", (B, P, D), F32, kind="ExternalOutput").ap()
    program(nc, args)
    r = run_bass_kernel_spmd(nc, [arrays], core_ids=[0])
    return r.results[0]["out"]
```

```python
from contextlib import ExitStack

import concourse.bass as bass
from concourse import mybir

F32 = mybir.dt.float32
F32R = mybir.dt.float32r
I32 = mybir.dt.int32
ALU = mybir.AluOpType
ACT = mybir.ActivationFunctionType
AX = mybir.AxisListType

B = 16
P = 128
D = 512
NC = D // P
CI = 64
H1, D1 = 16, 32
NF = 2048 // P
H2, D2 = 32, 16
NM, DM, DD = 5, 32, 64
H3, D3, KV3 = 32, 16, 8
G3 = H3 // KV3
HC = P // D3
NEG = 1.0e30

COLS = [("btheta", 1), ("bphi", 1), ("bg", 1), ("bz", 1), ("bn_gamma", 1), ("bn_beta", 1),
        ("q_b", NC), ("k_b", NC), ("v_b", NC), ("post_w", NC), ("b1", NF),
        ("ln1_w", NC), ("ln1_b", NC), ("ln2_w", NC), ("ln2_b", NC), ("maa_x", NC),
        ("maa_stack", NM * NC), ("decay", NC), ("u", NC), ("ffn_k", NC), ("ffn_r", NC),
        ("gn_w", NC), ("gn_b", NC), ("bq3", NC), ("bk3", 1), ("bv3", 1)]
ROWS = ["bo3", "gamma3", "beta3", "out_b", "b2"]
ROWS1 = 2
NCOLS = sum(n for _, n in COLS)


class Ring:

    def __init__(self, ready, free, banks, per_batch):
        self.ready, self.free, self.banks, self.per_batch = ready, free, banks, per_batch
        assert per_batch % len(banks) == 0
        self.n = 0
        self.base = 0

    def begin(self, i):
        self.base, self.n = i * self.per_batch, 0

    def read(self, i, k):
        return i * self.per_batch + k + len(self.banks)

    def written(self, i, k):
        return i * self.per_batch + k

    def next(self):
        self.bank = self.banks[self.n % len(self.banks)]
        self.n += 1
        self.count = self.base + self.n
        assert self.n <= self.per_batch
        return self.bank


class Steps:

    def __init__(self, per_batch):
        self.per_batch, self.n, self.base = per_batch, 0, 0

    def begin(self, i):
        self.base, self.n = i * self.per_batch, 0

    def tick(self):
        self.n += 1
        assert self.n <= self.per_batch, "more steps than per_batch"
        return 1

    @property
    def now(self):
        return self.base + self.n

    def end(self):
        assert self.n == self.per_batch, f"per_batch should be {self.n}"


def layer0(nc, a, PS, sem, C, cols, rows, rows1, ident, hsum, hsum4, halfs, s_const, s_ident, bn_scale, bn_shift, l0_out,
           weights1, s_w1):
    with ExitStack() as ctx:
        def sb(name, shape, dt=F32):
            return ctx.enter_context(nc.sbuf_tensor(name, shape, dt))

        w0 = sb("w0", [P, 3, CI])
        wz = sb("wz", [P, P])
        xin = sb("x_in", [P, D])
        cin = sb("ctx_in", [P, D])
        theta = sb("theta", [P, D])
        phi = sb("phi", [P, D])
        g = sb("g", [P, NC, CI])
        probs = sb("probs", [P, NC, D])
        probsT = sb("probsT", [P, NC, D])
        nmax = sb("nmax", [P, NC])
        rsum = sb("rsum", [P, NC])
        rinv = sb("rinv", [P, NC])
        y = sb("y", [P, D])
        wy = sb("wy", [P, D])
        stats = sb("stats", [P, B, 6])
        mv = sb("mv", [P, 2])
        bnt = sb("bnt", [P, 2])

        s_w0 = sem("l0_weights_loaded")
        s_in = sem("l0_inputs_loaded")
        s_pad = sem("l0_zero_rows_made")
        s_nmax = sem("l0_max_ready")
        s_rinv = sem("l0_rinv_ready")
        s_norm = sem("l0_probs_ready")
        s_stat = sem("l0_stats_done")
        s_store = sem("l0_wy_stored")
        s_bnv = sem("l0_bn_step")
        s_hsum = sem("l0_shared_constants_loaded")
        rings = dict(tp=([4, 5], 2), g=([6], 1), f=([0, 1], 4), t=([2, 3], 4), o=([7], 2))
        S = {k: (sem(f"l0_{k}_psum_ready"), sem(f"l0_{k}_psum_free")) for k in rings}

        def ring(k):
            return Ring(*S[k], *rings[k])

        with nc.Block() as block:
            @block.sync
            def _(sp):
                G = ring("g")

                def load(i):
                    sp.dma_start(xin[:, :], a["x"][i]).then_inc(s_in, 16)
                    sp.dma_start(cin[:, :], a["ctx"][i]).then_inc(s_in, 16)

                sp.dma_start(w0[:, :, :], a["w0"]).then_inc(s_w0, 16)
                load(0)
                sp.dma_start(cols[:, :], a["cols"]).then_inc(s_const, 16)
                sp.dma_start(wz[:, :], a["wz"]).then_inc(s_w0, 16)
                sp.dma_start(hsum[:, :], a["hsum"]).then_inc(s_hsum, 16)
                sp.dma_start(hsum4[:, :], a["hsum4"]).then_inc(s_hsum, 16)
                sp.dma_start(rows[:, :, :], a["rows"].unsqueeze(0).to_broadcast([P, len(ROWS) - ROWS1, D])).then_inc(s_hsum, 16)
                sp.dma_start(rows1[:, :, :], a["rows1"].unsqueeze(0).to_broadcast([P, ROWS1, D])).then_inc(s_hsum, 16)
                with sp.Fori(1, B) as i:
                    sp.wait_ge(G.ready, G.written(i - 1, 1))
                    load(i)

            @block.gpsimd
            def _(pool):
                nc.gpsimd.memset(ident[:, :], 0.0).then_inc(s_ident, 1)
                nc.gpsimd.memset(halfs[:, :], -0.5).then_inc(s_ident, 1)
                pool.wait_ge(s_ident, 2)
                nc.gpsimd.affine_select(out=ident[:, :], in_=ident[:, :], compare_op=ALU.not_equal, fill=1.0,
                                        base=0, pattern=[[-1, P]], channel_multiplier=1).then_inc(s_ident, 1)
                for t in (theta, phi, y):
                    nc.gpsimd.memset(t[:, :], 0.0).then_inc(s_pad, 1)
                k = 0
                for w, name in zip(weights1, ("q_w", "k_w", "v_w", "out_w", "mlp_w1", "mlp_w2")):
                    for piece in range(w.shape[1] * w.shape[2] // (NC * D)):
                        k += 1
                        pool.wait_ge(s_in, 32 * (k + 1))
                        part = (slice(None), slice(None), slice(piece * D, (piece + 1) * D)) if w.shape[1] == NC else \
                            (slice(None), slice(piece * NC, (piece + 1) * NC))
                        pool.dma_start(w[part], a[name][part]).then_inc(s_w1, 16)
                pool.wait_ge(s_bnv, 2)
                nc.gpsimd.tensor_tensor(bnt[:, 1:2], bnt[:, 0:1], halfs[:, 0:1], ALU.pow).then_inc(s_bnv, 1)
                pool.wait_ge(s_hsum, 64)
                pool.wait_ge(s_w1, 16 * k)

            @block.tensor
            def _(pe):
                for k in rings:
                    pe.sem_inc(S[k][1], len(rings[k][0]))
                pe.sem_inc(s_store, 16)
                TP, G, F, T, O = (ring(k) for k in ("tp", "g", "f", "t", "o"))
                pe.wait_ge(s_w0, 32)
                pe.wait_ge(s_ident, 3)
                pe.wait_ge(s_pad, 3)

                def theta_phi(i):
                    TP.begin(i)
                    pe.wait_ge(s_in, 32 * i + 32)
                    for n, x in ((0, xin), (1, cin)):
                        b = TP.next()
                        pe.wait_ge(TP.free, TP.count)
                        nc.tensor.matmul(PS[b][0:CI, :], w0[:, n, :], x[:, :], start=True, stop=True)\
                            .then_inc(TP.ready, 1)

                def g_proj(i):
                    G.begin(i)
                    b = G.next()
                    pe.wait_ge(G.free, G.count)
                    for j in range(NC):
                        mm = nc.tensor.matmul(PS[b][:, j * CI:(j + 1) * CI], xin[:, j * P:(j + 1) * P], w0[:, 2, :],
                                              start=True, stop=True)
                    mm.then_inc(G.ready, 1)

                def scores(i, chunks):
                    if 0 in chunks:
                        F.begin(i)
                        pe.wait_ge(TP.free, TP.read(i, 2))
                    for c in chunks:
                        b = F.next()
                        pe.wait_ge(F.free, F.count)
                        nc.tensor.matmul(PS[b][:, :], phi[:, c * P:(c + 1) * P], theta[:, :], start=True, stop=True)\
                            .then_inc(F.ready, 1)

                def turn_probs(i, chunks):
                    if 0 in chunks:
                        T.begin(i)
                    for c in chunks:
                        b = T.next()
                        pe.wait_ge(T.free, T.count)
                        pe.wait_ge(s_norm, NC * i + c + 1)
                        for j in range(NC):
                            mm = nc.tensor.transpose(PS[b][:, j * P:(j + 1) * P], probs[:, c, j * P:(j + 1) * P], ident[:, :])
                        mm.then_inc(T.ready, 1)

                def out_y(i):
                    O.begin(i)
                    b = O.next()
                    pe.wait_ge(O.free, O.count)
                    pe.wait_ge(G.free, G.read(i, 1))
                    pe.wait_ge(T.free, T.read(i, NC))
                    for j in range(NC):
                        mm = nc.tensor.matmul(PS[b][0:CI, :], g[:, j, :], probsT[:, j, :], start=(j == 0), stop=(j == NC - 1))
                    mm.then_inc(O.ready, 1)

                def out_z(i):
                    b = O.next()
                    pe.wait_ge(O.free, O.count)
                    pe.wait_ge(O.free, O.read(i, 1))
                    nc.tensor.matmul(PS[b][:, :], wz[:, :], y[:, :], start=True, stop=True).then_inc(O.ready, 1)

                theta_phi(0)
                g_proj(0)
                scores(0, (0, 1, 2, 3))
                with pe.Fori(1, B) as i:
                    turn_probs(i - 1, (0, 1))
                    theta_phi(i)
                    turn_probs(i - 1, (2, 3))
                    g_proj(i)
                    out_y(i - 1)
                    scores(i, (0, 1))
                    out_z(i - 1)
                    scores(i, (2, 3))
                turn_probs(B - 1, (0, 1, 2, 3))
                out_y(B - 1)
                out_z(B - 1)

            @block.scalar
            def _(act):
                TP, G, F, O = (ring(k) for k in ("tp", "g", "f", "o"))
                act.wait_ge(s_const, 16)
                act.wait_ge(s_pad, 3)

                def theta_phi(i):
                    TP.begin(i)
                    for dst, bias in ((theta, "btheta"), (phi, "bphi")):
                        b = TP.next()
                        act.wait_ge(TP.ready, TP.count)
                        nc.scalar.activation(dst[0:CI, :], PS[b][0:CI, :], ACT.Identity, bias=C(bias, 0, CI))\
                            .then_inc(TP.free, 1)

                def copy_g(i):
                    G.begin(i)
                    b = G.next()
                    act.wait_ge(G.ready, G.count)
                    nc.scalar.activation(g[:, :, :], PS[b][:, 0:NC * CI].rearrange("p (j o) -> p j o", j=NC), ACT.Copy)\
                        .then_inc(G.free, 1)

                def exps(i):
                    F.begin(i)
                    for c in range(NC):
                        b = F.next()
                        act.wait_ge(s_nmax, NC * i + c + 1)
                        nc.scalar.activation(probs[:, c, :], PS[b][:, :], ACT.Exp, bias=nmax[:, c:c + 1],
                                             accum_out=rsum[:, c:c + 1]).then_inc(F.free, 1)

                def copy_y(i):
                    O.begin(i)
                    b = O.next()
                    act.wait_ge(O.ready, O.count)
                    nc.scalar.activation(y[0:CI, :], PS[b][0:CI, :], ACT.Identity, bias=C("bg", 0, CI)).then_inc(O.free, 1)

                def copy_z(i):
                    b = O.next()
                    act.wait_ge(O.ready, O.count)
                    act.wait_ge(s_store, 16 * i + 16)
                    if not isinstance(i, int) or i > 0:
                        act.wait_ge(s_stat, i)
                    nc.scalar.activation(wy[:, :], PS[b][:, :], ACT.Identity, bias=C("bz")).then_inc(O.free, 1)
                    act.wait_ge(O.free, O.read(i, 2))
                    act.dma_start(l0_out[i], wy[:, :]).then_inc(s_store, 16)

                theta_phi(0)
                copy_g(0)
                exps(0)
                theta_phi(1)
                copy_y(0)
                copy_g(1)
                exps(1)
                copy_z(0)
                with act.Fori(2, B) as i:
                    theta_phi(i)
                    copy_y(i - 1)
                    copy_g(i)
                    exps(i)
                    copy_z(i - 1)
                copy_y(B - 1)
                copy_z(B - 1)
                act.wait_ge(s_store, 16 * (B + 1))

            @block.vector
            def _(dve):
                F, T, O = ring("f"), ring("t"), ring("o")

                def maxima(i):
                    F.begin(i)
                    for c in range(NC):
                        b = F.next()
                        dve.wait_ge(F.ready, F.count)
                        nc.vector.tensor_reduce(nmax[:, c:c + 1], PS[b][:, :], AX.X, ALU.max, negate=True)\
                            .then_inc(s_nmax, 1)

                def normalise(i):
                    for c in range(NC):
                        dve.wait_ge(F.free, F.read(i, c + 1))
                        nc.vector.reciprocal(rinv[:, c:c + 1], rsum[:, c:c + 1]).then_inc(s_rinv, 1)
                        dve.wait_ge(s_rinv, NC * i + c + 1)
                        nc.vector.tensor_scalar(probs[:, c, :], probs[:, c, :], rinv[:, c:c + 1], None, ALU.mult)\
                            .then_inc(s_norm, 1)

                def copy_probsT(i):
                    T.begin(i)
                    for c in range(NC):
                        b = T.next()
                        dve.wait_ge(T.ready, T.count)
                        nc.vector.tensor_copy(probsT[:, :, c * P:(c + 1) * P],
                                              PS[b][:, :].rearrange("p (j i) -> p j i", j=NC)).then_inc(T.free, 1)

                def statistics(i):
                    dve.wait_ge(O.free, O.read(i, 2))
                    nc.vector.bn_stats(stats[:, i, :], wy[:, :]).then_inc(s_stat, 1)

                maxima(0)
                normalise(0)
                with dve.Fori(1, B) as i:
                    copy_probsT(i - 1)
                    maxima(i)
                    normalise(i)
                    statistics(i - 1)
                copy_probsT(B - 1)
                statistics(B - 1)
                dve.wait_ge(s_stat, B)
                nc.vector.bn_aggr(mv[:, :], stats[:, :, :].rearrange("p b s -> p (b s)")).then_inc(s_bnv, 1)
                dve.wait_ge(s_bnv, 1)
                nc.vector.tensor_scalar(bnt[:, 0:1], mv[:, 1:2], 1e-5, None, ALU.add).then_inc(s_bnv, 1)
                dve.wait_ge(s_bnv, 3)
                nc.vector.tensor_scalar(bn_scale[:, :], bnt[:, 1:2], C("bn_gamma"), None, ALU.mult).then_inc(s_bnv, 1)
                dve.wait_ge(s_bnv, 4)
                nc.vector.tensor_scalar(bn_shift[:, :], mv[:, 0:1], bn_scale[:, :], -1.0, ALU.mult, ALU.mult)\
                    .then_inc(s_bnv, 1)
                dve.wait_ge(s_bnv, 5)
                nc.vector.tensor_scalar(bn_shift[:, :], bn_shift[:, :], C("bn_beta"), None, ALU.add).then_inc(s_bnv, 1)
                dve.wait_ge(s_bnv, 6)


def layer1(nc, a, PS, sem, C, R, cols_of, ident, hsum4, halfs, bn_scale, bn_shift, l0_out, l1_out, weights, early,
           s_early):
    q_w, k_w, v_w, out_w, mlp_w1, mlp_w2 = weights
    NK = 2
    NG = H1 // 2
    HQ = P // D1
    J_SCORE, J_TURN, J_RINV = list(range(1, 9)), [9, 10, 11, 12, 13, 15, 16, 17], [14, 18]

    def pair(g):
        return [2 * g, 2 * g + 1]

    with ExitStack() as ctx:
        def sb(name, shape, dt=F32):
            return ctx.enter_context(nc.sbuf_tensor(name, shape, dt))

        wyin = sb("wy_in", [P, D])
        xin = sb("x_in1", [P, D])
        maski = sb("mask_in", [P, P], I32)
        negm = sb("neg_mask", [P, NK * P])
        lat = sb("latents", [P, D])
        latb = sb("latents_out_b", [P, D])
        latb2n = sb("latents_b2_next", [P, D])
        latb2 = sb("latents_b2", [P, D])
        hT = sb("hT", [P, NC, NK * P])
        qT = sb("qT", [P, NC, P])
        kT = sb("kT", [P, NC, NK * P])
        kbd = [sb(f"k_blocks1_{q}", [P, HQ, NK * P]) for q in range(2)]
        v = sb("v", [P, NK, H1, D1])
        probs = sb("probs1", [P, H1, NK * P])
        probsT = sb("probsT1", [P, NG, 2 * NK, P])
        nmax = sb("nmax1", [P, H1])
        rinv = sb("rinv1", [P, H1])
        rsum = sb("rsum1", [P, H1])
        rrep = sb("rinv1_repeated", [P, H1, D1])
        attn = sb("attn", [P, NC, P])
        rT = attn
        attnT = sb("attnT", [P, NC, P])
        ao = sb("attn_out", [P, D])
        ss = sb("sumsq", [P, 1])
        ms = sb("mean_square", [P, 1])
        rstd = sb("rstd1", [P, 1])
        an = sb("normed", [P, D])
        sq = an
        nT = sb("normedT", [P, NC, P])
        gT = sb("geluT", [P, NF, P])
        xo = sb("l1_x", [P, D])

        s_in = sem("l1_inputs_loaded")
        s_ctx = sem("l1_context_loaded")
        s_mask = sem("l1_mask_loaded")
        s_bn = sem("l1_bn_applied")
        s_lat = sem("l1_latents_ready")
        s_latb = sem("l1_latents_out_b_ready")
        s_latb2n = sem("l1_latents_b2_made")
        s_latb2 = sem("l1_latents_b2_ready")
        s_negm = sem("l1_neg_mask_ready")
        s_exp = sem("l1_exp_ready")
        s_kbd = sem("l1_k_blocks_ready")
        s_rinv = sem("l1_rinv_ready")
        s_rrep = sem("l1_rinv_repeated")
        s_attnT = sem("l1_attention_ready")
        s_ss = sem("l1_sumsq_ready")
        s_ms = sem("l1_mean_square_ready")
        s_rstd = sem("l1_rstd_ready")
        s_an = sem("l1_normed_ready")
        s_ones = sem("l1_ones_made")
        s_store = sem("l1_x_stored")
        s_hold = sem("l1_wait_held")
        rings = dict(d=([0, 1], 2 * NG + 2), a=([2, 3], 6), o=([4], 2), h=([5, 6], NF // 4), m=([7], 2))
        S = {k: (sem(f"l1_{k}_psum_ready"), sem(f"l1_{k}_psum_free")) for k in rings}

        def ring(k):
            return Ring(*S[k], *rings[k])

        with nc.Block() as block:
            @block.sync
            def _(sp):
                A, DR = ring("a"), ring("d")

                def load_x(i):
                    sp.dma_start(wyin[:, :], l0_out[i]).then_inc(s_in, 16)
                    sp.dma_start(xin[:, :], a["x"][i]).then_inc(s_in, 16)

                def load_ctx(i):
                    sp.dma_start(maski[:, :], a["mask1"][i].unsqueeze(0).to_broadcast([P, P])).then_inc(s_mask, 16)
                    sp.dma_start(hT[:, :, 0:P], a["ctxT"][i]).then_inc(s_ctx, 16)

                load_x(0)
                load_ctx(0)
                for t, src in zip(early, (a["maa_w1"], a["maa_w2"][0:P], a["maa_w2"][P:2 * P], a["td_w1"], a["td_w2"],
                                          a["gather"])):
                    sp.dma_start(t, src).then_inc(s_early, 16)
                with sp.Fori(1, B) as i:
                    sp.wait_ge(s_lat, i)
                    load_x(i)
                    sp.wait_ge(s_negm, i)
                    sp.wait_ge(A.free, A.read(i - 1, 6))
                    load_ctx(i)

            @block.gpsimd
            def _(pool):
                M, O, A, DR = (ring(k) for k in "moad")
                nc.gpsimd.memset(negm[:, P:NK * P], 0.0).then_inc(s_ones, 1)

                def latents(i):
                    pool.wait_ge(s_bn, i + 1)
                    nc.gpsimd.tensor_tensor(lat[:, :], lat[:, :], xin[:, :], ALU.add).then_inc(s_lat, 1)

                def latents_b2(i):
                    pool.wait_ge(s_lat, i + 1)
                    if not isinstance(i, int) or i > 0:
                        pool.wait_ge(s_latb2, i)
                    nc.gpsimd.tensor_tensor(latb2n[:, :], lat[:, :], R("b2"), ALU.add).then_inc(s_latb2n, 1)

                def latents_out_b(i):
                    if not isinstance(i, int) or i > 0:
                        pool.wait_ge(O.free, O.read(i - 1, 2))
                    nc.gpsimd.tensor_tensor(latb[:, :], lat[:, :], R("out_b"), ALU.add).then_inc(s_latb, 1)

                def blocks(i, c):
                    if c == 0:
                        pool.wait_ge(A.free, A.read(i, 4))
                    if c >= 2:
                        pool.wait_ge(DR.ready, DR.written(i, J_SCORE[2 * (c - 2) + 1]))
                    nc.gpsimd.tensor_tensor(kbd[c % 2][:, :, :], kT[:, c, :].unsqueeze(1).to_broadcast([P, HQ, NK * P]),
                                            hsum4[:, :].unsqueeze(2).to_broadcast([P, HQ, NK * P]), ALU.mult)\
                        .then_inc(s_kbd, 1)

                def repeat_rinv(i, half):
                    pool.wait_ge(s_rinv, 2 * i + half + 1)
                    pool.sem_inc(s_hold, 1)
                    nc.gpsimd.tensor_copy(rrep[:, 8 * half:8 * half + 8, :],
                                          rinv[:, 8 * half:8 * half + 8].unsqueeze(2).to_broadcast([P, 8, D1]))\
                        .then_inc(s_rrep, 1)

                def batch(i, first=False, last=False):
                    for c in range(NC):
                        blocks(i, c)
                    if not last:
                        latents(i + 1)
                    repeat_rinv(i, 0)
                    repeat_rinv(i, 1)
                    if not first:
                        pool.wait_ge(M.free, M.read(i - 1, 2))
                    pool.wait_ge(s_latb2n, i + 1)
                    pool.sem_inc(s_hold, 1)
                    nc.gpsimd.tensor_copy(latb2[:, :], latb2n[:, :]).then_inc(s_latb2, 1)
                    if not last:
                        latents_b2(i + 1)
                    pool.wait_ge(s_ms, i + 1)
                    nc.gpsimd.tensor_tensor(rstd[:, :], ms[:, :], halfs[:, 0:1], ALU.pow).then_inc(s_rstd, 1)
                    if not last:
                        latents_out_b(i + 1)

                latents(0)
                latents_b2(0)
                latents_out_b(0)
                batch(0, first=True)
                with pool.Fori(1, B - 1) as i:
                    batch(i)
                batch(B - 1, last=True)

            @block.tensor
            def _(pe):
                for k in rings:
                    pe.sem_inc(S[k][1], len(rings[k][0]))
                DR, A, O, H, M = (ring(k) for k in "daohm")
                AL = ring("a")

                def turn_latents(i):
                    AL.begin(i)
                    b = AL.next()
                    pe.wait_ge(AL.free, AL.count)
                    pe.wait_ge(s_lat, i + 1)
                    for c in range(NC):
                        mm = nc.tensor.transpose(PS[b][:, c * P:(c + 1) * P], lat[:, c * P:(c + 1) * P], ident[:, :])
                    mm.then_inc(AL.ready, 1)

                def queries(i):
                    A.begin(i)
                    A.next()
                    b = A.next()
                    pe.wait_ge(A.free, A.count)
                    pe.wait_ge(A.free, A.read(i, 1))
                    for m in range(NC):
                        for c in range(NC):
                            mm = nc.tensor.matmul(PS[b][:, m * P:(m + 1) * P], q_w[:, c, m * P:(m + 1) * P],
                                                  hT[:, c, P:2 * P], start=(c == 0), stop=(c == NC - 1))
                    mm.then_inc(A.ready, 1)

                def keys(i):
                    pe.wait_ge(s_ctx, 16 * i + 16)
                    for half in range(2):
                        b = A.next()
                        pe.wait_ge(A.free, A.count)
                        for e in range(2):
                            m = 2 * half + e
                            for c in range(NC):
                                mm = nc.tensor.matmul(PS[b][:, e * 256:(e + 1) * 256], k_w[:, c, m * P:(m + 1) * P],
                                                      hT[:, c, :], start=(c == 0), stop=(c == NC - 1))
                        mm.then_inc(A.ready, 1)

                def values(i):
                    for n in range(NK):
                        b = A.next()
                        pe.wait_ge(A.free, A.count)
                        for c in range(NC):
                            mm = nc.tensor.matmul(PS[b][:, :], hT[:, c, n * P:(n + 1) * P], v_w[:, c, :],
                                                  start=(c == 0), stop=(c == NC - 1))
                        mm.then_inc(A.ready, 1)

                def scores(i, g):
                    b = DR.next()
                    pe.wait_ge(DR.free, DR.count)
                    c = g // 2
                    pe.wait_ge(s_kbd, NC * i + c + 1)
                    nc.tensor.matmul(PS[b][:, :], qT[:, c, :], kbd[c % 2][:, 2 * (g % 2):2 * (g % 2) + 2, :]
                                     .rearrange("p h k -> p (h k)"), start=True, stop=True).then_inc(DR.ready, 1)

                def turn_probs(i, g):
                    b = DR.next()
                    pe.wait_ge(DR.free, DR.count)
                    pe.wait_ge(s_exp, NG * i + g + 1)
                    for e, h in enumerate(pair(g)):
                        for n in range(NK):
                            o = (e * NK + n) * P
                            mm = nc.tensor.transpose(PS[b][:, o:o + P], probs[:, h, n * P:(n + 1) * P], ident[:, :])
                    mm.then_inc(DR.ready, 1)

                def turn_rinv(i, half):
                    b = DR.next()
                    pe.wait_ge(DR.free, DR.count)
                    pe.wait_ge(s_rrep, 2 * i + half + 1)
                    for c in range(2):
                        mm = nc.tensor.transpose(PS[b][:, c * P:(c + 1) * P],
                                                 rrep[:, 8 * half + 4 * c:8 * half + 4 * c + 4, :].rearrange("p h d -> p (h d)"),
                                                 ident[:, :])
                    mm.then_inc(DR.ready, 1)

                def attend(i, half):
                    if half == 0:
                        O.next()
                        pe.wait_ge(O.free, O.count)
                        pe.wait_ge(A.free, A.read(i, 6))
                    pe.wait_ge(DR.free, DR.read(i, J_TURN[4 * half + 3]))
                    for c in (2 * half, 2 * half + 1):
                        for n in range(NK):
                            for q in range(HQ):
                                h = HQ * c + q
                                mm = nc.tensor.matmul(PS[O.bank][D1 * q:D1 * (q + 1), c * P:(c + 1) * P], v[:, n, h, :],
                                                      probsT[:, h // 2, (h % 2) * NK + n, :],
                                                      start=(n == 0), stop=(n == NK - 1))
                    if half == 1:
                        mm.then_inc(O.ready, 1)

                def project(i):
                    b = O.next()
                    pe.wait_ge(O.free, O.count)
                    pe.wait_ge(s_attnT, i + 1)
                    for c in range(NC):
                        mm = nc.tensor.matmul(PS[b][:, :], attnT[:, c, :], out_w[:, c, :], start=(c == 0), stop=(c == NC - 1))
                    mm.then_inc(O.ready, 1)

                def turn_normed(i):
                    M.begin(i)
                    b = M.next()
                    pe.wait_ge(M.free, M.count)
                    pe.wait_ge(s_an, i + 1)
                    for c in range(NC):
                        mm = nc.tensor.transpose(PS[b][:, c * P:(c + 1) * P], an[:, c * P:(c + 1) * P], ident[:, :])
                    mm.then_inc(M.ready, 1)

                def hidden(i, j):
                    if j == 0:
                        H.begin(i)
                        pe.wait_ge(M.free, M.read(i, 1))
                    b = H.next()
                    pe.wait_ge(H.free, H.count)
                    for f in range(4):
                        m = 4 * j + f
                        for c in range(NC):
                            mm = nc.tensor.matmul(PS[b][:, f * P:(f + 1) * P], mlp_w1[:, c, m * P:(m + 1) * P],
                                                  nT[:, c, :], start=(c == 0), stop=(c == NC - 1))
                    mm.then_inc(H.ready, 1)

                def mlp_out(i, j):
                    if j == 0:
                        b = M.next()
                        pe.wait_ge(M.free, M.count)
                    pe.wait_ge(H.free, H.read(i, j + 1))
                    for f in range(4 * j, 4 * j + 4):
                        mm = nc.tensor.matmul(PS[M.bank][:, :], gT[:, f, :], mlp_w2[:, f, :], start=(f == 0), stop=(f == NF - 1))
                    if j == 3:
                        mm.then_inc(M.ready, 1)

                def batch(i, mlp, last=False):
                    queries(i)
                    keys(i)
                    if mlp:
                        turn_normed(i - 1)
                    values(i)
                    DR.begin(i)
                    O.begin(i)
                    scores(i, 0)
                    scores(i, 1)
                    for j in range(4):
                        if mlp:
                            hidden(i - 1, j)
                        scores(i, 2 + j)
                    if mlp:
                        mlp_out(i - 1, 0)
                    scores(i, 6)
                    scores(i, 7)
                    turn_probs(i, 0)
                    turn_probs(i, 1)
                    if mlp:
                        mlp_out(i - 1, 1)
                    for g in range(2, 6):
                        turn_probs(i, g)
                        if g == 4:
                            turn_rinv(i, 0)
                            attend(i, 0)
                    if mlp:
                        mlp_out(i - 1, 2)
                    turn_probs(i, 6)
                    turn_probs(i, 7)
                    turn_rinv(i, 1)
                    if not last:
                        turn_latents(i + 1)
                    attend(i, 1)
                    if mlp:
                        mlp_out(i - 1, 3)
                    project(i)

                turn_latents(0)
                batch(0, False)
                with pe.Fori(1, B - 1) as i:
                    batch(i, True)
                batch(B - 1, True, last=True)
                turn_normed(B - 1)
                for j in range(4):
                    hidden(B - 1, j)
                for j in range(4):
                    mlp_out(B - 1, j)

            @block.scalar
            def _(act):
                DR, A, O, H, M = (ring(k) for k in "daohm")
                AL = ring("a")
                act.wait_ge(s_ones, 1)

                def batch_norm(i, first=False):
                    act.wait_ge(s_in, 32 * i + 32)
                    if not first:
                        act.wait_ge(s_latb2n, i)
                        act.wait_ge(s_latb, i)
                        act.wait_ge(A.free, A.read(i - 1, 1))
                    nc.scalar.activation(lat[:, :], wyin[:, :], ACT.Identity, bias=bn_shift[:, :], scale=bn_scale[:, :])\
                        .then_inc(s_bn, 1)

                def copy_latents(i):
                    AL.begin(i)
                    b = AL.next()
                    act.wait_ge(AL.ready, AL.count)
                    nc.scalar.activation(hT[:, :, P:2 * P], PS[b][:, :].rearrange("p (c t) -> p c t", c=NC), ACT.Copy)\
                        .then_inc(AL.free, 1)

                def copy_q(i):
                    A.begin(i)
                    A.next()
                    b = A.next()
                    act.wait_ge(A.ready, A.count)
                    for c in range(NC):
                        ac = nc.scalar.activation(qT[:, c, :], PS[b][:, c * P:(c + 1) * P], ACT.Identity, bias=C("q_b", c))
                    ac.then_inc(A.free, 1)

                def copy_k(i):
                    for half in range(2):
                        b = A.next()
                        act.wait_ge(A.ready, A.count)
                        for e in range(2):
                            c = 2 * half + e
                            ac = nc.scalar.activation(kT[:, c, :], PS[b][:, e * 256:(e + 1) * 256], ACT.Identity,
                                                      bias=C("k_b", c))
                        ac.then_inc(A.free, 1)

                def copy_v(i):
                    for n in range(NK):
                        b = A.next()
                        act.wait_ge(A.ready, A.count)
                        nc.scalar.activation(v[:, n, :, :], PS[b][:, :].rearrange("p (h d) -> p h d", h=H1), ACT.Copy)\
                            .then_inc(A.free, 1)

                def gelu(i, j):
                    if j == 0:
                        H.begin(i)
                    b = H.next()
                    act.wait_ge(H.ready, H.count)
                    for f in range(4):
                        ac = nc.scalar.activation(gT[:, 4 * j + f, :], PS[b][:, f * P:(f + 1) * P], ACT.Gelu_apprx_tanh,
                                                  bias=C("b1", 4 * j + f))
                    ac.then_inc(H.free, 1)

                def exps(i, g):
                    act.wait_ge(DR.free, DR.read(i, J_SCORE[g]))
                    for h in pair(g):
                        ac = nc.scalar.activation(probs[:, h, :], probs[:, h, :], ACT.Exp, bias=nmax[:, h:h + 1],
                                                  scale=-1.0, accum_out=rsum[:, h:h + 1])
                    ac.then_inc(s_exp, 1)

                def squares(i):
                    act.wait_ge(O.free, O.read(i, 2))
                    nc.scalar.activation(sq[:, :], ao[:, :], ACT.Square, accum_out=ss[:, :]).then_inc(s_ss, 1)

                def store(i):
                    act.wait_ge(M.free, M.read(i, 2))
                    act.dma_start(l1_out[i], xo[:, :]).then_inc(s_store, 16)

                def batch(i, mlp, last=False):
                    copy_q(i)
                    copy_k(i)
                    copy_v(i)
                    if not last:
                        batch_norm(i + 1)
                    if mlp:
                        for j in range(4):
                            gelu(i - 1, j)
                    for g in range(NG):
                        exps(i, g)
                    if not last:
                        copy_latents(i + 1)
                    squares(i)
                    if mlp:
                        store(i - 1)

                batch_norm(0, True)
                copy_latents(0)
                batch(0, False)
                with act.Fori(1, B - 1) as i:
                    batch(i, True)
                batch(B - 1, True, last=True)
                for j in range(4):
                    gelu(B - 1, j)
                store(B - 1)
                act.wait_ge(s_store, 16 * (B + 1))

            @block.vector
            def _(dve):
                DR, O, M = (ring(k) for k in "dom")
                dve.wait_ge(s_ones, 1)

                def mask(i):
                    dve.wait_ge(s_mask, 16 * i + 16)
                    nc.vector.tensor_scalar(negm[:, 0:P], maski[:, :], 0.0, -NEG, ALU.is_equal, ALU.mult)\
                        .then_inc(s_negm, 1)
                    dve.wait_ge(s_negm, i + 1)

                def maxima(i, g):
                    b = DR.next()
                    dve.wait_ge(DR.ready, DR.count)
                    dve.sem_inc(s_hold, 1)
                    for e, h in enumerate(pair(g)):
                        mx = nc.vector.tensor_tensor_reduce(probs[:, h, :], PS[b][:, e * 256:(e + 1) * 256], negm[:, :],
                                                            -1.0 / D1, 3.0e38, ALU.add, ALU.min, nmax[:, h:h + 1])
                    mx.then_inc(DR.free, 1)

                def copy_probsT(i, g):
                    b = DR.next()
                    dve.wait_ge(DR.ready, DR.count)
                    nc.vector.tensor_copy(probsT[:, g, :, :], PS[b][:, :].rearrange("p (n q) -> p n q", q=P))\
                        .then_inc(DR.free, 1)

                def reciprocals(i, half):
                    dve.wait_ge(s_exp, NG * i + 4 * half + 4)
                    r = slice(8 * half, 8 * half + 8)
                    nc.vector.reciprocal(rinv[:, r], rsum[:, r]).then_inc(s_rinv, 1)

                def copy_rinvT(i, half):
                    b = DR.next()
                    dve.wait_ge(DR.ready, DR.count)
                    nc.vector.tensor_copy(rT[:, 2 * half:2 * half + 2, :],
                                          PS[b][:, 0:2 * P].rearrange("p (c t) -> p c t", c=2)).then_inc(DR.free, 1)

                def normalise(i):
                    b = O.next()
                    dve.wait_ge(O.ready, O.count)
                    dve.wait_ge(DR.free, DR.read(i, J_RINV[1]))
                    nc.vector.tensor_tensor(attn[:, :, :], PS[b][:, :].rearrange("p (c t) -> p c t", c=NC), rT[:, :, :],
                                            ALU.mult).then_inc(O.free, 1)
                    dve.wait_ge(O.free, O.read(i, 1))
                    nc.vector.tensor_tensor(attnT[:, :, :], attn[:, :, :],
                                            cols_of("v_b").unsqueeze(2).to_broadcast([P, NC, P]), ALU.add)\
                        .then_inc(s_attnT, 1)

                def residual(i):
                    b = O.next()
                    dve.wait_ge(O.ready, O.count)
                    dve.wait_ge(s_latb, i + 1)
                    nc.vector.tensor_tensor(ao[:, :], PS[b][:, :], latb[:, :], ALU.add).then_inc(O.free, 1)

                def rms_norm(i):
                    dve.wait_ge(s_ss, i + 1)
                    nc.vector.tensor_scalar(ms[:, :], ss[:, :], 1.0 / D, 1e-6, ALU.mult, ALU.add).then_inc(s_ms, 1)
                    dve.wait_ge(s_rstd, i + 1)
                    nc.vector.tensor_scalar(an[:, :], ao[:, :], rstd[:, :], None, ALU.mult).then_inc(s_an, 1)

                def copy_normed(i):
                    M.begin(i)
                    b = M.next()
                    dve.wait_ge(M.ready, M.count)
                    nc.vector.tensor_tensor(nT[:, :, :], PS[b][:, :].rearrange("p (c t) -> p c t", c=NC),
                                            cols_of("post_w").unsqueeze(2).to_broadcast([P, NC, P]), ALU.mult)\
                        .then_inc(M.free, 1)

                def output(i):
                    b = M.next()
                    dve.wait_ge(M.ready, M.count)
                    dve.wait_ge(s_latb2, i + 1)
                    dve.wait_ge(s_store, 16 * i + 16)
                    nc.vector.tensor_tensor(xo[:, :], PS[b][:, :], latb2[:, :], ALU.add).then_inc(M.free, 1)

                def batch(i, mlp):
                    mask(i)
                    if mlp:
                        copy_normed(i - 1)
                    DR.begin(i)
                    O.begin(i)
                    for g in range(NG):
                        maxima(i, g)
                    for g in range(NG):
                        if g in (3, 6):
                            reciprocals(i, g // 6)
                        copy_probsT(i, g)
                        if g in (4, 7):
                            copy_rinvT(i, g // 7)
                    normalise(i)
                    if mlp:
                        output(i - 1)
                    residual(i)
                    rms_norm(i)

                dve.sem_inc(s_store, 16)
                batch(0, False)
                with dve.Fori(1, B) as i:
                    batch(i, True)
                copy_normed(B - 1)
                output(B - 1)


def layers23(nc, a, PS, sem, C, R, CS, ident, hsum, halfs, l1_out, early, s_early):
    JS = D2
    JQ = JS // 4
    JO = [JQ * q + e for e in range(JQ) for q in range(4)]
    LAG = 4
    GO = [0, 2, 4, 6, 1, 3, 5, 7]
    V2 = 2 * D3

    with ExitStack() as ctx:
        def sb(name, shape, dt=F32):
            return ctx.enter_context(nc.sbuf_tensor(name, shape, dt))

        def flat(t):
            return t[:, :, :].rearrange("p c t -> p (c t)")

        maa_w1, maa_w2, maa_w2b, td_w1, td_w2, gather = early
        W = {n: sb(n, [P, NC, D]) for n in ("Wk", "Wv", "Wr", "Wg", "Wo", "Wfk", "Wfr", "Wfv", "Wq3", "Wo3")}
        Wk3 = sb("Wk3", [P, NC, KV3 * D3])
        Wv3 = sb("Wv3", [P, NC, KV3 * D3])
        spread = sb("spread", [P, JS, P], F32R)
        blocks = sb("head_blocks", [P, 2, P])
        x = sb("x_in2", [P, D])
        row1 = sb("state_row1", [P, NC])
        st6 = sb("ln1_stats", [P, 6])
        mv = sb("ln1_mean_var", [P, 2])
        ve = sb("ln1_var_eps", [P, 1])
        rstd = sb("ln1_rstd", [P, 1])
        nx = sb("ln1_x", [P, D])
        xaT = sb("xaT", [P, NC, P + 1])
        sx = sb("shifted", [P, NC, P])
        z = sb("z", [P, NC, P])
        t5 = sb("t5", [P, NM - 1, P])
        t5b = sb("t5b", [P, P])
        xm = [sb(f"xm{f}", [P, NC, P]) for f in range(NM)]
        u1 = sb("u1", [P, P])
        kT = sb("kT2", [P, NC, P])
        rT = sb("rT2", [P, NC, P])
        vT = sb("vT2", [P, NC, P])
        vH = sb("v_rounded", [P, NC, P], F32R)
        vL = sb("v_rest", [P, NC, P], F32R)
        wS = sb("w_shifted", [P, NC, P])
        ruk = xm[0]
        g = sb("g2", [P, NC, P])
        eps5 = sb("eps5", [P, 1])
        xres = sb("x_res2", [P, D])
        s0 = sb("state0", [P, NC, D2])
        row0 = sb("state_row0", [P, NC])
        bonus = sb("bonus", [P, NC, P])
        kv = [sb(f"kv{q}", [P, NC, P]) for q in range(3)]
        state = [sb(f"states{q}", [P, NC, P]) for q in range(2)]
        rs = [sb(f"r_states{q}", [P, NC, P]) for q in range(4)]
        xcT = sb("xcT", [P, NC, P + 1])
        x1 = sb("x1", [P, D])
        st6b = sb("ln2_stats", [P, 6])
        mvb = sb("ln2_mean_var", [P, 2])
        veb = sb("ln2_var_eps", [P, 1])
        rstdb = sb("ln2_rstd", [P, 1])
        x3 = sb("x3", [P, D])
        og, dev, sq, gstd, grstd = state[0], state[1], kv[0], kv[1], kv[2]
        gated = rs[0]
        nx2 = flat(rs[1])
        sx2, xk2, xr2, kk, sig = kv[0], kv[1], state[0], state[1], flat(bonus)
        ctxT = sb("ctxT3", [P, NC, P])
        mask = sb("mask3", [P, P])
        x3T = sb("x3T", [P, NC, P])
        x3b = sb("x3_bo", [P, D])
        qT = sb("qT3", [P, G3, P])
        bq = sb("bq3_scaled", [P, G3])
        kS = sb("kT3", [P, P])
        kbd = sb("k_blocks", [P, KV3, P])
        v3 = sb("v3", [P, KV3 // 2, 2, V2])
        sc = [sb(f"scores{q}", [P, G3, P]) for q in range(3)]
        scT = [sb(f"probsT3_{q}", [P, G3, P]) for q in range(2)]
        nmax = sb("nmax3", [P, KV3, G3])
        rsum = sb("rsum3", [P, KV3, G3])
        rinv = sb("rinv3", [P, KV3, G3])
        rrep = sb("rinv3_repeated", [P, G3, KV3, D3])
        attn = sc[2]
        attnT = x3T
        y = rrep[:, :, :, :].rearrange("p a b d -> p (a b d)")
        lst6 = sb("ln3_stats", [P, 6])
        lmv = sb("ln3_mean_var", [P, 2])
        lve = sb("ln3_var_eps", [P, 1])
        lrstd = sb("ln3_rstd", [P, 1])
        out = sb("out3", [P, D])

        s_w2 = sem("p_weights_loaded")
        s_w3 = sem("w_weights_loaded")
        s_spread = sem("w_spread_loaded")
        s_w4 = sem("a_weights_loaded")
        s_zero = sem("l23_zeros_made")
        s_inP = sem("p_inputs_loaded")
        s_inW = sem("w_inputs_loaded")
        s_inA = sem("a_inputs_loaded")
        s_hold = sem("l23_wait_held")
        s_dveN, s_dveW, s_dveA = sem("n_dve_step"), sem("w_dve_step"), sem("a_dve_step")
        s_var1 = sem("p_ln1_var_ready")
        s_rstd1 = sem("p_ln1_rstd_ready")
        s_nx1 = sem("p_ln1_ready")
        s_first1 = sem("p_first_row1_ready")
        s_z = sem("p_z_ready")
        s_mixed = sem("p_mix_times_difference_ready")
        s_xm = sem("p_mix_ready")
        s_wS = sem("p_decay_ready")
        s_gate = sem("p_silu_ready")
        s_vL = sem("p_v_rest_ready")
        s_ruk = sem("p_ruk_ready")
        s_scan = sem("w_states_ready")
        s_prod = sem("w_r_states_ready")
        s_sum = sem("w_sums_done")
        s_og = sem("w_outputs_read")
        s_sq = sem("w_gn_squares_ready")
        s_grstd = sem("w_gn_rstd_ready")
        s_scaled = sem("w_gn_scaled")
        s_gnorm = sem("w_gn_normed")
        s_gated = sem("w_gated_ready")
        s_var2 = sem("w_ln2_var_ready")
        s_rstd2 = sem("w_ln2_rstd_ready")
        s_nx2 = sem("w_ln2_ready")
        s_first2 = sem("w_first_row0_ready")
        s_xk2 = sem("w_ffn_k_ready")
        s_xr2 = sem("w_ffn_r_ready")
        s_kk = sem("w_ffn_kk_ready")
        s_x3 = sem("w_x_ready")
        s_x3b = sem("a_x_bo_ready")
        s_kbd = sem("a_k_blocks_ready")
        s_bq = sem("a_query_bias_scaled")
        s_exp = sem("a_exp_ready")
        s_av = sem("a_values_weighted")
        s_rinv = sem("a_rinv_ready")
        s_rrep = sem("a_rinv_repeated")
        s_attn = sem("a_attention_ready")
        s_attnT = sem("a_attention_bias_added")
        s_var3 = sem("a_ln_var_ready")
        s_rstd3 = sem("a_ln_rstd_ready")
        s_out = sem("a_out_ready")
        s_store = sem("out_stored")
        OSUM, OAV = 2, 7
        rings = dict(pd=([3], NM), pa=([4], 8), w=([0, 1], JS + 8), ad=([5], KV3 + 1), aa=([6], 4 + KV3))
        S = {k: (sem(f"{k}_psum_ready"), sem(f"{k}_psum_free")) for k in rings}
        J_XA, J_T5, J_U1, J_Z, J_K, J_R, J_V, J_G = range(1, 9)
        J_BONUS, J_MEAN = 1, JS + 2
        J_GVAR, J_WO, J_XC, J_FK, J_FR, J_FV = (J_MEAN + k for k in range(1, 7))
        J3_KV, J3_X, J3_Q, J3_RINV = 1, 2, 3, 4 + KV3
        J3_WO = KV3 + 1

        def ring(k):
            return Ring(*S[k], *rings[k])

        beside = {0: [("a_kv",)], 2: [("p_t5",), ("a_x",)], 3: [("b_res",)], 4: [("a_q",), ("b_rstd",)], 5:
                  [("b_ln",)], 6: [("p_mix", 0), ("b_store",)], 7: [("a_score", 0), ("p_mix", 1)], 9:
                  [("a_score", 1), ("a_exp", 0)], 10: [("a_turn", 0)], 11: [("p_mix", 2), ("a_score", 2),
                  ("a_exp", 1)], 12: [("p_mix", 3), ("a_turn", 1)], 13: [("a_score", 3), ("a_exp", 2),
                  ("p_mix", 4)], 14: [("a_turn", 2), ("a_value", 1)], 15: [("a_score", 4), ("a_exp", 3)], 16:
                  [("a_turn", 3)], 17: [("a_value", 3), ("a_exp", 4)], 18: [("a_turn", 4)]}
        ORDER = [("w_bonus",), ("b_out",)]
        for j in range(JS + LAG):
            ORDER += [("w_step", j)] + beside.get(j, [])
        ORDER += [("p_u1",), ("w_og",), ("w_mean",), ("a_score", 5), ("p_w",), ("w_var",), ("a_exp", 5),
                  ("a_score", 6), ("p_k",), ("w_scale",), ("w_gnorm",), ("w_gate",), ("a_exp", 6), ("a_turn", 5),
                  ("p_r",), ("a_score", 7), ("a_exp", 7), ("p_ruk",), ("w_out",), ("a_value", 5), ("a_turn", 6),
                  ("p_v",), ("w_ln2",), ("w_xc",), ("p_split",), ("a_turn", 7), ("p_g",), ("n_ln1",), ("a_rinv",),
                  ("p_gate",), ("n_nx",), ("a_value", 7), ("w_fk",), ("a_norm",), ("n_xa",), ("n_shift",),
                  ("w_fr",), ("w_fv",)]

        def steps(eng, segments, begin):
            stages = "npwab"
            last = len(stages) - 1

            def step(*index):
                index = dict(zip(stages, index))
                for stage in stages:
                    if index[stage] is not None:
                        begin(stage, index[stage])
                for name, *k in ORDER:
                    if index[name[0]] is not None and name in segments:
                        segments[name](index[name[0]], *k)

            for i in range(last):
                step(*(i - k if i >= k else None for k in range(last + 1)))
            with eng.Fori(last, B) as i:
                step(i, *(i - k for k in range(1, last + 1)))
            for i in range(B, B + last):
                step(*(i - k if i - k < B else None for k in range(last + 1)))

        with nc.Block() as block:
            @block.sync
            def _(sp):
                AD = ring("ad")

                def load_p(i):
                    sp.dma_start(x[:, :], l1_out[i]).then_inc(s_inP, 16)
                    sp.dma_start(row1[:, :], a["row1"][i]).then_inc(s_inP, 16)

                def load_w(i):
                    sp.dma_start(s0[:, :, :], a["state"][i]).then_inc(s_inW, 16)
                    sp.dma_start(xres[:, :], l1_out[i]).then_inc(s_inW, 16)
                    sp.dma_start(row0[:, :], a["row0"][i]).then_inc(s_inW, 16)

                def load_a(i):
                    sp.dma_start(ctxT[:, :, :], a["ctxT"][i]).then_inc(s_inA, 16)
                    sp.dma_start(mask[:, :], a["mask3"][i]).then_inc(s_inA, 16)

                def reload_p(i):
                    sp.wait_ge(s_nx1, i)
                    sp.wait_ge(s_first1, i)
                    load_p(i)

                def reload_w(i):
                    sp.wait_ge(s_scan, JS * i)
                    sp.wait_ge(s_var2, i)
                    sp.wait_ge(s_first2, i)
                    load_w(i)

                def reload_a(i):
                    sp.wait_ge(AD.free, AD.read(i - 1, KV3))
                    load_a(i)

                load_p(0)
                for n in ("Wk", "Wr", "Wv", "Wg"):
                    sp.dma_start(W[n][:, :, :], a[n]).then_inc(s_w2, 16)
                load_w(0)
                reload_p(1)
                sp.dma_start(blocks[:, :, :], a["blocks"]).then_inc(s_w3, 16)
                for n in ("Wo", "Wfk", "Wfr", "Wfv"):
                    sp.dma_start(W[n][:, :, :], a[n]).then_inc(s_w3, 16)
                for t, n in ((W["Wq3"], "Wq3"), (Wk3, "Wk3"), (Wv3, "Wv3"), (W["Wo3"], "Wo3")):
                    sp.dma_start(t[:, :, :], a[n]).then_inc(s_w4, 16)
                load_a(0)
                reload_w(1)
                with sp.Fori(2, B) as i:
                    reload_p(i)
                    reload_a(i - 1)
                    reload_w(i)
                reload_a(B - 1)

            @block.gpsimd
            def _(pool):
                PD, AD, AA = ring("pd"), ring("ad"), ring("aa")
                pool.dma_start(spread[:, :, :], a["spread"]).then_inc(s_spread, 16)
                for t in (t5[:, :, :], t5b[:, :], u1[:, :], wS[:, :, 0:1], v3[:, :, :, :]):
                    nc.gpsimd.memset(t, 0.0).then_inc(s_zero, 1)
                nc.gpsimd.memset(eps5[:, :], 1e-5).then_inc(s_zero, 1)

                def power(dst, src):
                    return nc.gpsimd.tensor_tensor(dst, src, halfs[:, 0:1], ALU.pow)

                def n_ln1(i):
                    pool.wait_ge(s_inP, 32 * i + 32)
                    if not isinstance(i, int) or i > 0:
                        pool.wait_ge(s_z, i)
                    pool.sem_inc(s_hold, 1)
                    nc.gpsimd.tensor_copy(xaT[:, :, 0], row1[:, :]).then_inc(s_first1, 1)
                    pool.wait_ge(s_var1, i + 1)
                    power(rstd[:, :], ve[:, :]).then_inc(s_rstd1, 1)

                def p_mix(i, f):
                    pool.wait_ge(s_mixed, NM * i + f + 1)
                    nc.gpsimd.tensor_tensor(xm[f][:, :, :], xm[f][:, :, :], xaT[:, :, 1:P + 1], ALU.add)\
                        .then_inc(s_xm, 1)

                def w_step(i, j):
                    if not 1 <= j <= JS:
                        return
                    j -= 1
                    pool.wait_ge(s_scan, JS * i + j + 1)
                    if j >= 4:
                        pool.wait_ge(s_sum, JS // 2 * i + (j - 4) // 2 + 1)
                    nc.gpsimd.tensor_tensor(rs[j % 4][:, :, :], state[j % 2][:, :, :], rT[:, :, :], ALU.mult)\
                        .then_inc(s_prod, 1)

                def w_out(i):
                    pool.wait_ge(s_inW, 48 * i + 48)
                    pool.sem_inc(s_hold, 1)
                    nc.gpsimd.tensor_copy(xcT[:, :, 0], row0[:, :]).then_inc(s_first2, 1)
                    pool.wait_ge(s_var2, i + 1)
                    power(rstdb[:, :], veb[:, :]).then_inc(s_rstd2, 1)

                def a_x(i):
                    pool.wait_ge(s_x3, i + 1)
                    if not isinstance(i, int) or i > 0:
                        pool.wait_ge(AD.free, AD.read(i - 1, J3_WO))
                    nc.gpsimd.tensor_tensor(x3b[:, :], x3[:, :], R("bo3"), ALU.add).then_inc(s_x3b, 1)

                def a_kv(i):
                    pool.wait_ge(AA.free, AA.read(i, J3_KV))
                    nc.gpsimd.tensor_tensor(kbd[:, :, :], kS[:, :].unsqueeze(1).to_broadcast([P, KV3, P]),
                                            hsum[:, :].unsqueeze(2).to_broadcast([P, KV3, P]), ALU.mult)\
                        .then_inc(s_kbd, 1)

                def a_norm(i):
                    pool.wait_ge(s_rinv, i + 1)
                    pool.sem_inc(s_hold, 1)
                    nc.gpsimd.tensor_copy(rrep[:, :, :, :], rinv[:, :, :].rearrange("p g c -> p c g").unsqueeze(3)
                                          .to_broadcast([P, G3, KV3, D3])).then_inc(s_rrep, 1)

                def b_rstd(i):
                    pool.wait_ge(s_var3, i + 1)
                    power(lrstd[:, :], lve[:, :]).then_inc(s_rstd3, 1)

                steps(pool, dict(n_ln1=n_ln1, p_mix=p_mix, w_step=w_step, w_out=w_out, a_x=a_x,
                                 a_kv=a_kv, a_norm=a_norm, b_rstd=b_rstd), lambda stage, i: None)

            @block.tensor
            def _(pe):
                for k in rings:
                    pe.sem_inc(S[k][1], len(rings[k][0]))
                pe.sem_inc(s_og, 1)
                pe.sem_inc(s_attn, 1)
                PD, PA, WR, AD, AA, BD, NA = (ring(k) for k in ("pd", "pa", "w", "ad", "aa", "ad", "pa"))

                def begin(stage, i):
                    for r in dict(n=(NA,), p=(PD, PA), w=(WR,), a=(AD, AA), b=(BD,))[stage]:
                        r.begin(i)
                    PA.n = 1
                    if stage == "p" and isinstance(i, int) and i == 0:
                        pe.wait_ge(s_early, 16 * 6)
                    BD.n = KV3
                    if stage == "w" and isinstance(i, int) and i == 0:
                        pe.wait_ge(s_w3, 16 * 5)
                        pe.wait_ge(s_spread, 16)
                    if stage == "a" and isinstance(i, int) and i == 0:
                        pe.wait_ge(s_w4, 16 * 4)

                def turn4(r, src):
                    b = r.next()
                    pe.wait_ge(r.free, r.count)
                    for c in range(NC):
                        mm = nc.tensor.transpose(PS[b][:, c * P:(c + 1) * P], src[:, c * P:(c + 1) * P], ident[:, :])
                    mm.then_inc(r.ready, 1)

                def channel_major(r, w, xT):
                    b = r.next()
                    pe.wait_ge(r.free, r.count)
                    for m in range(NC):
                        for c in range(NC):
                            mm = nc.tensor.matmul(PS[b][:, m * P:(m + 1) * P], w[:, c, m * P:(m + 1) * P], xT[:, c, :],
                                                  start=(c == 0), stop=(c == NC - 1))
                    mm.then_inc(r.ready, 1)

                def token_major(r, w, xT):
                    b = r.next()
                    pe.wait_ge(r.free, r.count)
                    for c in range(NC):
                        mm = nc.tensor.matmul(PS[b][:, :], xT[:, c, :], w[:, c, :], start=(c == 0), stop=(c == NC - 1))
                    mm.then_inc(r.ready, 1)

                def over_head(r, k, src):
                    b = r.next()
                    pe.wait_ge(r.free, r.count)
                    nc.tensor.matmul(PS[b][:, :], blocks[:, k, :], flat(src), start=True, stop=True).then_inc(r.ready, 1)

                def n_xa(i):
                    pe.wait_ge(s_nx1, i + 1)
                    turn4(NA, nx)

                def p_t5(i):
                    b = PA.next()
                    pe.wait_ge(PA.free, PA.count)
                    pe.wait_ge(s_z, i + 1)
                    for c in range(NC):
                        nc.tensor.matmul(PS[b][:, 0:P], maa_w1[:, c, 0:P], z[:, c, :], start=(c == 0), stop=(c == NC - 1))
                    for c in range(NC):
                        mm = nc.tensor.matmul(PS[b][0:DM, P:2 * P], maa_w1[:, c, P:P + DM], z[:, c, :],
                                              start=(c == 0), stop=(c == NC - 1))
                    mm.then_inc(PA.ready, 1)

                def p_mix(i, f):
                    b = PD.next()
                    pe.wait_ge(PD.free, PD.count)
                    if f == 0:
                        pe.wait_ge(PA.free, PA.read(i, J_T5))
                    w, t = (maa_w2, t5[:, f, :]) if f < NM - 1 else (maa_w2b, t5b[:, :])
                    for m in range(NC):
                        mm = nc.tensor.matmul(PS[b][:, m * P:(m + 1) * P], w[:, m * P:(m + 1) * P], t, start=True, stop=True)
                    mm.then_inc(PD.ready, 1)

                def p_u1(i):
                    b = PA.next()
                    pe.wait_ge(PA.free, PA.count)
                    pe.wait_ge(s_xm, NM * i + 2)
                    for c in range(NC):
                        mm = nc.tensor.matmul(PS[b][0:DD, 0:P], td_w1[:, c, :], xm[1][:, c, :], start=(c == 0), stop=(c == NC - 1))
                    mm.then_inc(PA.ready, 1)

                def p_w(i):
                    b = PA.next()
                    pe.wait_ge(PA.free, PA.count)
                    pe.wait_ge(PA.free, PA.read(i, J_U1))
                    for m in range(NC):
                        mm = nc.tensor.matmul(PS[b][:, m * P:(m + 1) * P], td_w2[:, m * P:(m + 1) * P], u1[:, :], start=True, stop=True)
                    mm.then_inc(PA.ready, 1)

                def projected(f, w):
                    def seg(i):
                        if isinstance(i, int) and i == 0:
                            pe.wait_ge(s_w2, 16 * 4)
                        pe.wait_ge(s_xm, NM * i + f + 1)
                        channel_major(PA, W[w], xm[f])
                    return seg

                def w_bonus(i):
                    pe.wait_ge(s_ruk, i + 1)
                    over_head(WR, 0, ruk)

                def w_step(i, j):
                    if j < JS:
                        b = WR.next()
                        pe.wait_ge(WR.free, WR.count)
                        if j == 0:
                            pe.wait_ge(s_vL, i + 1)
                        nc.tensor.matmul(PS[b][:, :], spread[:, JO[j], :], flat(vH), start=True, stop=False)
                        nc.tensor.matmul(PS[b][:, :], spread[:, JO[j], :], flat(vL), start=False, stop=True).then_inc(WR.ready, 1)
                    if j >= LAG and (j - LAG) % 2:
                        j -= LAG
                        if j == 1:
                            pe.wait_ge(s_og, i + 1)
                        pe.wait_ge(s_prod, JS * i + j + 1)
                        for k in (j - 1, j):
                            q, e = JO[k] // JQ, JO[k] % JQ
                            mm = nc.tensor.matmul(PS[OSUM][JQ * HC * q:JQ * HC * (q + 1), :], gather[:, e, :], flat(rs[k % 4]),
                                                  start=(e == 0), stop=(e == JQ - 1))
                        mm.then_inc(s_sum, 1)

                def w_mean(i):
                    pe.wait_ge(s_og, i + 2)
                    over_head(WR, 1, og)

                def w_var(i):
                    pe.wait_ge(s_sq, i + 1)
                    over_head(WR, 1, sq)

                def w_out(i):
                    pe.wait_ge(s_gated, i + 1)
                    token_major(WR, W["Wo"], gated)

                def w_xc(i):
                    pe.wait_ge(s_nx2, i + 1)
                    turn4(WR, nx2)

                def w_fk(i):
                    pe.wait_ge(s_xk2, i + 1)
                    channel_major(WR, W["Wfk"], xk2)

                def w_fr(i):
                    pe.wait_ge(s_xr2, i + 1)
                    token_major(WR, W["Wfr"], xr2)

                def w_fv(i):
                    pe.wait_ge(s_kk, i + 1)
                    token_major(WR, W["Wfv"], kk)

                def a_x(i):
                    pe.wait_ge(s_x3, i + 1)
                    turn4(AA, x3)

                def a_q(i):
                    pe.wait_ge(AA.free, AA.read(i, J3_X))
                    channel_major(AA, W["Wq3"], x3T)

                def a_kv(i):
                    b = AA.next()
                    pe.wait_ge(AA.free, AA.count)
                    pe.wait_ge(s_inA, 32 * i + 32)
                    for c in range(NC):
                        nc.tensor.matmul(PS[b][:, 0:P], Wk3[:, c, :], ctxT[:, c, :], start=(c == 0), stop=(c == NC - 1))
                    for c in range(NC):
                        mm = nc.tensor.matmul(PS[b][:, P:2 * P], ctxT[:, c, :], Wv3[:, c, :], start=(c == 0), stop=(c == NC - 1))
                    mm.then_inc(AA.ready, 1)

                def a_score(i, u):
                    b = AD.next()
                    pe.wait_ge(AD.free, AD.count)
                    if u == 0:
                        pe.wait_ge(s_kbd, i + 1)
                        pe.wait_ge(AA.free, AA.read(i, J3_Q))
                    for c in range(G3):
                        mm = nc.tensor.matmul(PS[b][:, c * P:(c + 1) * P], qT[:, c, :], kbd[:, GO[u], :], start=True, stop=True)
                    mm.then_inc(AD.ready, 1)

                def a_turn(i, u):
                    pe.wait_ge(s_exp, KV3 * i + u + 1)
                    turn4(AA, flat(sc[u % 3]))

                def a_value(i, u):
                    if u == 1:
                        pe.wait_ge(s_attn, i + 1)
                    pe.wait_ge(AA.free, AA.read(i, J3_Q + 1 + u))
                    for k in (u - 1, u):
                        m, e = GO[k] // 2, GO[k] % 2
                        mm = nc.tensor.matmul(PS[OAV][V2 * m:V2 * (m + 1), :], v3[:, m, e, :], flat(scT[k % 2]),
                                              start=(e == 0), stop=(e == 1))
                    mm.then_inc(s_av, 1)

                def a_norm(i):
                    pe.wait_ge(s_rrep, i + 1)
                    turn4(AA, y)

                def b_out(i):
                    pe.wait_ge(s_attnT, i + 1)
                    token_major(BD, W["Wo3"], attnT)

                steps(pe, dict(n_xa=n_xa, p_t5=p_t5, p_mix=p_mix, p_u1=p_u1, p_w=p_w, p_k=projected(0, "Wk"),
                               p_r=projected(3, "Wr"), p_v=projected(2, "Wv"), p_g=projected(4, "Wg"),
                               w_bonus=w_bonus, w_step=w_step, w_mean=w_mean, w_var=w_var, w_out=w_out, w_xc=w_xc,
                               w_fk=w_fk, w_fr=w_fr, w_fv=w_fv, a_x=a_x, a_q=a_q, a_kv=a_kv, a_score=a_score,
                               a_turn=a_turn, a_value=a_value, a_norm=a_norm, b_out=b_out), begin)

            @block.scalar
            def _(act):
                PD, PA, WR, AD, AA, NA = (ring(k) for k in ("pd", "pa", "w", "ad", "aa", "pa"))
                act.wait_ge(s_zero, 6)
                act.wait_ge(s_bq, 1)

                def begin(stage, i):
                    for r in dict(n=(NA,), p=(PD, PA), w=(WR,), a=(AA,), b=())[stage]:
                        r.begin(i)
                    PA.n = 1

                def c4(ps):
                    return ps[:, :].rearrange("p (c t) -> p c t", c=NC)

                def next_bank(r):
                    b = r.next()
                    act.wait_ge(r.ready, r.count)
                    return PS[b]

                def later(i):
                    return not isinstance(i, int) or i > 0

                def scaled(dst, ps, w, b, free):
                    for c in range(NC):
                        ac = nc.scalar.activation(dst[:, c, 1:P + 1], ps[:, c * P:(c + 1) * P], ACT.Identity,
                                                  bias=C(b, c), scale=C(w, c))
                    ac.then_inc(free, 1)

                def n_xa(i):
                    ps = next_bank(NA)
                    if later(i):
                        act.wait_ge(s_xm, NM * i)
                    scaled(xaT, ps, "ln1_w", "ln1_b", NA.free)

                def p_t5(i):
                    ps = next_bank(PA)
                    if later(i):
                        act.wait_ge(PD.ready, PD.written(i - 1, NM))
                    for f in range(NM - 1):
                        rows = slice(DM * f, DM * f + DM)
                        nc.scalar.activation(t5[rows, f, :], ps[rows, 0:P], ACT.Tanh)
                    nc.scalar.activation(t5b[0:DM, :], ps[0:DM, P:2 * P], ACT.Tanh).then_inc(PA.free, 1)

                def p_mix(i, f):
                    ps = next_bank(PD)
                    for c in range(NC):
                        ac = nc.scalar.activation(xm[f][:, c, :], ps[:, c * P:(c + 1) * P], ACT.Identity,
                                                  bias=C("maa_stack", f * NC + c))
                    ac.then_inc(PD.free, 1)

                def p_u1(i):
                    ps = next_bank(PA)
                    nc.scalar.activation(u1[0:DD, :], ps[0:DD, 0:P], ACT.Tanh).then_inc(PA.free, 1)

                def p_w(i):
                    ps = next_bank(PA)
                    for c in range(NC):
                        ac = nc.scalar.activation(z[:, c, :], ps[:, c * P:(c + 1) * P], ACT.Exp, bias=C("decay", c))
                    ac.then_inc(PA.free, 1)
                    act.wait_ge(PA.free, PA.read(i, J_Z))
                    if later(i):
                        act.wait_ge(s_scan, JS * i)
                    nc.scalar.activation(wS[:, :, 1:P], z[:, :, 0:P - 1], ACT.Exp, scale=-1.0).then_inc(s_wS, 1)

                def p_k(i):
                    ps = next_bank(PA)
                    if later(i):
                        act.wait_ge(s_scan, JS * i)
                    nc.scalar.activation(kT[:, :, :], c4(ps), ACT.Copy).then_inc(PA.free, 1)

                def p_r(i):
                    ps = next_bank(PA)
                    if later(i):
                        act.wait_ge(s_prod, JS * i)
                    nc.scalar.activation(rT[:, :, :], c4(ps), ACT.Copy).then_inc(PA.free, 1)

                def p_v(i):
                    ps = next_bank(PA)
                    nc.scalar.activation(vH[:, :, :], c4(ps), ACT.Copy)
                    nc.scalar.activation(vT[:, :, :], c4(ps), ACT.Copy).then_inc(PA.free, 1)

                def p_g(i):
                    ps = next_bank(PA)
                    nc.scalar.activation(z[:, :, :], c4(ps), ACT.Tanh, scale=0.5)
                    if later(i):
                        act.wait_ge(s_gated, i)
                    nc.scalar.activation(g[:, :, :], c4(ps), ACT.Copy).then_inc(PA.free, 1)

                def w_mean(i):
                    WR.n += 1 + JS + 1
                    act.wait_ge(WR.free, WR.read(i, J_MEAN))
                    nc.scalar.activation(sq[:, :, :], dev[:, :, :], ACT.Square).then_inc(s_sq, 1)

                def w_var(i):
                    nc.scalar.activation(gstd[:, :, :], c4(next_bank(WR)), ACT.Sqrt, bias=eps5[:, :]).then_inc(WR.free, 1)

                def w_gnorm(i):
                    WR.n += 1
                    act.wait_ge(s_scaled, i + 1)
                    for c in range(NC):
                        ac = nc.scalar.activation(dev[:, c, :], dev[:, c, :], ACT.Identity, bias=C("gn_b", c), scale=C("gn_w", c))
                    ac.then_inc(s_gnorm, 1)

                def w_xc(i):
                    scaled(xcT, next_bank(WR), "ln2_w", "ln2_b", WR.free)

                def w_fk(i):
                    nc.scalar.activation(kk[:, :, :], c4(next_bank(WR)), ACT.Relu).then_inc(WR.free, 1)
                    act.wait_ge(WR.free, WR.read(i, J_FK))
                    nc.scalar.activation(kk[:, :, :], kk[:, :, :], ACT.Square).then_inc(s_kk, 1)

                def w_fr(i):
                    nc.scalar.activation(sig, next_bank(WR)[:, :], ACT.Tanh, scale=0.5).then_inc(WR.free, 1)

                def a_x(i):
                    nc.scalar.activation(x3T[:, :, :], c4(next_bank(AA)), ACT.Copy).then_inc(AA.free, 1)

                def a_q(i):
                    ps = next_bank(AA)
                    for c in range(G3):
                        ac = nc.scalar.activation(qT[:, c, :], ps[:, c * P:(c + 1) * P], ACT.Identity, bias=bq[:, c:c + 1],
                                                  scale=D3 ** -0.5)
                    ac.then_inc(AA.free, 1)

                def a_kv(i):
                    ps = next_bank(AA)
                    nc.scalar.activation(kS[:, :], ps[:, 0:P], ACT.Identity, bias=C("bk3"))
                    vals = ps[:, P:2 * P].rearrange("p (g two d) -> p g two d", two=2, d=D3)
                    nc.scalar.activation(v3[:, :, 0, 0:D3], vals[:, :, 0, :], ACT.Copy)
                    nc.scalar.activation(v3[:, :, 1, D3:V2], vals[:, :, 1, :], ACT.Copy).then_inc(AA.free, 1)

                def a_exp(i, u):
                    act.wait_ge(AD.free, AD.read(i, u + 1))
                    for c in range(G3):
                        s = sc[u % 3][:, c, :]
                        ac = nc.scalar.activation(s, s, ACT.Exp, bias=nmax[:, u, c:c + 1], scale=-1.0,
                                                  accum_out=rsum[:, GO[u], c:c + 1])
                    ac.then_inc(s_exp, 1)

                def a_turn(i, u):
                    ps = next_bank(AA)
                    if u >= 2:
                        act.wait_ge(s_av, KV3 // 2 * i + u // 2)
                    nc.scalar.activation(scT[u % 2][:, :, :], c4(ps), ACT.Copy).then_inc(AA.free, 1)

                def a_norm(i):
                    nc.scalar.activation(attn[:, :, :], c4(next_bank(AA)), ACT.Copy).then_inc(AA.free, 1)
                    act.wait_ge(s_attn, i + 2)
                    nc.scalar.activation(attnT[:, :, :], attn[:, :, :], ACT.Identity, bias=C("bv3")).then_inc(s_attnT, 1)

                def b_store(i):
                    act.wait_ge(s_out, i + 1)
                    act.dma_start(a["out"][i], out[:, :]).then_inc(s_store, 16)

                steps(act, dict(p_mix=p_mix, n_xa=n_xa, p_t5=p_t5, p_u1=p_u1, p_w=p_w, p_k=p_k, p_r=p_r, p_v=p_v, p_g=p_g,
                                w_mean=w_mean, w_var=w_var, w_gnorm=w_gnorm, w_xc=w_xc, w_fk=w_fk, w_fr=w_fr, a_x=a_x, a_q=a_q,
                                a_kv=a_kv, a_exp=a_exp, a_turn=a_turn, a_norm=a_norm, b_store=b_store), begin)
                act.wait_ge(s_store, 16 * (B + 1))

            @block.vector
            def _(dve):
                PD, PA, WR, AD, AA, BD = (ring(k) for k in ("pd", "pa", "w", "ad", "aa", "ad"))
                E = dict(n=Steps(3), w=Steps(3), b=Steps(3))
                nc.vector.tensor_scalar(bq[:, :], CS("bq3"), D3 ** -0.5, None, ALU.mult).then_inc(s_bq, 1)
                dve.sem_inc(s_store, 16)

                def begin(stage, i):
                    for r in dict(n=(E["n"],), p=(PD,), w=(WR, E["w"]), a=(AD,), b=(BD, E["b"]))[stage]:
                        r.begin(i)
                    BD.n = KV3

                def next_bank(r):
                    b = r.next()
                    dve.wait_ge(r.ready, r.count)
                    return PS[b]

                def c4(ps):
                    return ps[:, :].rearrange("p (c t) -> p c t", c=NC)

                def layer_norm_stats(src, t6, tmv, tve, eps, steps, s_step, s_var):
                    nc.vector.bn_stats(t6[:, :], src).then_inc(s_step, steps.tick())
                    dve.wait_ge(s_step, steps.now)
                    dve.sem_inc(s_hold, 1)
                    nc.vector.bn_aggr(tmv[:, :], t6[:, :]).then_inc(s_step, steps.tick())
                    dve.wait_ge(s_step, steps.now)
                    nc.vector.tensor_scalar(tve[:, :], tmv[:, 1:2], eps, None, ALU.add).then_inc(s_var, 1)

                def n_ln1(i):
                    dve.wait_ge(s_inP, 32 * i + 32)
                    layer_norm_stats(x[:, :], st6, mv, ve, 1e-5, E["n"], s_dveN, s_var1)

                def n_nx(i):
                    dve.wait_ge(s_rstd1, i + 1)
                    nc.vector.tensor_scalar(nx[:, :], x[:, :], mv[:, 0:1], rstd[:, :], ALU.subtract, ALU.mult)\
                        .then_inc(s_nx1, 1)

                def n_shift(i):
                    dve.wait_ge(PA.free, PA.read(i, J_XA))
                    dve.wait_ge(s_first1, i + 1)
                    nc.vector.tensor_tensor(sx[:, :, :], xaT[:, :, 0:P], xaT[:, :, 1:P + 1], ALU.subtract)\
                        .then_inc(s_dveN, E["n"].tick())
                    dve.wait_ge(s_dveN, E["n"].now)
                    for c in range(NC):
                        v_ = nc.vector.scalar_tensor_tensor(out=z[:, c, :], in0=sx[:, c, :], scalar=C("maa_x", c),
                                                            in1=xaT[:, c, 1:P + 1], op0=ALU.mult, op1=ALU.add)
                    v_.then_inc(s_z, 1)
                    E["n"].end()

                def p_mix(i, f):
                    dve.wait_ge(PD.free, PD.read(i, f + 1))
                    nc.vector.tensor_tensor(xm[f][:, :, :], xm[f][:, :, :], sx[:, :, :], ALU.mult).then_inc(s_mixed, 1)

                def p_ruk(i):
                    dve.wait_ge(PA.free, PA.read(i, J_R))
                    for c in range(NC):
                        v_ = nc.vector.scalar_tensor_tensor(out=ruk[:, c, :], in0=kT[:, c, :], scalar=C("u", c),
                                                            in1=rT[:, c, :], op0=ALU.mult, op1=ALU.mult)
                    v_.then_inc(s_ruk, 1)

                def p_split(i):
                    dve.wait_ge(PA.free, PA.read(i, J_V))
                    nc.vector.tensor_tensor(vL[:, :, :], vT[:, :, :], vH[:, :, :], ALU.subtract).then_inc(s_vL, 1)

                def p_gate(i):
                    dve.wait_ge(PA.free, PA.read(i, J_G))
                    nc.vector.scalar_tensor_tensor(out=g[:, :, :], in0=z[:, :, :], scalar=1.0, in1=g[:, :, :],
                                                   op0=ALU.add, op1=ALU.mult).then_inc(s_gate, 1)

                def w_bonus(i):
                    ps = next_bank(WR)
                    dve.wait_ge(PA.free, PA.read(i, J_V))
                    if later(i):
                        dve.wait_ge(s_x3, i)
                    nc.vector.tensor_tensor(bonus[:, :, :], c4(ps), vT[:, :, :], ALU.mult).then_inc(WR.free, 1)
                    dve.wait_ge(s_wS, i + 1)
                    dve.wait_ge(s_inW, 48 * i + 48)

                def w_step(i, j):
                    if j < JS:
                        if j >= 3:
                            dve.wait_ge(s_scan, JS * i + j - 2)
                        nc.vector.tensor_copy(kv[j % 3][:, :, 0], s0[:, :, JO[j]])
                        ps = next_bank(WR)
                        nc.vector.tensor_tensor(kv[j % 3][:, :, 1:P], c4(ps)[:, :, 0:P - 1], kT[:, :, 0:P - 1], ALU.mult)\
                            .then_inc(WR.free, 1)
                    if 1 <= j <= JS:
                        j -= 1
                        if j >= 2:
                            dve.wait_ge(s_prod, JS * i + j - 1)
                        dve.wait_ge(WR.free, WR.read(i, J_BONUS + 1 + j))
                        nc.vector.tensor_tensor_scan(flat(state[j % 2]), flat(wS), flat(kv[j % 3]), 0.0,
                                                     ALU.mult, ALU.add).then_inc(s_scan, 1)

                def w_og(i):
                    dve.wait_ge(s_sum, JS // 2 * (i + 1))
                    nc.vector.tensor_tensor(og[:, :, :], c4(PS[OSUM]), bonus[:, :, :], ALU.add).then_inc(s_og, 1)

                def w_mean(i):
                    ps = next_bank(WR)
                    dve.wait_ge(s_og, i + 2)
                    nc.vector.tensor_tensor(dev[:, :, :], og[:, :, :], c4(ps), ALU.subtract).then_inc(WR.free, 1)

                def w_scale(i):
                    WR.n += 1
                    dve.wait_ge(WR.free, WR.read(i, J_GVAR))
                    nc.vector.reciprocal(grstd[:, :, :], gstd[:, :, :]).then_inc(s_grstd, 1)
                    dve.wait_ge(s_grstd, i + 1)
                    nc.vector.tensor_tensor(dev[:, :, :], dev[:, :, :], grstd[:, :, :], ALU.mult).then_inc(s_scaled, 1)

                def w_gate(i):
                    dve.wait_ge(s_gnorm, i + 1)
                    nc.vector.scalar_tensor_tensor(out=gated[:, :, :], in0=dev[:, :, :], scalar=0.5, in1=g[:, :, :],
                                                   op0=ALU.mult, op1=ALU.mult).then_inc(s_gated, 1)

                def w_out(i):
                    nc.vector.tensor_tensor(x1[:, :], next_bank(WR)[:, :], xres[:, :], ALU.add).then_inc(WR.free, 1)
                    dve.wait_ge(WR.free, WR.read(i, J_WO))
                    layer_norm_stats(x1[:, :], st6b, mvb, veb, 1e-5, E["w"], s_dveW, s_var2)

                def w_ln2(i):
                    dve.wait_ge(s_rstd2, i + 1)
                    nc.vector.tensor_scalar(nx2, x1[:, :], mvb[:, 0:1], rstdb[:, :], ALU.subtract, ALU.mult)\
                        .then_inc(s_nx2, 1)

                def w_xc(i):
                    dve.wait_ge(WR.free, WR.read(i, J_XC))
                    dve.wait_ge(s_first2, i + 1)
                    nc.vector.tensor_tensor(sx2[:, :, :], xcT[:, :, 0:P], xcT[:, :, 1:P + 1], ALU.subtract)\
                        .then_inc(s_dveW, E["w"].tick())
                    dve.wait_ge(s_dveW, E["w"].now)
                    for dst, name, done in ((xk2, "ffn_k", s_xk2), (xr2, "ffn_r", s_xr2)):
                        for c in range(NC):
                            v_ = nc.vector.scalar_tensor_tensor(out=dst[:, c, :], in0=sx2[:, c, :], scalar=C(name, c),
                                                                in1=xcT[:, c, 1:P + 1], op0=ALU.mult, op1=ALU.add)
                        v_.then_inc(done, 1)
                    E["w"].end()

                def w_fv(i):
                    WR.n += 3
                    ps = next_bank(WR)
                    dve.wait_ge(WR.free, WR.read(i, J_FR))
                    nc.vector.scalar_tensor_tensor(out=sig, in0=sig, scalar=1.0, in1=ps[:, :],
                                                   op0=ALU.add, op1=ALU.mult).then_inc(WR.free, 1)
                    dve.wait_ge(WR.free, WR.read(i, J_FV))
                    if later(i):
                        dve.wait_ge(s_x3b, i)
                        dve.wait_ge(AA.ready, AA.written(i - 1, J3_X))
                    nc.vector.scalar_tensor_tensor(out=x3[:, :], in0=sig, scalar=0.5, in1=x1[:, :],
                                                   op0=ALU.mult, op1=ALU.add).then_inc(s_x3, 1)

                def later(i):
                    return not isinstance(i, int) or i > 0

                def a_score(i, u):
                    ps = next_bank(AD)
                    if u >= 3:
                        dve.wait_ge(AA.ready, AA.written(i, J3_Q + 1 + u - 3))
                    dve.sem_inc(s_hold, 1)
                    for c in range(G3):
                        v_ = nc.vector.tensor_tensor_reduce(sc[u % 3][:, c, :], ps[:, c * P:(c + 1) * P], mask[:, :],
                                                            -1.0, 3.0e38, ALU.add, ALU.min, nmax[:, u, c:c + 1])
                    v_.then_inc(AD.free, 1)

                def a_rinv(i):
                    dve.wait_ge(s_exp, KV3 * i + KV3)
                    nc.vector.reciprocal(rinv[:, :, :], rsum[:, :, :]).then_inc(s_rinv, 1)

                def a_norm(i):
                    dve.wait_ge(s_av, KV3 // 2 * (i + 1))
                    dve.wait_ge(AA.free, AA.read(i, J3_RINV))
                    nc.vector.tensor_tensor(attn[:, :, :], c4(PS[OAV]), attn[:, :, :], ALU.mult).then_inc(s_attn, 1)

                def b_res(i):
                    ps = next_bank(BD)
                    dve.wait_ge(s_x3b, i + 1)
                    nc.vector.tensor_tensor(y, ps[:, :], x3b[:, :], ALU.add).then_inc(BD.free, 1)
                    dve.wait_ge(BD.free, BD.read(i, J3_WO))
                    layer_norm_stats(y, lst6, lmv, lve, 1e-6, E["b"], s_dveA, s_var3)

                def b_ln(i):
                    dve.wait_ge(s_rstd3, i + 1)
                    dve.wait_ge(s_store, 16 * i + 16)
                    nc.vector.scalar_tensor_tensor(out=out[:, :], in0=y, scalar=lmv[:, 0:1], in1=R("gamma3"),
                                                   op0=ALU.subtract, op1=ALU.mult).then_inc(s_dveA, E["b"].tick())
                    dve.wait_ge(s_dveA, E["b"].now)
                    nc.vector.scalar_tensor_tensor(out=out[:, :], in0=out[:, :], scalar=lrstd[:, :], in1=R("beta3"),
                                                   op0=ALU.mult, op1=ALU.add).then_inc(s_out, 1)
                    E["b"].end()

                steps(dve, dict(n_ln1=n_ln1, n_nx=n_nx, n_shift=n_shift, p_mix=p_mix, p_ruk=p_ruk, p_split=p_split, p_gate=p_gate,
                                w_bonus=w_bonus, w_step=w_step, w_og=w_og, w_mean=w_mean,
                                w_scale=w_scale, w_gate=w_gate, w_out=w_out, w_ln2=w_ln2, w_xc=w_xc, w_fv=w_fv,
                                a_score=a_score, a_rinv=a_rinv, a_norm=a_norm, b_res=b_res, b_ln=b_ln), begin)


def program(nc, a):
    ctx = ExitStack()
    with ctx:
        def sb(name, shape, dt=F32):
            return ctx.enter_context(nc.sbuf_tensor(name, shape, dt))

        def sem(name):
            return ctx.enter_context(nc.semaphore(name))

        PS = [ctx.enter_context(nc.psum_tensor(f"bank{k}", [P, 512], F32)) for k in range(8)]

        cols = sb("cols", [P, NCOLS])
        rows = sb("rows", [P, len(ROWS) - ROWS1, D])
        ident = sb("ident", [P, P])
        hsum = sb("hsum", [P, HC])
        hsum4 = sb("hsum4", [P, P // D1])
        halfs = sb("halfs", [P, H2])
        at, col = 0, {}
        for name, n in COLS:
            col[name] = (at, n)
            at += n

        def C(name, k=0, parts=P):
            return cols[0:parts, col[name][0] + k:col[name][0] + k + 1]

        def CS(name):
            return cols[:, col[name][0]:col[name][0] + col[name][1]]

        def R(name):
            k = ROWS.index(name)
            return rows[:, k, :] if k < len(ROWS) - ROWS1 else rows1[:, k - len(ROWS) + ROWS1, :]


        s_const = sem("const_loaded")
        s_ident = sem("ident_made")
        s_bn = sem("bn_scale_ready")
        l0_out = nc.dram_tensor("l0_out", (B, P, D), F32, kind="Internal").ap()
        l1_out = nc.dram_tensor("l1_out", (B, P, D), F32, kind="Internal").ap()
        bn_scale = sb("bn_scale", [P, 1])
        bn_shift = sb("bn_shift", [P, 1])

        maa_w1 = sb("maa_w1", [P, NC, NM * DM])
        maa_w2 = sb("maa_w2", [P, D])
        maa_w2b = sb("maa_w2b", [P, D])
        td_w1 = sb("td_w1", [P, NC, DD])
        td_w2 = sb("td_w2", [P, D])
        gather = sb("gather", [P, 4, 4 * HC])
        tiles = (maa_w1, maa_w2, maa_w2b, td_w1, td_w2, gather)
        early = (maa_w1[:, :, :], maa_w2[:, :], maa_w2b[:, :], td_w1[:, :, :], td_w2[:, :], gather[:, :, :])
        s_early = sem("layer2_first_weights_loaded")

        w1_scope = ctx.enter_context(ExitStack())

        def sb1(name, shape, dt=F32):
            return w1_scope.enter_context(nc.sbuf_tensor(name, shape, dt))

        rows1 = sb1("rows1", [P, ROWS1, D])
        q_w = sb1("q_w", [P, NC, D])
        k_w = sb1("k_w", [P, NC, D])
        v_w = sb1("v_w", [P, NC, D])
        out_w = sb1("out_w", [P, NC, D])
        mlp_w1 = sb1("mlp_w1", [P, NC, NF * P])
        mlp_w2 = sb1("mlp_w2", [P, NF, D])
        s_w1 = sem("layer1_weights_loaded")

        layer0(nc, a, PS, sem, C, cols, rows, rows1, ident, hsum, hsum4, halfs, s_const, s_ident, bn_scale, bn_shift,
               l0_out, (q_w, k_w, v_w, out_w, mlp_w1, mlp_w2), s_w1)
        layer1(nc, a, PS, sem, C, R, CS, ident, hsum4, halfs, bn_scale, bn_shift, l0_out, l1_out,
               (q_w, k_w, v_w, out_w, mlp_w1, mlp_w2), early, s_early)
        w1_scope.close()
        layers23(nc, a, PS, sem, C, R, CS, ident, hsum, halfs, l1_out, tiles, s_early)


def _layout(v):
    import numpy as np

    f = {k: np.asarray(x) for k, x in v.items()}

    def chunks(w):
        w = np.asarray(w)
        return np.ascontiguousarray(w.reshape(w.shape[0] // P, P, w.shape[1]).transpose(1, 0, 2))

    def col(x):
        x = np.asarray(x).reshape(-1)
        if x.size < P:
            x = np.pad(x, (0, P - x.size))
        return x.reshape(-1, P).T

    l0, l1, l2, l3 = (lambda n: f["L0_xattn_" + n]), (lambda n: f["L1_xattn_" + n]), \
        (lambda n: f["L2_xattn_" + n]), (lambda n: f["L3_xattn_" + n])
    byq = np.arange(H3 * D3).reshape(KV3, G3, D3).transpose(1, 0, 2).reshape(-1)

    byj = np.arange(D).reshape(NC, HC, D2).transpose(0, 2, 1).reshape(-1)

    def padded(w, rows):
        return np.pad(w, ((0, rows - w.shape[0]), (0, 0)))

    o = {}
    o["x"] = f["x"]
    o["ctx"] = f["ctx_2048"]
    o["ctxT"] = np.ascontiguousarray(f["ctx_2048"].reshape(B, P, NC, P).transpose(0, 3, 2, 1))
    state = f["ctx_2048"]
    o["state"] = state[:, 2:2 + D2].reshape(B, NC, P, D2).transpose(0, 2, 1, 3)
    o["row0"] = state[:, 0].reshape(B, NC, P).transpose(0, 2, 1)
    o["row1"] = state[:, 1].reshape(B, NC, P).transpose(0, 2, 1)
    o["mask1"] = f["mask_BxS2_ik0"]
    o["mask3"] = f["mask_Bx1xSxS2_ff0"].reshape(B, P, P)
    o["w0"] = np.stack([l0("Wtheta").T, l0("Wphi").T, l0("Wg").T], axis=1)
    o["wz"] = padded(l0("Wz").T, P)
    o["q_w"] = chunks(l1("q_w"))
    o["k_w"] = chunks(l1("kv_w")[:, 0::2])
    o["v_w"] = chunks(l1("kv_w")[:, 1::2])
    o["out_w"] = chunks(l1("out_w"))
    o["mlp_w1"] = chunks(l1("mlp_w1"))
    o["mlp_w2"] = chunks(l1("mlp_w2"))
    o["maa_w1"] = chunks(l2("maa_w1"))
    o["maa_w2"] = padded(l2("maa_w2").reshape(NM * DM, D), 2 * P)
    o["td_w1"] = chunks(l2("td_w1"))
    o["td_w2"] = padded(l2("td_w2"), P)
    for n in ("Wr", "Wk", "Wfk", "Wfr", "Wfv"):
        o[n] = chunks(l2(n).T)
    for n in ("Wv", "Wg"):
        o[n] = chunks(l2(n).T[:, byj])
    o["Wo"] = chunks(l2("Wo").T[byj])
    o["Wq3"] = chunks(l3("Wq")[:, byq])
    o["Wk3"] = chunks(l3("Wk"))
    o["Wv3"] = chunks(l3("Wv"))
    o["Wo3"] = chunks(l3("Wo")[byq])
    vec = dict(btheta=l0("btheta"), bphi=l0("bphi"), bg=l0("bg"), bz=l0("bz"), bn_gamma=l0("gamma"),
               bn_beta=l0("beta"), q_b=l1("q_b"), k_b=l1("kv_b")[0::2], v_b=l1("kv_b")[1::2],
               post_w=l1("postnorm_w"), b1=l1("mlp_b1"), ln1_w=l2("ln1_w"), ln1_b=l2("ln1_b"),
               ln2_w=l2("ln2_w"), ln2_b=l2("ln2_b"), maa_x=l2("maa_x"), maa_stack=l2("maa_stack"),
               decay=l2("time_decay"), u=l2("u"), ffn_k=l2("ffn_maa_k"), ffn_r=l2("ffn_maa_r"),
               gn_w=l2("gn_w")[byj], gn_b=l2("gn_b")[byj],
               bq3=l3("bq")[byq], bk3=l3("bk"), bv3=l3("bv"))
    o["cols"] = np.concatenate([col(vec[n]) for n, _ in COLS], axis=1)
    row = dict(out_b=l1("out_b"), b2=l1("mlp_b2"), bo3=l3("bo"),
               gamma3=l3("gamma"), beta3=l3("beta"))
    o["rows"] = np.stack([row[n] for n in ROWS[:-ROWS1]])
    o["rows1"] = np.stack([row[n] for n in ROWS[-ROWS1:]])
    o["hsum"] = (np.arange(P)[:, None] // D2 == np.arange(HC)[None, :]).astype(np.float32)
    o["hsum4"] = (np.arange(P)[:, None] // D1 == np.arange(P // D1)[None, :]).astype(np.float32)
    head = np.arange(P) // D2
    o["spread"] = ((np.arange(P)[:, None, None] == (HC * np.arange(D2)[:, None] + head[None, :])[None])).astype(np.float32)
    o["gather"] = (np.arange(4 * HC)[None, None, :] == (HC * np.arange(4)[None, :, None] + head[:, None, None])).astype(np.float32)
    vhead = np.arange(P) % HC
    o["blocks"] = np.stack([head[:, None] == vhead[None, :],
                            (vhead[:, None] == vhead[None, :]) / np.float32(D2)], axis=1).astype(np.float32)
    return {k: np.ascontiguousarray(x) for k, x in o.items()}


def kernel(**inputs):
    from concourse import bacc
    from concourse.bass_utils import run_bass_kernel_spmd

    nc = bacc.Bacc("TRN2", target_bir_lowering=False, num_devices=1)
    arrays, args = {}, {}
    for name, x in _layout(inputs).items():
        arrays[f"in_{name}"] = x
        args[name] = nc.dram_tensor(f"in_{name}", x.shape, mybir.dt.from_np(x.dtype), kind="ExternalInput").ap()
    args["out"] = nc.dram_tensor("out", (B, P, D), F32, kind="ExternalOutput").ap()
    program(nc, args)
    r = run_bass_kernel_spmd(nc, [arrays], core_ids=[0])
    return r.results[0]["out"]
```
